# Optimizing a Trainium2 kernel written in Bass

```python
import numpy as np
import jax
import jax.numpy as jnp

def _softmax(x, axis=-1):
    return jax.nn.softmax(x, axis=axis)

def _gelu(x):
    return jax.nn.gelu(x, approximate=True)

def _silu(x):
    return jax.nn.silu(x)

def _sigmoid(x):
    return jax.nn.sigmoid(x)

def _layernorm(x, axis=-1, eps=1e-05):
    m = jnp.mean(x, axis=axis, keepdims=True)
    v = jnp.var(x, axis=axis, keepdims=True)
    return (x - m) / jnp.sqrt(v + eps)

def _scatter_add(tgt, idx, src, axis=0):
    return tgt.at[idx].add(src)

def _segment_sum(src, seg, n):
    return jax.ops.segment_sum(src, seg, n)
kernel_name = 'mk_lm_tower_d4_tok_ids256_r4_dabc02'

def setup_inputs(seed: int=0):
    np.random.seed(seed)
    _w = jnp.asarray

    def _rec_inputs():
        import jax
        import jax.numpy as jnp
        _rk = jax.random.key(seed)
        x = jax.random.randint(jax.random.fold_in(_rk, 1), (32, 128), 0, 4360, jnp.int32)
        return x
    x = _rec_inputs()

    def _L0_tok_setup():
        import jax, jax.numpy as jnp
        import numpy as np
        VOCAB = 4360
        PROJ = 64
        PAD_IDX = 0
        key = jax.random.key(seed)
        k1, k2 = jax.random.split(key)
        x = jax.random.randint(k1, (64, 512), 0, VOCAB, dtype=jnp.int64)
        W = jax.random.normal(k2, (PROJ, VOCAB), dtype=jnp.float32) * 0.02
        return {'x': x, 'W': W}
    _L0_tok_all = _L0_tok_setup()
    _L0_tok_in = {k: v for k, v in _L0_tok_all.items() if k in ('W',)}
    del _L0_tok_all

    def _L0_attn_setup():
        import jax, jax.numpy as jnp
        import numpy as np
        GAMMA = 0.96875
        B, S, D = (4, 1024, 64)

        def _decay_mask(seq_len: int, gamma: float, dtype=jnp.float32) -> jnp.ndarray:
            i = jnp.arange(seq_len)
            diff = i[:, None] - i[None, :]
            lower = diff >= 0
            vals = jnp.exp(diff.astype(dtype) * jnp.log(jnp.asarray(gamma, dtype)))
            return jnp.where(lower, vals, jnp.zeros((), dtype))
        key = jax.random.key(seed)
        k1, k2, k3, k4 = jax.random.split(key, 4)
        scale = 1.0 / np.sqrt(D)
        return {'x': jax.random.normal(k1, (B, S, D), dtype=jnp.float32), 'Wq': jax.random.normal(k2, (D, D), dtype=jnp.float32) * scale, 'Wk': jax.random.normal(k3, (D, D), dtype=jnp.float32) * scale, 'Wv': jax.random.normal(k4, (D, D), dtype=jnp.float32) * scale}
    _L0_attn_all = _L0_attn_setup()
    _L0_attn_in = {k: v for k, v in _L0_attn_all.items() if k in ('Wq', 'Wk', 'Wv')}
    del _L0_attn_all

    def _L0_ffn_setup():
        import jax, jax.numpy as jnp
        import numpy as np
        B, S, H, F, E, K = (8, 1024, 64, 128, 16, 2)
        EPS = 1e-05
        key = jax.random.key(seed)
        ks = jax.random.split(key, 9)
        sc = 0.02
        return {'x': jax.random.normal(ks[0], (B, S, H), dtype=jnp.float32), 'gate_w': jax.random.normal(ks[1], (H, E), dtype=jnp.float32) * sc, 'gate_b': jnp.zeros((E,), dtype=jnp.float32), 'w1': jax.random.normal(ks[2], (E, H, F), dtype=jnp.float32) * sc, 'b1': jnp.zeros((E, F), dtype=jnp.float32), 'w2': jax.random.normal(ks[3], (E, F, H), dtype=jnp.float32) * sc, 'b2': jnp.zeros((E, H), dtype=jnp.float32), 'gamma': jnp.ones((H,), dtype=jnp.float32), 'beta': jnp.zeros((H,), dtype=jnp.float32)}
    _L0_ffn_all = _L0_ffn_setup()
    _L0_ffn_in = {k: v for k, v in _L0_ffn_all.items() if k in ('gate_w', 'gate_b', 'w1', 'b1', 'w2', 'b2', 'gamma', 'beta')}
    del _L0_ffn_all

    def _L1_attn_setup():
        import jax, jax.numpy as jnp
        import numpy as np
        B, N, E, H, BS = (8, 2048, 64, 2, 8)
        D = E // H
        key = jax.random.key(seed)
        ks = jax.random.split(key, 8)
        s = 0.02
        return {'x': jax.random.normal(ks[0], (B, N, E), jnp.float32), 'Wq': jax.random.normal(ks[1], (E, E), jnp.float32) * s, 'bq': jnp.zeros((E,), jnp.float32), 'Wk': jax.random.normal(ks[2], (E, E), jnp.float32) * s, 'bk': jnp.zeros((E,), jnp.float32), 'Wv': jax.random.normal(ks[3], (E, E), jnp.float32) * s, 'bv': jnp.zeros((E,), jnp.float32), 'P': jax.random.normal(ks[4], (D, D), jnp.float32) / jnp.sqrt(jnp.float32(D))}
    _L1_attn_all = _L1_attn_setup()
    _L1_attn_in = {k: v for k, v in _L1_attn_all.items() if k in ('Wq', 'bq', 'Wk', 'bk', 'Wv', 'bv', 'P')}
    del _L1_attn_all

    def _L1_ffn_setup():
        import jax, jax.numpy as jnp
        import numpy as np
        B, K, D = (128, 16, 64)
        E = 32
        H = int(D * 0.25)
        key = jax.random.key(seed)
        ks = jax.random.split(key, 7)
        d_rs = D ** (-0.5)
        h_rs = H ** (-0.5)
        x = jax.random.normal(ks[0], (B, K, D), dtype=jnp.float32)
        router_w = jax.random.uniform(ks[1], (E, D), jnp.float32, -d_rs, d_rs)
        router_b = jax.random.uniform(ks[2], (E,), jnp.float32, -d_rs, d_rs)
        W1 = jax.random.uniform(ks[3], (E, D, H), jnp.float32, -h_rs, h_rs)
        b1 = jax.random.uniform(ks[4], (E, H), jnp.float32, -h_rs, h_rs)
        W2 = jax.random.uniform(ks[5], (E, H, D), jnp.float32, -d_rs, d_rs)
        b2 = jax.random.uniform(ks[6], (E, D), jnp.float32, -d_rs, d_rs)
        return {'x': x, 'router_w': router_w, 'router_b': router_b, 'W1': W1, 'b1': b1, 'W2': W2, 'b2': b2}
    _L1_ffn_all = _L1_ffn_setup()
    _L1_ffn_in = {k: v for k, v in _L1_ffn_all.items() if k in ('router_w', 'router_b', 'W1', 'b1', 'W2', 'b2')}
    del _L1_ffn_all

    def _L2_attn_setup():
        import jax, jax.numpy as jnp
        import numpy as np
        N, F, C, H = (32, 1024, 64, 8)
        D = C // H
        EPS_ATTN = 1e-06
        EPS_LN = 1e-05

        def layer_norm(x, g, b):
            mu = jnp.mean(x, axis=-1, keepdims=True)
            var = jnp.var(x, axis=-1, keepdims=True)
            return (x - mu) * jax.lax.rsqrt(var + EPS_LN) * g + b
        key = jax.random.key(seed)
        ks = jax.random.split(key, 8)
        s = 1.0 / np.sqrt(C)
        return {'x': jax.random.normal(ks[0], (N, F, C), jnp.float32), 'Wqkv': jax.random.uniform(ks[1], (3 * C, C), jnp.float32, -s, s), 'ln1_g': jnp.ones((C,), jnp.float32), 'ln1_b': jnp.zeros((C,), jnp.float32), 'W1': jax.random.uniform(ks[2], (C, C), jnp.float32, -s, s), 'b1': jax.random.uniform(ks[3], (C,), jnp.float32, -s, s), 'W2': jax.random.uniform(ks[4], (C, C), jnp.float32, -s, s), 'b2': jax.random.uniform(ks[5], (C,), jnp.float32, -s, s), 'ln2_g': jnp.ones((C,), jnp.float32), 'ln2_b': jnp.zeros((C,), jnp.float32)}
    _L2_attn_all = _L2_attn_setup()
    _L2_attn_in = {k: v for k, v in _L2_attn_all.items() if k in ('Wqkv', 'ln1_g', 'ln1_b', 'W1', 'b1', 'W2', 'b2', 'ln2_g', 'ln2_b')}
    del _L2_attn_all

    def _L2_ffn_setup():
        import jax, jax.numpy as jnp
        import numpy as np
        NUM_EXPERTS = 8
        TOP_K = 2
        B, S, D = (8, 2048, 64)

        def _moe(tokens, router_w, w1, b1, w2, b2):
            N = tokens.shape[0]
            E = router_w.shape[0]
            logits = tokens.astype(jnp.float32) @ router_w.astype(jnp.float32).T
            probs = jax.nn.softmax(logits, axis=-1)
            rw, re = jax.lax.top_k(probs, TOP_K)
            if TOP_K > 1:
                rw = rw / jnp.maximum(rw.sum(-1, keepdims=True), 1e-12)
            rw = rw.astype(tokens.dtype)
            combine = jnp.zeros((N, E), tokens.dtype).at[jnp.arange(N)[:, None], re].set(rw)
            out = tokens
            for e in range(E):
                h = jax.nn.gelu(tokens @ w1[e] + b1[e], approximate=False)
                y = h @ w2[e] + b2[e]
                out = out + combine[:, e:e + 1] * y
            return out
        key = jax.random.key(seed)
        ks = jax.random.split(key, 4)
        scale = 1.0 / np.sqrt(D).astype(np.float32)
        return {'input_embeddings': jax.random.normal(ks[0], (B, S, D), jnp.float32), 'router_w': jax.random.normal(ks[1], (NUM_EXPERTS, D), jnp.float32) * scale, 'w1': jax.random.normal(ks[2], (NUM_EXPERTS, D, D), jnp.float32) * scale, 'b1': jnp.zeros((NUM_EXPERTS, D), jnp.float32), 'w2': jax.random.normal(ks[3], (NUM_EXPERTS, D, D), jnp.float32) * scale, 'b2': jnp.zeros((NUM_EXPERTS, D), jnp.float32)}
    _L2_ffn_all = _L2_ffn_setup()
    _L2_ffn_in = {k: v for k, v in _L2_ffn_all.items() if k in ('router_w', 'w1', 'b1', 'w2', 'b2')}
    del _L2_ffn_all

    def _L3_attn_setup():
        import jax, jax.numpy as jnp
        import numpy as np
        STATE_DIM = 64
        HIDDEN_DIM = 64
        R_MIN, R_MAX, THETA_MAX = (0.9, 0.999, 6.283)
        BATCH, SEQLEN = (16, 1024)

        def binary_operator_diag(element_i, element_j):
            a_i, bu_i = element_i
            a_j, bu_j = element_j
            return (a_j * a_i, a_j * bu_i + bu_j)
        key = jax.random.key(seed)
        ks = jax.random.split(key, 8)
        u1 = jax.random.uniform(ks[0], (STATE_DIM,))
        u2 = jax.random.uniform(ks[1], (STATE_DIM,))
        nu_log = jnp.log(-0.5 * jnp.log(u1 * (R_MAX ** 2 - R_MIN ** 2) + R_MIN ** 2))
        theta_log = jnp.log(THETA_MAX * u2)
        B_re = jax.random.normal(ks[2], (STATE_DIM, HIDDEN_DIM)) / jnp.sqrt(2.0 * HIDDEN_DIM)
        B_im = jax.random.normal(ks[3], (STATE_DIM, HIDDEN_DIM)) / jnp.sqrt(2.0 * HIDDEN_DIM)
        C_re = jax.random.normal(ks[4], (HIDDEN_DIM, STATE_DIM)) / jnp.sqrt(1.0 * STATE_DIM)
        C_im = jax.random.normal(ks[5], (HIDDEN_DIM, STATE_DIM)) / jnp.sqrt(1.0 * STATE_DIM)
        D = jax.random.normal(ks[6], (HIDDEN_DIM,))
        diag_lambda = jnp.exp(-jnp.exp(nu_log) + 1j * jnp.exp(theta_log))
        gamma_log = jnp.log(jnp.sqrt(1.0 - jnp.abs(diag_lambda) ** 2))
        x = jax.random.normal(ks[7], (BATCH, SEQLEN, HIDDEN_DIM), dtype=jnp.float32)
        return {'x': x, 'nu_log': nu_log, 'theta_log': theta_log, 'B_re': B_re, 'B_im': B_im, 'C_re': C_re, 'C_im': C_im, 'D': D, 'gamma_log': gamma_log}
    _L3_attn_all = _L3_attn_setup()
    _L3_attn_in = {k: v for k, v in _L3_attn_all.items() if k in ('nu_log', 'theta_log', 'B_re', 'B_im', 'C_re', 'C_im', 'D', 'gamma_log')}
    del _L3_attn_all

    def _L3_ffn_setup():
        import jax, jax.numpy as jnp
        import numpy as np
        B, H, E, IN, OUT = (1024, 1, 8, 64, 64)

        @jax.custom_vjp
        def bin_active(x):
            return jnp.sign(x)

        def _ba_fwd(x):
            return (jnp.sign(x), x)

        def _ba_bwd(x, g):
            return (g * (jnp.abs(x) <= 1.0).astype(g.dtype),)
        bin_active.defvjp(_ba_fwd, _ba_bwd)

        @jax.custom_vjp
        def bin_gate(x):
            return (x > 0.5).astype(x.dtype)

        def _bg_fwd(x):
            return ((x > 0.5).astype(x.dtype), None)

        def _bg_bwd(_, g):
            return (g,)
        bin_gate.defvjp(_bg_fwd, _bg_bwd)
        key = jax.random.key(seed)
        k1, k2, k3, k4, k5 = jax.random.split(key, 5)
        x = jax.random.normal(k1, (B, H, IN), dtype=jnp.float32)
        weight = jax.random.normal(k2, (H, E, IN, OUT), dtype=jnp.float32) * 0.05
        proj_w = jax.random.normal(k3, (E, IN), dtype=jnp.float32) * 0.05
        proj_b = jax.random.normal(k4, (E,), dtype=jnp.float32) * 0.05
        scale = jax.random.normal(k5, (H, 1, OUT), dtype=jnp.float32) * 0.1
        return {'x': x, 'weight': weight, 'proj_w': proj_w, 'proj_b': proj_b, 'scale': scale}
    _L3_ffn_all = _L3_ffn_setup()
    _L3_ffn_in = {k: v for k, v in _L3_ffn_all.items() if k in ('weight', 'proj_w', 'proj_b', 'scale')}
    del _L3_ffn_all
    return {'x': x, 'L0_tok_W': _L0_tok_in['W'], 'L0_attn_Wq': _L0_attn_in['Wq'], 'L0_attn_Wk': _L0_attn_in['Wk'], 'L0_attn_Wv': _L0_attn_in['Wv'], 'L0_ffn_gate_w': _L0_ffn_in['gate_w'], 'L0_ffn_gate_b': _L0_ffn_in['gate_b'], 'L0_ffn_w1': _L0_ffn_in['w1'], 'L0_ffn_b1': _L0_ffn_in['b1'], 'L0_ffn_w2': _L0_ffn_in['w2'], 'L0_ffn_b2': _L0_ffn_in['b2'], 'L0_ffn_gamma': _L0_ffn_in['gamma'], 'L0_ffn_beta': _L0_ffn_in['beta'], 'L1_attn_Wq': _L1_attn_in['Wq'], 'L1_attn_bq': _L1_attn_in['bq'], 'L1_attn_Wk': _L1_attn_in['Wk'], 'L1_attn_bk': _L1_attn_in['bk'], 'L1_attn_Wv': _L1_attn_in['Wv'], 'L1_attn_bv': _L1_attn_in['bv'], 'L1_attn_P': _L1_attn_in['P'], 'L1_ffn_router_w': _L1_ffn_in['router_w'], 'L1_ffn_router_b': _L1_ffn_in['router_b'], 'L1_ffn_W1': _L1_ffn_in['W1'], 'L1_ffn_b1': _L1_ffn_in['b1'], 'L1_ffn_W2': _L1_ffn_in['W2'], 'L1_ffn_b2': _L1_ffn_in['b2'], 'L2_attn_Wqkv': _L2_attn_in['Wqkv'], 'L2_attn_ln1_g': _L2_attn_in['ln1_g'], 'L2_attn_ln1_b': _L2_attn_in['ln1_b'], 'L2_attn_W1': _L2_attn_in['W1'], 'L2_attn_b1': _L2_attn_in['b1'], 'L2_attn_W2': _L2_attn_in['W2'], 'L2_attn_b2': _L2_attn_in['b2'], 'L2_attn_ln2_g': _L2_attn_in['ln2_g'], 'L2_attn_ln2_b': _L2_attn_in['ln2_b'], 'L2_ffn_router_w': _L2_ffn_in['router_w'], 'L2_ffn_w1': _L2_ffn_in['w1'], 'L2_ffn_b1': _L2_ffn_in['b1'], 'L2_ffn_w2': _L2_ffn_in['w2'], 'L2_ffn_b2': _L2_ffn_in['b2'], 'L3_attn_nu_log': _L3_attn_in['nu_log'], 'L3_attn_theta_log': _L3_attn_in['theta_log'], 'L3_attn_B_re': _L3_attn_in['B_re'], 'L3_attn_B_im': _L3_attn_in['B_im'], 'L3_attn_C_re': _L3_attn_in['C_re'], 'L3_attn_C_im': _L3_attn_in['C_im'], 'L3_attn_D': _L3_attn_in['D'], 'L3_attn_gamma_log': _L3_attn_in['gamma_log'], 'L3_ffn_weight': _L3_ffn_in['weight'], 'L3_ffn_proj_w': _L3_ffn_in['proj_w'], 'L3_ffn_proj_b': _L3_ffn_in['proj_b'], 'L3_ffn_scale': _L3_ffn_in['scale']}

def reference(x, L0_tok_W, L0_attn_Wq, L0_attn_Wk, L0_attn_Wv, L0_ffn_gate_w, L0_ffn_gate_b, L0_ffn_w1, L0_ffn_b1, L0_ffn_w2, L0_ffn_b2, L0_ffn_gamma, L0_ffn_beta, L1_attn_Wq, L1_attn_bq, L1_attn_Wk, L1_attn_bk, L1_attn_Wv, L1_attn_bv, L1_attn_P, L1_ffn_router_w, L1_ffn_router_b, L1_ffn_W1, L1_ffn_b1, L1_ffn_W2, L1_ffn_b2, L2_attn_Wqkv, L2_attn_ln1_g, L2_attn_ln1_b, L2_attn_W1, L2_attn_b1, L2_attn_W2, L2_attn_b2, L2_attn_ln2_g, L2_attn_ln2_b, L2_ffn_router_w, L2_ffn_w1, L2_ffn_b1, L2_ffn_w2, L2_ffn_b2, L3_attn_nu_log, L3_attn_theta_log, L3_attn_B_re, L3_attn_B_im, L3_attn_C_re, L3_attn_C_im, L3_attn_D, L3_attn_gamma_log, L3_ffn_weight, L3_ffn_proj_w, L3_ffn_proj_b, L3_ffn_scale):
    import jax
    import jax.numpy as jnp

    def _L0_tok_ref(x, W):
        import jax, jax.numpy as jnp
        import numpy as np
        VOCAB = 4360
        PROJ = 64
        PAD_IDX = 0
        out = jnp.take(W.T, x, axis=0)
        mask = (x != PAD_IDX)[..., None]
        return jnp.where(mask, out, jnp.zeros((), dtype=out.dtype))

    def _L0_attn_ref(x, Wq, Wk, Wv):
        import jax, jax.numpy as jnp
        import numpy as np
        GAMMA = 0.96875
        B, S, D = (4, 1024, 64)

        def _decay_mask(seq_len: int, gamma: float, dtype=jnp.float32) -> jnp.ndarray:
            i = jnp.arange(seq_len)
            diff = i[:, None] - i[None, :]
            lower = diff >= 0
            vals = jnp.exp(diff.astype(dtype) * jnp.log(jnp.asarray(gamma, dtype)))
            return jnp.where(lower, vals, jnp.zeros((), dtype))
        q = jnp.einsum('bsh,dh->bsd', x, Wq)
        k = jnp.einsum('bsh,dh->bsd', x, Wk)
        v = jnp.einsum('bsh,dh->bsd', x, Wv)
        seq_len = x.shape[1]
        mask = _decay_mask(seq_len, GAMMA, x.dtype)
        scores = jnp.einsum('bsd,btd->bst', q, k) * mask[None, :, :]
        return jnp.einsum('bst,btd->bsd', scores, v)

    def _L0_ffn_ref(x, gate_w, gate_b, w1, b1, w2, b2, gamma, beta):
        import jax, jax.numpy as jnp
        import numpy as np
        B, S, H, F, E, K = (8, 1024, 64, 128, 16, 2)
        EPS = 1e-05
        gate_logits = x @ gate_w + gate_b
        topk_vals, topk_idx = jax.lax.top_k(gate_logits, K)
        topk_w = jax.nn.softmax(topk_vals, axis=-1)
        h = jax.nn.relu(jnp.einsum('bsh,ehf->bsef', x, w1) + b1)
        expert_out = jnp.einsum('bsef,efh->bseh', h, w2) + b2
        sel = jnp.take_along_axis(expert_out, topk_idx[:, :, :, None], axis=2)
        moe = jnp.sum(topk_w[..., None] * sel, axis=2)
        y = x + moe
        mu = jnp.mean(y, axis=-1, keepdims=True)
        var = jnp.var(y, axis=-1, keepdims=True)
        return (y - mu) / jnp.sqrt(var + EPS) * gamma + beta

    def _L1_attn_ref(x, Wq, bq, Wk, bk, Wv, bv, P):
        import jax, jax.numpy as jnp
        import numpy as np
        B, N, E, H, BS = (8, 2048, 64, 2, 8)
        D = E // H
        Bx, Nx, Ex = x.shape
        nb = Nx // BS
        q = (x @ Wq.T + bq).reshape(Bx, Nx, H, D)
        k = (x @ Wk.T + bk).reshape(Bx, Nx, H, D)
        v = (x @ Wv.T + bv).reshape(Bx, Nx, H, D)
        q = jnp.einsum('bnhe,ei->bnhi', q, P)
        k = jnp.einsum('bnhe,ei->bnhi', k, P)
        qb = q.reshape(Bx, nb, BS, H, D)
        kb = k.reshape(Bx, nb, BS, H, D)
        vb = v.reshape(Bx, nb, BS, H, D)
        scores = jnp.einsum('bgnhd,bgmhd->bgnhm', qb, kb) / jnp.sqrt(jnp.asarray(D, x.dtype))
        attn = jax.nn.softmax(scores, axis=-1)
        out = jnp.einsum('bgnhm,bgmhd->bgnhd', attn, vb)
        return out.reshape(Bx, Nx, Ex)

    def _L1_ffn_ref(x, router_w, router_b, W1, b1, W2, b2):
        import jax, jax.numpy as jnp
        import numpy as np
        B, K, D = (128, 16, 64)
        E = 32
        H = int(D * 0.25)
        xf = x.reshape(-1, D)
        logits = xf @ router_w.T + router_b
        idx = jnp.argmax(logits, axis=-1)
        w1t = jnp.take(W1, idx, axis=0)
        h = jnp.einsum('nd,ndh->nh', xf, w1t) + jnp.take(b1, idx, axis=0)
        h = jax.nn.relu(h)
        w2t = jnp.take(W2, idx, axis=0)
        out = jnp.einsum('nh,nhd->nd', h, w2t) + jnp.take(b2, idx, axis=0)
        out = jax.nn.relu(out)
        return out.reshape(x.shape)

    def _L2_attn_ref(x, Wqkv, ln1_g, ln1_b, W1, b1, W2, b2, ln2_g, ln2_b):
        import jax, jax.numpy as jnp
        import numpy as np
        N, F, C, H = (32, 1024, 64, 8)
        D = C // H
        EPS_ATTN = 1e-06
        EPS_LN = 1e-05

        def layer_norm(x, g, b):
            mu = jnp.mean(x, axis=-1, keepdims=True)
            var = jnp.var(x, axis=-1, keepdims=True)
            return (x - mu) * jax.lax.rsqrt(var + EPS_LN) * g + b
        n, f, c = x.shape
        qkv = jnp.einsum('nfc,oc->nfo', x, Wqkv)
        q, k, v = jnp.split(qkv, 3, axis=-1)
        q = q.reshape(n, f, H, D)
        k = k.reshape(n, f, H, D)
        v = v.reshape(n, f, H, D)
        q = jax.nn.elu(q) + 1.0
        k = jax.nn.elu(k) + 1.0
        kv = jnp.einsum('nshd,nshm->nhmd', k, v)
        ksum = jnp.sum(k, axis=1)
        z = 1.0 / (jnp.einsum('nlhd,nhd->nlh', q, ksum) + EPS_ATTN)
        t = jnp.einsum('nlhd,nhmd,nlh->nlhm', q, kv, z)
        t = t.reshape(n, f, c)
        x1 = layer_norm(t + x, ln1_g, ln1_b)
        h = jax.nn.gelu(jnp.einsum('nfc,oc->nfo', x1, W1) + b1, approximate=False)
        y = jnp.einsum('nfc,oc->nfo', h, W2) + b2
        return layer_norm(y + x1, ln2_g, ln2_b)

    def _L2_ffn_ref(input_embeddings, router_w, w1, b1, w2, b2):
        import jax, jax.numpy as jnp
        import numpy as np
        NUM_EXPERTS = 8
        TOP_K = 2
        B, S, D = (8, 2048, 64)

        def _moe(tokens, router_w, w1, b1, w2, b2):
            N = tokens.shape[0]
            E = router_w.shape[0]
            logits = tokens.astype(jnp.float32) @ router_w.astype(jnp.float32).T
            probs = jax.nn.softmax(logits, axis=-1)
            rw, re = jax.lax.top_k(probs, TOP_K)
            if TOP_K > 1:
                rw = rw / jnp.maximum(rw.sum(-1, keepdims=True), 1e-12)
            rw = rw.astype(tokens.dtype)
            combine = jnp.zeros((N, E), tokens.dtype).at[jnp.arange(N)[:, None], re].set(rw)
            out = tokens
            for e in range(E):
                h = jax.nn.gelu(tokens @ w1[e] + b1[e], approximate=False)
                y = h @ w2[e] + b2[e]
                out = out + combine[:, e:e + 1] * y
            return out
        b, s, d = input_embeddings.shape
        tokens = input_embeddings.reshape(b * s, d)
        return _moe(tokens, router_w, w1, b1, w2, b2).reshape(b, s, d)

    def _L3_attn_ref(x, nu_log, theta_log, B_re, B_im, C_re, C_im, D, gamma_log):
        import jax, jax.numpy as jnp
        import numpy as np
        STATE_DIM = 64
        HIDDEN_DIM = 64
        R_MIN, R_MAX, THETA_MAX = (0.9, 0.999, 6.283)
        BATCH, SEQLEN = (16, 1024)

        def binary_operator_diag(element_i, element_j):
            a_i, bu_i = element_i
            a_j, bu_j = element_j
            return (a_j * a_i, a_j * bu_i + bu_j)
        Lambda = jnp.exp(-jnp.exp(nu_log) + 1j * jnp.exp(theta_log))
        B_norm = (B_re + 1j * B_im) * jnp.exp(gamma_log)[:, None]
        C = C_re + 1j * C_im

        def run_seq(u):
            Bu = u.astype(B_norm.dtype) @ B_norm.T
            Lambda_elems = jnp.broadcast_to(Lambda, Bu.shape)
            _, states = jax.lax.associative_scan(binary_operator_diag, (Lambda_elems, Bu))
            return jnp.real(states @ C.T) + D * u
        return jax.vmap(run_seq)(x)

    def _L3_ffn_ref(x, weight, proj_w, proj_b, scale):
        import jax, jax.numpy as jnp
        import numpy as np
        B, H, E, IN, OUT = (1024, 1, 8, 64, 64)

        @jax.custom_vjp
        def bin_active(x):
            return jnp.sign(x)

        def _ba_fwd(x):
            return (jnp.sign(x), x)

        def _ba_bwd(x, g):
            return (g * (jnp.abs(x) <= 1.0).astype(g.dtype),)
        bin_active.defvjp(_ba_fwd, _ba_bwd)

        @jax.custom_vjp
        def bin_gate(x):
            return (x > 0.5).astype(x.dtype)

        def _bg_fwd(x):
            return ((x > 0.5).astype(x.dtype), None)

        def _bg_bwd(_, g):
            return (g,)
        bin_gate.defvjp(_bg_fwd, _bg_bwd)
        xh = jnp.transpose(x, (1, 0, 2))
        gate = jax.nn.sigmoid(jnp.einsum('hbi,ei->hbe', xh, proj_w) + proj_b)
        gate = bin_gate(gate)
        w = jnp.einsum('hbe,heio->hbio', gate, weight)
        xb = bin_active(xh)
        wb = bin_active(w)
        y = jnp.einsum('hbi,hbio->hbo', xb, wb)
        y = y * scale
        return jnp.transpose(y, (1, 0, 2))
    h = _L0_tok_ref(x, L0_tok_W)
    h = h + _L0_attn_ref(_layernorm(h, axis=-1), L0_attn_Wq, L0_attn_Wk, L0_attn_Wv)
    h = h + _L0_ffn_ref(_layernorm(h, axis=-1), L0_ffn_gate_w, L0_ffn_gate_b, L0_ffn_w1, L0_ffn_b1, L0_ffn_w2, L0_ffn_b2, L0_ffn_gamma, L0_ffn_beta)
    h = h + _L1_attn_ref(_layernorm(h, axis=-1), L1_attn_Wq, L1_attn_bq, L1_attn_Wk, L1_attn_bk, L1_attn_Wv, L1_attn_bv, L1_attn_P)
    h = h + _L1_ffn_ref(_layernorm(h, axis=-1), L1_ffn_router_w, L1_ffn_router_b, L1_ffn_W1, L1_ffn_b1, L1_ffn_W2, L1_ffn_b2)
    h = h + _L2_attn_ref(_layernorm(h, axis=-1), L2_attn_Wqkv, L2_attn_ln1_g, L2_attn_ln1_b, L2_attn_W1, L2_attn_b1, L2_attn_W2, L2_attn_b2, L2_attn_ln2_g, L2_attn_ln2_b)
    h = h + _L2_ffn_ref(_layernorm(h, axis=-1), L2_ffn_router_w, L2_ffn_w1, L2_ffn_b1, L2_ffn_w2, L2_ffn_b2)
    h = h + _L3_attn_ref(_layernorm(h, axis=-1), L3_attn_nu_log, L3_attn_theta_log, L3_attn_B_re, L3_attn_B_im, L3_attn_C_re, L3_attn_C_im, L3_attn_D, L3_attn_gamma_log)
    h = h + _L3_ffn_ref(_layernorm(h, axis=-1), L3_ffn_weight, L3_ffn_proj_w, L3_ffn_proj_b, L3_ffn_scale)
    return h

_drawn_inputs = setup_inputs


def setup_inputs(seed=0):
    import zlib

    import numpy as np

    out = dict(_drawn_inputs(seed))
    spreads = {'L0_ffn_gate_b': (0.0, 0.8),
     'L0_ffn_b1': (0.0, 0.8),
     'L0_ffn_b2': (0.0, 0.8),
     'L0_ffn_gamma': (1.0, 0.6),
     'L0_ffn_beta': (0.0, 0.8),
     'L1_attn_bq': (0.0, 0.8),
     'L1_attn_bk': (0.0, 2.0),
     'L1_attn_bv': (0.0, 0.8),
     'L2_attn_ln1_g': (1.0, 0.6),
     'L2_attn_ln1_b': (0.0, 0.8),
     'L2_attn_ln2_g': (1.0, 0.6),
     'L2_attn_ln2_b': (0.0, 0.8),
     'L2_ffn_b1': (0.0, 0.8),
     'L2_ffn_b2': (0.0, 2.0)}
    factors = {'L0_ffn_gate_w': 8.0,
     'L0_ffn_w1': 8.0,
     'L0_ffn_w2': 8.0,
     'L1_attn_Wq': 8.0,
     'L1_attn_Wk': 8.0,
     'L1_attn_Wv': 8.0,
     'L1_attn_P': 8.0,
     'L1_ffn_router_w': 8.0,
     'L1_ffn_router_b': 8.0,
     'L1_ffn_W1': 8.0,
     'L1_ffn_b1': 8.0,
     'L1_ffn_W2': 8.0,
     'L1_ffn_b2': 24.0,
     'L2_attn_Wqkv': 8.0,
     'L2_attn_W1': 8.0,
     'L2_attn_b1': 30.583,
     'L2_attn_W2': 8.0,
     'L2_attn_b2': 64.0,
     'L2_ffn_router_w': 5.285,
     'L2_ffn_w1': 5.332,
     'L2_ffn_w2': 4.902,
     'L3_attn_nu_log': 32.4,
     'L3_attn_theta_log': 2.796,
     'L3_attn_B_re': 3.74,
     'L3_attn_B_im': 3.661,
     'L3_attn_C_re': 3.674,
     'L3_attn_C_im': 3.626,
     'L3_attn_gamma_log': 4.38,
     'L3_ffn_weight': 3.24,
     'L3_ffn_proj_w': 3.987,
     'L3_ffn_proj_b': 7.492,
     'L3_ffn_scale': 3.162}
    for name, (base, spread) in spreads.items():
        noise = np.random.default_rng([zlib.crc32(name.encode()), seed]).standard_normal(out[name].shape)
        drawn = base * np.exp(spread * noise) if base else spread * noise
        out[name] = jnp.asarray(drawn.astype(out[name].dtype))
    for name, factor in factors.items():
        out[name] = (out[name] * factor).astype(out[name].dtype)
    return out
```

```python
import concourse.bass as bass
from concourse import mybir
from contextlib import ExitStack

P = 128
D = 64
LANES = 4
TILES = 4
NT = TILES * P
NSEQ = 32
PASSES = NSEQ // (LANES * TILES)

E0, F0 = 16, 128
E1, F1 = 32, 16
E2, F2 = 8, 64
E3 = 8
HID = 512
MT = HID // P
H1, D1, BS1 = 2, 32, 8
H2, D2 = 8, 8
KV2 = D + H2
PAIRS = D // 2
SPLIT = 3
G3 = SPLIT * E3
N_LN = 11
NT_USES = 9
BIG = 1.0e30
LN_EPS = 1e-5
DEN_EPS = 1e-6
GATE_MIN = 2.0 ** -24
LOG2E = 1.4426950408889634
MAGIC = 12582912.0
LN2_HI, LN2_LO = 0.693359375, -2.12194440e-4
PI = 3.141592653589793
TWO_PI_1 = 6.28125
TWO_PI_2 = 0.00193500518798828125
TWO_PI_3 = 2.0 * PI - TWO_PI_1 - TWO_PI_2
HALF_PI = PI / 2.0
QUANT = 6144.0

def columns(widths):
    at, out = 0, {}
    for name, width in widths:
        out[name] = (at, at + width)
        at += width
    out["_"] = (0, at)
    return out


C65 = columns([("gate0", E0), ("w1_0", E0 * F0), ("wv1", D), ("route1", E1), ("w1_1", HID),
               ("w2_2a", D), ("route2", E2), ("w1_2", HID), ("proj3", G3)])
C64 = columns([("wq0", D), ("wk0", D), ("wv0", D), ("q2", D), ("kv2", 2 * D), ("w1_2a", D),
               ("b1_2a", 1), ("b_re", D), ("b_im", D), ("gamma3", 1), ("d3", 1), ("scale3", 1)])
C128 = columns([("w2_0", E0 * D), ("w2_1", MT * D), ("w2_2", MT * D), ("c_a", D), ("c_b", D),
                ("nu", 1), ("theta", 1), ("w3", 256)])
C32 = columns([("qb1", H1 * 65), ("kb1", H1 * 65), ("p1", D1), ("b2_0", D), ("b2_1", D), ("b2_2", D)])
CROW = columns([("g0", D), ("be0", D), ("g2a", D), ("be2a", D), ("g2b", D), ("be2b", D)])
CC = columns([("ident", P), ("decay", P), ("block", P), ("heads", KV2), ("rank0", E0),
              ("rank1", E1), ("rank2", E2), ("time", P), ("later", P), ("sign", 1),
              ("sel2", MT * P), ("exp1", MT * P), ("pick3", 2 * D)])


def nth(lane, use=0):
    return use * LANES + lane + 1


def tower(nc, ids, emb_w, w65, w64, w128, w32, wrow, consts, part3, out):
    F32, BF16, I32, U32 = mybir.dt.float32, mybir.dt.bfloat16, mybir.dt.int32, mybir.dt.uint32
    ACT = mybir.ActivationFunctionType
    ALU = mybir.AluOpType
    X = mybir.AxisListType.X

    with ExitStack() as ctx:
        def sb(name, shape, dt=F32):
            return ctx.enter_context(nc.sbuf_tensor(name, shape, dt))

        def per_lane(name, shape, dt=F32):
            return [sb(f"{name}{l}", shape, dt) for l in range(LANES)]

        def sem(name):
            s = ctx.enter_context(nc.semaphore(name))
            sems.append(s)
            return s

        sems = []
        lanes = range(LANES)

        k65 = sb("k65", [65, C65["_"][1]])
        k64 = sb("k64", [64, C64["_"][1]])
        k128 = sb("k128", [P, C128["_"][1]])
        k32 = sb("k32", [32, C32["_"][1]])
        krow = sb("krow", [P, CROW["_"][1]])
        kc = sb("kc", [P, CC["_"][1]])

        def c65(name):
            a, b = C65[name]
            return k65[:, a:b]

        def c64(name):
            a, b = C64[name]
            return k64[:, a:b]

        def c128(name):
            a, b = C128[name]
            return k128[:, a:b]

        def c32(name, rows=32):
            a, b = C32[name]
            return k32[0:rows, a:b]

        def crow(name):
            a, b = CROW[name]
            return krow[:, None, a:b].broadcast_to([P, TILES, D])

        def cc(name, rows=P):
            a, b = CC[name]
            return kc[0:rows, a:b]

        def rank(E):
            return cc({E0: "rank0", E1: "rank1", E2: "rank2"}[E])[:, None, :].broadcast_to([P, TILES, E])

        ident = cc("ident")
        ids_sb = sb("ids_sb", [P, NSEQ], I32)
        ids_f = sb("ids_f", [P, NSEQ])
        keep = sb("keep", [P, NSEQ])
        emb = sb("emb", [P, NSEQ, D])

        score0 = sb("score0", [64, D])
        qp1 = sb("qp1", [65, D])
        kp1 = sb("kp1", [65, D])
        b_sc = sb("b_sc", [64, 2, D])
        b1_3 = sb("b1_3", [64, P])
        b2_3 = sb("b2_3", [64, P])
        c_cos = sb("c_cos", [P, D])
        c_sin = sb("c_sin", [P, D])
        diag3 = sb("diag3", [64, D])
        cosines = sb("cosines", [P, P])
        sines = sb("sines", [P, P])
        decay3 = sb("decay3", [P, NT])
        w3_rows = sb("w3_rows", [G3, PAIRS * P], BF16)
        sel_bf = sb("sel_bf", [E1, MT * P], BF16)
        pick3 = sb("pick3", [P, 2 * D], BF16)
        neg_half = sb("neg_half", [P, TILES])
        ln_logs = sb("ln_logs", [P, 3])
        ex = sb("ex", [P, 6, 3])
        ex_i = sb("ex_i", [P, 3], I32)
        ph = sb("ph", [P, 8, P])
        th = sb("th", [P, 8])
        w3_hi = sb("w3_hi", [P, 256], BF16)
        w3_mid = sb("w3_mid", [P, 256], BF16)
        w3_lo = sb("w3_lo", [P, 256], BF16)
        w3_r1 = sb("w3_r1", [P, 256])
        w3_r2 = sb("w3_r2", [P, 256])

        h = per_lane("h", [P, TILES, D])
        xn = per_lane("xn", [P, TILES, D])
        y = per_lane("y", [P, TILES, D])
        cen = per_lane("cen", [P, TILES, D])
        sq = per_lane("sq", [P, TILES, D])
        aff = per_lane("aff", [P, TILES, D])
        stat = per_lane("stat", [P, 4, TILES])
        xT = per_lane("xT", [65, NT])
        fm = per_lane("fm", [65, NT])
        fm2 = per_lane("fm2", [64, NT])
        v_sb = per_lane("v_sb", [P, TILES, KV2])
        big_a = per_lane("big_a", [P, NT])
        big_b = per_lane("big_b", [P, NT])
        big_c = per_lane("big_c", [P, NT])
        hid = per_lane("hid", [P, MT, NT])
        kvm = per_lane("kvm", [64, TILES, KV2])
        lg = per_lane("lg", [P, TILES, E1])
        ge = per_lane("ge", [P, TILES, E1])
        gk = per_lane("gk", [P, TILES, E1])
        oh1 = per_lane("oh1", [P, TILES, E1])
        oh2 = per_lane("oh2", [P, TILES, E1])
        gate = per_lane("gate", [P, TILES, E1])
        gs = per_lane("gs", [P, 8, TILES])
        gT = per_lane("gT", [E1, NT])
        gTb = per_lane("gTb", [E1, NT], BF16)
        s8 = per_lane("s8", [P, H1 * TILES, BS1])
        s8b = per_lane("s8b", [P, H1 * TILES, BS1])
        s8s = per_lane("s8s", [P, 4, H1 * TILES])
        kf = [hid[l][:, 3, :].rearrange("p (b t d) -> p b t d", b=2, t=TILES) for l in lanes]
        sg = [hid[l][:, 0, :].bitcast(BF16).rearrange("p (b n) -> p b n", b=2) for l in lanes]
        pr = [hid[l][:, 1, :].bitcast(BF16).rearrange("p (b n) -> p b n", b=2) for l in lanes]
        sx = [hid[l][:, 2, :].bitcast(BF16)[:, 0:NT] for l in lanes]

        psA = [ctx.enter_context(nc.psum_tensor(f"psA{l}", [P, NT], F32)) for l in lanes]
        psB = [ctx.enter_context(nc.psum_tensor(f"psB{l}", [P, NT], F32)) for l in lanes]

        w3_bounce = nc.dram_tensor("w3_bounce", [SPLIT, E3, PAIRS * P], BF16).ap()

        ids_in = sem("ids_in")
        weights_in = sem("weights_in")
        gathered = sem("gathered")
        ids_ready = sem("ids_ready")
        v_chain = sem("v_chain")
        folded = sem("folded")
        unfolded = sem("unfolded")
        angles = sem("angles")
        waves = sem("waves")
        halves = sem("halves")
        w3_split = sem("w3_split")
        w3_out = sem("w3_out")
        w3_in = sem("w3_in")
        b_scaled = sem("b_scaled")
        N_WEIGHTS = 6

        with nc.Block() as block:
            @block.sync
            def _(sp):
                sp.dma_start(ids_sb[:, :], ids).then_inc(ids_in, 16)
                sp.dma_start(k64[:, :], w64).then_inc(weights_in, 16)
                sp.dma_start(kc[:, :], consts).then_inc(weights_in, 16)
                sp.dma_start(k65[:, :], w65).then_inc(weights_in, 16)
                sp.wait_ge(w3_split, 3)
                for s, part in enumerate((w3_hi, w3_mid, w3_lo)):
                    sp.dma_start(w3_bounce[s].rearrange("e (c x) -> (e c) x", x=256),
                                 part[:, :]).then_inc(w3_out, 16)
                sp.wait_ge(w3_out, 16 * SPLIT)
                sp.dma_start(w3_rows[:, :], w3_bounce.rearrange("s e x -> (s e) x")).then_inc(w3_in, 16)
                sp.wait_ge(w3_in, 16)

            @block.gpsimd
            def _(pool):
                pool.wait_ge(ids_in, 16)
                for s in range(NSEQ):
                    pool.indirect_dma_start(
                        emb[:, s, :], None, emb_w,
                        bass.IndirectOffsetOnAxis(ap=ids_sb[:, s:s + 1].bitcast(U32), axis=0)
                    ).then_inc(gathered, 16)
                pool.wait_ge(gathered, 16 * NSEQ)

            @block.tensor
            def _(pe):
                pe.wait_ge(weights_in, 16 * N_WEIGHTS)
                pe.matmul(psA[0][0:64, 0:D], c64("wq0"), c64("wk0"), start=True, stop=True)
                qb = c32("qb1").rearrange("e (h i) -> e h i", h=H1)
                kb = c32("kb1").rearrange("e (h i) -> e h i", h=H1)
                for hh in range(H1):
                    pe.matmul(psA[1][0:65, D1 * hh:D1 * (hh + 1)], qb[:, hh, :], c32("p1"),
                              start=True, stop=True)
                for hh in range(H1):
                    pe.matmul(psA[2][0:65, D1 * hh:D1 * (hh + 1)], kb[:, hh, :], c32("p1"),
                              start=True, stop=True).then_inc(folded, 1)
                pe.wait_ge(b_scaled, 2)
                pe.transpose(psA[3][0:64, 0:64], b_sc[:, 0, :], cc("ident", 64)[:, 0:64])
                pe.transpose(psA[3][0:64, 64:128], b_sc[:, 1, :], cc("ident", 64)[:, 0:64]).then_inc(folded, 1)

            @block.scalar
            def _(act):
                act.dma_start(k128[:, :], w128).then_inc(weights_in, 16)
                act.dma_start(k32[:, :], w32).then_inc(weights_in, 16)
                act.dma_start(krow[:, :], wrow.broadcast_to([P, CROW["_"][1]])).then_inc(weights_in, 16)
                act.wait_ge(folded, 2)
                act.activation(score0[:, :], psA[0][0:64, 0:D], ACT.Copy)
                act.activation(qp1[:, :], psA[1][0:65, 0:D], ACT.Copy, scale=float(D1) ** -0.5)
                act.activation(kp1[:, :], psA[2][0:65, 0:D], ACT.Copy)
                act.wait_ge(angles, 2)
                act.activation(sines[:, :], ph[:, 5, :], ACT.Sin)
                act.activation(cosines[:, :], ph[:, 7, :], ACT.Sin)

            @block.vector
            def _(dve):
                count = [0]

                def then(ins):
                    count[0] += 1
                    ins.then_inc(v_chain, 1)
                    dve.wait_ge(v_chain, count[0])

                V = nc.vector
                V.memset(neg_half[:, :], -0.5)
                for l in lanes:
                    V.memset(xT[l][64:65, :], 1.0)
                    V.memset(fm[l][64:65, :], 1.0)
                    V.memset(v_sb[l][:, :, D:KV2], 1.0)
                dve.wait_ge(ids_in, 16)
                then(V.tensor_copy(ids_f[:, :], ids_sb[:, :]))
                V.tensor_scalar(keep[:, :], ids_f[:, :], 0.0, None, ALU.not_equal)
                dve.wait_ge(weights_in, 16 * N_WEIGHTS)

                w3 = c128("w3")
                then(V.tensor_copy(w3_hi[:, :], w3))
                then(V.tensor_tensor(w3_r1[:, :], w3, w3_hi[:, :], ALU.subtract))
                then(V.tensor_copy(w3_mid[:, :], w3_r1[:, :]))
                then(V.tensor_tensor(w3_r2[:, :], w3_r1[:, :], w3_mid[:, :], ALU.subtract))
                V.tensor_copy(w3_lo[:, :], w3_r2[:, :]).then_inc(w3_split, 3)

                def exponential(dst, src, n):
                    x, r, k, p = (ex[:, i, 0:n] for i in range(4))
                    then(V.tensor_scalar(x, src, -87.0, 88.0, ALU.max, ALU.min))
                    then(V.tensor_scalar(k, x, LOG2E, MAGIC, ALU.mult, ALU.add))
                    then(V.tensor_scalar(k, k, MAGIC, None, ALU.subtract))
                    then(V.scalar_tensor_tensor(r, k, -LN2_HI, x, ALU.mult, ALU.add))
                    then(V.scalar_tensor_tensor(r, k, -LN2_LO, r, ALU.mult, ALU.add))
                    then(V.tensor_scalar(p, r, 1.0 / 5040.0, 1.0 / 720.0, ALU.mult, ALU.add))
                    for c in (1.0 / 120.0, 1.0 / 24.0, 1.0 / 6.0, 0.5, 1.0, 1.0):
                        then(V.tensor_tensor(p, p, r, ALU.mult))
                        then(V.tensor_scalar(p, p, c, None, ALU.add))
                    then(V.tensor_scalar(ex_i[:, 0:n], k, 127.0, None, ALU.add))
                    then(V.tensor_scalar(ex_i[:, 0:n], ex_i[:, 0:n], 23, None, ALU.logical_shift_left))
                    then(V.tensor_tensor(dst, p, ex_i[:, 0:n].bitcast(F32), ALU.mult))

                V.tensor_copy(ln_logs[:, 0:2], k128[:, C128["nu"][0]:C128["theta"][1]])
                V.memset(ln_logs[64:128, 2:3], 0.0)
                then(V.tensor_copy(ln_logs[0:64, 2:3], c64("gamma3")))
                exponential(ex[:, 4, :], ln_logs[:, :], 3)
                for part, name in enumerate(("b_re", "b_im")):
                    V.tensor_scalar(b_sc[:, part, :], c64(name), ex[0:64, 4, 2:3], None,
                                    ALU.mult).then_inc(b_scaled, 1)
                then(V.tensor_scalar(th[:, 0:1], ex[:, 4, 0:1], -1.0, None, ALU.mult))
                then(V.tensor_copy(th[:, 1:2], ex[:, 4, 1:2]))
                exponential(th[:, 2:3], th[:, 0:1], 1)
                later = cc("later")[:, None, :].broadcast_to([P, TILES, P])
                V.tensor_scalar(decay3[:, :].rearrange("p (t s) -> p t s", t=TILES), later,
                                th[:, 2:3], None, ALU.mult)
                then(V.tensor_scalar(th[:, 3:4], th[:, 1:2], 0.5 / PI, MAGIC, ALU.mult, ALU.add))
                then(V.tensor_scalar(th[:, 3:4], th[:, 3:4], MAGIC, None, ALU.subtract))
                for c in (TWO_PI_1, TWO_PI_2, TWO_PI_3):
                    then(V.scalar_tensor_tensor(th[:, 1:2], th[:, 3:4], -c, th[:, 1:2], ALU.mult, ALU.add))
                then(V.tensor_scalar(th[:, 4:5], th[:, 1:2], QUANT, None, ALU.add))
                then(V.tensor_scalar(th[:, 4:5], th[:, 4:5], QUANT, None, ALU.subtract))
                then(V.tensor_tensor(th[:, 5:6], th[:, 1:2], th[:, 4:5], ALU.subtract))
                then(V.tensor_scalar(ph[:, 0, :], cc("time"), th[:, 4:5], None, ALU.mult))
                then(V.tensor_scalar(ph[:, 1, :], ph[:, 0, :], 0.5 / PI, MAGIC, ALU.mult, ALU.add))
                then(V.tensor_scalar(ph[:, 1, :], ph[:, 1, :], MAGIC, None, ALU.subtract))
                then(V.tensor_scalar(ph[:, 2, :], cc("time"), th[:, 5:6], None, ALU.mult))
                for c in (TWO_PI_1, TWO_PI_2, TWO_PI_3):
                    then(V.scalar_tensor_tensor(ph[:, 0, :], ph[:, 1, :], -c, ph[:, 0, :], ALU.mult, ALU.add))
                then(V.tensor_tensor(ph[:, 3, :], ph[:, 0, :], ph[:, 2, :], ALU.add))
                V.tensor_scalar(ph[:, 5, :], ph[:, 3, :], -3.1415925, 3.1415925, ALU.max, ALU.min).then_inc(angles, 1)
                then(V.tensor_scalar(ph[:, 6, :], ph[:, 3, :], HALF_PI, None, ALU.add))
                then(V.tensor_scalar(ph[:, 4, :], ph[:, 6, :], PI, -2.0 * PI, ALU.is_gt, ALU.mult))
                then(V.tensor_tensor(ph[:, 6, :], ph[:, 6, :], ph[:, 4, :], ALU.add))
                V.tensor_scalar(ph[:, 7, :], ph[:, 6, :], -3.1415925, 3.1415925, ALU.max, ALU.min).then_inc(angles, 1)
                V.tensor_scalar(c_cos[:, :], c128("c_a"), cc("sign"), None, ALU.mult)
                V.tensor_scalar(c_sin[:, :], c128("c_b"), -1.0, None, ALU.mult)
                V.tensor_scalar(diag3[:, :], cc("ident", 64)[:, 0:64], c64("d3"), None, ALU.mult)
                V.tensor_copy(sel_bf[:, :], cc("exp1", E1))
                V.tensor_copy(pick3[:, :], cc("pick3"))
                dve.wait_ge(folded, 3)
                V.tensor_copy(b1_3[:, :], psA[3][0:64, 0:P])
                V.tensor_copy(b2_3[:, 0:64], psA[3][0:64, 64:128])
                V.tensor_scalar(b2_3[:, 64:128], psA[3][0:64, 0:64], -1.0, None, ALU.mult)

        first = sems[0].num
        nc.sync.sem_clear(range(first, sems[-1].num + 1))
        nc.all_engine_barrier()

        sems_setup = len(sems)
        h_new = sem("h_new")
        y_new = sem("y_new")
        ln_sum = sem("ln_sum")
        ln_cen = sem("ln_cen")
        ln_sq = sem("ln_sq")
        ln_var = sem("ln_var")
        ln_vare = sem("ln_vare")
        ln_rstd = sem("ln_rstd")
        ln_out = sem("ln_out")
        ln_scaled = sem("ln_scaled")
        ln_affine = sem("ln_affine")
        x_turned = sem("x_turned")
        x_ready = sem("x_ready")
        logits = sem("logits")
        gstep = sem("gstep")
        g_exp = sem("g_exp")
        g_done = sem("g_done")
        g_turned = sem("g_turned")
        gT_ready = sem("gT_ready")
        gTb_ready = sem("gTb_ready")
        a0_rv = sem("a0_rv")
        a0_r = sem("a0_r")
        a0_v = sem("a0_v")
        a0_s = sem("a0_s")
        a0_p = sem("a0_p")
        a0_o = sem("a0_o")
        m0_z = sem("m0_z")
        m0_h = sem("m0_h")
        m0_o = sem("m0_o")
        m0_half = sem("m0_half")
        m0_acc = sem("m0_acc")
        m0_b = sem("m0_b")
        a1_qk = sem("a1_qk")
        a1_q = sem("a1_q")
        a1_k = sem("a1_k")
        a1_v = sem("a1_v")
        a1_vs = sem("a1_vs")
        a1_s = sem("a1_s")
        a1_m = sem("a1_m")
        a1_e8 = sem("a1_e8")
        a1_step = sem("a1_step")
        a1_exp = sem("a1_exp")
        a1_full = sem("a1_full")
        a1_turned = sem("a1_turned")
        a1_aT = sem("a1_aT")
        a1_o = sem("a1_o")
        m1_z = sem("m1_z")
        m1_h = sem("m1_h")
        m1_o = sem("m1_o")
        a2_q = sem("a2_q")
        a2_kv = sem("a2_kv")
        a2_qe = sem("a2_qe")
        a2_ke = sem("a2_ke")
        a2_qf = sem("a2_qf")
        a2_kf = sem("a2_kf")
        a2_v = sem("a2_v")
        a2_s = sem("a2_s")
        a2_sm = sem("a2_sm")
        a2_n = sem("a2_n")
        a2_step = sem("a2_step")
        a2_z = sem("a2_z")
        a2_g = sem("a2_g")
        a2_y = sem("a2_y")
        m2_z = sem("m2_z")
        m2_h = sem("m2_h")
        m2_g = sem("m2_g")
        m2_hg = sem("m2_hg")
        m2_o = sem("m2_o")
        m2_res = sem("m2_res")
        a3_p = sem("a3_p")
        a3_m = sem("a3_m")
        a3_w = sem("a3_w")
        a3_z = sem("a3_z")
        a3_c = sem("a3_c")
        a3_y = sem("a3_y")
        m3_sx = sem("m3_sx")
        m3_z = sem("m3_z")
        m3_g = sem("m3_g")
        m3_w = sem("m3_w")
        m3_s = sem("m3_s")
        m3_p = sem("m3_p")
        m3_used = sem("m3_used")
        m3_y = sem("m3_y")
        m3_ys = sem("m3_ys")
        m3_t = sem("m3_t")
        stored = sem("stored")

        (LN_A0, LN_M0, LN_IN0, LN_A1, LN_M1, LN_A2, LN_IN2, LN_OUT2, LN_M2, LN_A3, LN_M3) = range(N_LN)
        (H_EMB, H_A0, H_M0, H_A1, H_M1, H_A2, H_M2, H_A3, H_OUT) = range(9)
        (X_A0, X_M0, X_A1, X_M1, X_A2, X_IN2, X_M2, X_A3, X_M3) = range(NT_USES)
        G_M0, G_M1, G_M2 = range(3)
        Y_IN0, Y_IN2, Y_OUT2 = range(3)
        TOP2_DIFF, TOP2_STEPS, TOP1_STEPS = 12, 18, 6

        def rows(ap):
            return ap[:, 0:TILES * D].rearrange("p (t d) -> p t d", t=TILES)

        def spread(stat_ap, n):
            return stat_ap[:, :, None].broadcast_to([P, TILES, n])

        with nc.Fori(0, PASSES) as it:
            with nc.Block() as block:

                @block.sync
                def _(sp):
                    for l in lanes:
                        sp.wait_ge(h_new, nth(l, H_OUT))
                        sp.dma_start(out[it, l].rearrange("t p d -> p t d"), h[l][:, :, :]).then_inc(stored, 16)
                    sp.wait_ge(stored, 16 * LANES)

                @block.gpsimd
                def _(pool):
                    G = nc.gpsimd

                    def rstd(use):
                        for l in lanes:
                            pool.wait_ge(ln_var, nth(l, use))
                            G.tensor_scalar(stat[l][:, 2, :], stat[l][:, 1, :], 1.0 / D, LN_EPS,
                                            ALU.mult, ALU.add).then_inc(ln_vare, 1)
                        for l in lanes:
                            pool.wait_ge(ln_vare, nth(l, use))
                            G.tensor_tensor(stat[l][:, 3, :], stat[l][:, 2, :], neg_half[:, :],
                                            ALU.pow).then_inc(ln_rstd, 1)

                    def affine(ln, use, gamma, beta):
                        for l in lanes:
                            pool.wait_ge(ln_out, nth(l, ln))
                            G.tensor_tensor(aff[l][:, :, :], xn[l][:, :, :], crow(gamma), ALU.mult).then_inc(ln_scaled, 1)
                        for l in lanes:
                            pool.wait_ge(ln_scaled, nth(l, use))
                            G.tensor_tensor(aff[l][:, :, :], aff[l][:, :, :], crow(beta), ALU.add).then_inc(ln_affine, 1)

                    rstd(LN_A0)
                    rstd(LN_M0)
                    rstd(LN_IN0)
                    affine(LN_IN0, 0, "g0", "be0")
                    rstd(LN_A1)
                    block1 = cc("block").rearrange("p (g j) -> p g j", j=BS1)[:, None, :, :].broadcast_to(
                        [P, TILES, P // BS1, BS1])
                    for l in lanes:
                        pool.wait_ge(a1_step, nth(l, 4))
                        for hh, dst in enumerate((big_a, big_b)):
                            w = s8[l][:, TILES * hh:TILES * (hh + 1), None, :].broadcast_to([P, TILES, P // BS1, BS1])
                            G.tensor_tensor(dst[l][:, :].rearrange("p (t g j) -> p t g j", t=TILES, j=BS1),
                                            w, block1, ALU.mult).then_inc(a1_full, 1)
                    rstd(LN_M1)
                    rstd(LN_A2)
                    rstd(LN_IN2)
                    affine(LN_IN2, 1, "g2a", "be2a")
                    rstd(LN_OUT2)
                    affine(LN_OUT2, 2, "g2b", "be2b")
                    rstd(LN_M2)
                    for l in lanes:
                        pool.wait_ge(ln_out, nth(l, LN_M2))
                        G.tensor_tensor(y[l][:, :, :], h[l][:, :, :], xn[l][:, :, :], ALU.add).then_inc(m2_res, 1)
                    rstd(LN_A3)
                    for l in lanes:
                        pool.wait_ge(a3_m, 2 * (l + 1))
                        G.tensor_tensor(big_c[l][:, :], big_a[l][:, :], big_b[l][:, :], ALU.add).then_inc(a3_w, 1)
                    for l in lanes:
                        pool.wait_ge(a3_z, nth(l))
                        for wave, dst in ((cosines, big_a), (sines, big_b)):
                            G.tensor_tensor(dst[l][:, :].rearrange("p (t s) -> p t s", t=TILES),
                                            hid[l][:, 0, :].rearrange("p (t s) -> p t s", t=TILES),
                                            wave[:, None, :].broadcast_to([P, TILES, P]), ALU.mult).then_inc(a3_c, 1)
                    rstd(LN_M3)

                @block.scalar
                def _(act):
                    def squares(use):
                        for l in lanes:
                            act.wait_ge(ln_cen, nth(l, use))
                            act.activation(sq[l][:, :, :], cen[l][:, :, :], ACT.Square).then_inc(ln_sq, 1)

                    def turned(use):
                        for l in lanes:
                            act.wait_ge(x_turned, nth(l, use))
                            act.activation(xT[l][0:64, :], psA[l][0:64, :], ACT.Copy).then_inc(x_ready, 1)

                    def gate_exp(use):
                        for l in lanes:
                            act.wait_ge(gstep, nth(l, use * (TOP2_STEPS + TOP1_STEPS) + TOP2_DIFF))
                            act.activation(gs[l][:, 4, :], gs[l][:, 3, :], ACT.Exp).then_inc(g_exp, 1)

                    def gates_turned(use, E):
                        for l in lanes:
                            act.wait_ge(g_turned, nth(l, use))
                            act.activation(gT[l][0:E, :], psA[l][0:E, :], ACT.Copy).then_inc(gT_ready, 1)

                    squares(LN_A0)
                    turned(X_A0)
                    for l in lanes:
                        act.wait_ge(a0_rv, nth(l))
                        act.activation(fm[l][0:64, :], psB[l][0:64, :], ACT.Copy).then_inc(a0_r, 1)
                    squares(LN_M0)
                    turned(X_M0)
                    gate_exp(0)
                    gates_turned(G_M0, E0)
                    for e in range(E0):
                        for l in lanes:
                            act.wait_ge(m0_z, nth(l, e))
                            if e >= 4:
                                act.wait_ge(m0_o, nth(l, e // 2 - 2))
                            act.activation(hid[l][:, e % 4, :], psA[l][:, :], ACT.Relu).then_inc(m0_h, 1)
                    squares(LN_IN0)
                    squares(LN_A1)
                    turned(X_A1)
                    for l in lanes:
                        act.wait_ge(a1_qk, nth(l))
                        act.activation(fm[l][0:64, :], psA[l][0:64, :], ACT.Copy).then_inc(a1_q, 1)
                    for l in lanes:
                        act.wait_ge(a1_step, nth(l, 1))
                        act.activation(s8b[l][:, :, :], s8b[l][:, :, :], ACT.Exp).then_inc(a1_exp, 1)
                    for l in lanes:
                        act.wait_ge(a1_turned, nth(l))
                        act.activation(hid[l][:, 0, :], psA[l][:, :], ACT.Copy)
                        act.activation(hid[l][:, 1, :], psB[l][:, :], ACT.Copy).then_inc(a1_aT, 1)
                    squares(LN_M1)
                    turned(X_M1)
                    gates_turned(G_M1, E1)
                    for m in range(0, MT, 2):
                        for l in lanes:
                            act.wait_ge(m1_z, nth(l, m))
                            act.activation(hid[l][:, m, :], psA[l][:, :], ACT.Relu).then_inc(m1_h, 1)
                    squares(LN_A2)
                    turned(X_A2)
                    for l in lanes:
                        act.wait_ge(a2_q, nth(l))
                        act.activation(fm2[l][:, :], psB[l][0:64, :], ACT.Exp)
                        act.activation(big_a[l][0:64, :], psB[l][0:64, :], ACT.Relu).then_inc(a2_qe, 1)
                        act.wait_ge(a2_kv, nth(l))
                        kv = psA[l][:, :].rearrange("p (t c) -> p t c", t=TILES)
                        act.activation(kf[l][:, 0, :, :], kv[:, :, 0:D], ACT.Exp)
                        act.activation(kf[l][:, 1, :, :], kv[:, :, 0:D], ACT.Relu).then_inc(a2_ke, 1)
                    squares(LN_IN2)
                    turned(X_IN2)
                    for l in lanes:
                        act.wait_ge(a2_z, nth(l))
                        act.activation(fm[l][0:64, :], psB[l][0:64, :], ACT.Gelu, bias=c64("b1_2a")).then_inc(a2_g, 1)
                    squares(LN_OUT2)
                    squares(LN_M2)
                    turned(X_M2)
                    gate_exp(1)
                    gates_turned(G_M2, E2)
                    for m in range(MT):
                        for l in lanes:
                            act.wait_ge(m2_z, nth(l, m))
                            act.activation(hid[l][:, m, :], psA[l][:, :], ACT.Gelu).then_inc(m2_h, 1)
                    squares(LN_A3)
                    turned(X_A3)
                    squares(LN_M3)
                    for l in lanes:
                        act.wait_ge(x_turned, nth(l, X_M3))
                        act.activation(xT[l][0:64, :], psA[l][0:64, :], ACT.Copy).then_inc(x_ready, 1)
                        act.activation(sx[l][0:64, :], psA[l][0:64, :], ACT.Sign)
                        act.activation(sx[l][64:128, :], psA[l][0:64, :], ACT.Sign).then_inc(m3_sx, 1)
                    for p in range(PAIRS):
                        for l in lanes:
                            act.wait_ge(m3_w, nth(l, p))
                            if p >= 2:
                                act.wait_ge(m3_p, nth(l, p - 2))
                            act.activation(sg[l][:, p % 2, :], psA[l][:, :], ACT.Sign).then_inc(m3_s, 1)

                @block.tensor
                def _(pe):
                    def turn(ln, use, src, ready):
                        for l in lanes:
                            pe.wait_ge(ready, ln(l))
                            for t in range(TILES):
                                last = pe.transpose(psA[l][0:64, P * t:P * (t + 1)], src[l][:, t, :], ident)
                            last.then_inc(x_turned, 1)

                    def tile(ap, t):
                        return ap[:, P * t:P * (t + 1)]

                    def route(use, x_use, name, E):
                        for l in lanes:
                            pe.wait_ge(x_ready, nth(l, x_use))
                            for t in range(TILES):
                                last = pe.matmul(psB[l][:, E * t:E * (t + 1)], tile(xT[l], t), c65(name),
                                                 start=True, stop=True)
                            last.then_inc(logits, 1)

                    def turn_gates(use, src, E):
                        for l in lanes:
                            pe.wait_ge(g_done, nth(l, use))
                            for t in range(TILES):
                                last = pe.transpose(psA[l][0:E, P * t:P * (t + 1)], src[l][:, t, 0:E], ident)
                            last.then_inc(g_turned, 1)

                    turn(lambda l: nth(l, LN_A0), X_A0, xn, ln_out)
                    for l in lanes:
                        pe.wait_ge(x_ready, nth(l, X_A0))
                        pe.matmul(psB[l][0:64, :], score0[:, :], xT[l][0:64, :], start=True, stop=True)
                        for t in range(TILES):
                            last = pe.matmul(psA[l][:, D * t:D * (t + 1)], tile(xT[l][0:64, :], t), c64("wv0"),
                                             start=True, stop=True)
                        last.then_inc(a0_rv, 1)
                    for l in lanes:
                        pe.wait_ge(a0_r, nth(l))
                        for t in range(TILES):
                            last = pe.matmul(tile(psB[l], t), tile(xT[l][0:64, :], t), tile(fm[l][0:64, :], t),
                                             start=True, stop=True)
                        last.then_inc(a0_s, 1)
                    for l in lanes:
                        pe.wait_ge(a0_v, nth(l))
                        pe.wait_ge(a0_p, nth(l))
                        for t in range(TILES):
                            last = pe.matmul(psA[l][:, D * t:D * (t + 1)], tile(big_a[l], t), v_sb[l][:, t, 0:D],
                                             start=True, stop=True)
                        last.then_inc(a0_o, 1)

                    turn(lambda l: nth(l, LN_M0), X_M0, xn, ln_out)
                    route(G_M0, X_M0, "gate0", E0)
                    turn_gates(G_M0, gate, E0)

                    def up0(e):
                        a = C65["w1_0"][0] + F0 * e
                        for l in lanes:
                            if e == 0:
                                pe.wait_ge(gT_ready, nth(l, G_M0))
                            else:
                                pe.wait_ge(m0_h, nth(l, e - 1))
                            pe.matmul(psA[l][:, :], k65[:, a:a + F0], xT[l][:, :], start=True, stop=True).then_inc(m0_z, 1)

                    def down0(q):
                        for l in lanes:
                            pe.wait_ge(m0_h, nth(l, 2 * q + 1))
                            if q:
                                pe.wait_ge(m0_acc, nth(l, q - 1))
                            for e in (2 * q, 2 * q + 1):
                                a = C128["w2_0"][0] + D * e
                                for t in range(TILES):
                                    at = 256 * (e % 2) + D * t
                                    last = pe.matmul(psB[l][:, at:at + D], tile(hid[l][:, e % 4, :], t),
                                                     k128[:, a:a + D], start=True, stop=True)
                            last.then_inc(m0_o, 1)

                    up0(0)
                    up0(1)
                    for q in range(E0 // 2):
                        for e in (2 * q + 2, 2 * q + 3):
                            if e < E0:
                                up0(e)
                        down0(q)
                    for l in lanes:
                        for t in range(TILES):
                            last = pe.matmul(psA[l][:, D * t:D * (t + 1)], tile(gT[l][0:E0, :], t),
                                             c32("b2_0", E0), start=True, stop=True)
                        last.then_inc(m0_b, 1)

                    turn(lambda l: nth(l, LN_A1), X_A1, xn, ln_out)
                    for l in lanes:
                        pe.wait_ge(x_ready, nth(l, X_A1))
                        pe.matmul(psA[l][0:64, :], qp1[:, :], xT[l][:, :], start=True, stop=True)
                        pe.matmul(psB[l][0:64, :], kp1[:, :], xT[l][:, :], start=True, stop=True).then_inc(a1_qk, 1)
                    for l in lanes:
                        pe.wait_ge(a1_q, nth(l))
                        for t in range(TILES):
                            last = pe.matmul(psA[l][:, D * t:D * (t + 1)], tile(xT[l], t), c65("wv1"),
                                             start=True, stop=True)
                        last.then_inc(a1_v, 1)
                    for l in lanes:
                        pe.wait_ge(a1_k, nth(l))
                        pe.wait_ge(a1_vs, nth(l))
                        for hh, ps in enumerate((psA, psB)):
                            r = slice(D1 * hh, D1 * (hh + 1))
                            for t in range(TILES):
                                last = pe.matmul(tile(ps[l], t), tile(fm[l][r, :], t), tile(fm2[l][r, :], t),
                                                 start=True, stop=True)
                        last.then_inc(a1_s, 1)
                    for l in lanes:
                        pe.wait_ge(a1_full, 2 * (l + 1))
                        pe.wait_ge(a1_m, 2 * (l + 1))
                        for ps, src in ((psA, big_a), (psB, big_b)):
                            for t in range(TILES):
                                last = pe.transpose(tile(ps[l], t), tile(src[l], t), ident)
                        last.then_inc(a1_turned, 1)
                    for l in lanes:
                        pe.wait_ge(a1_aT, nth(l))
                        for t in range(TILES):
                            for hh in range(H1):
                                c = D1 * hh
                                last = pe.matmul(psA[l][:, D * t + c:D * t + c + D1], tile(hid[l][:, hh, :], t),
                                                 v_sb[l][:, t, c:c + D1], start=True, stop=True)
                        last.then_inc(a1_o, 1)

                    turn(lambda l: nth(l, LN_M1), X_M1, xn, ln_out)
                    route(G_M1, X_M1, "route1", E1)
                    turn_gates(G_M1, oh1, E1)
                    for m in range(MT):
                        a = C65["w1_1"][0] + P * m
                        for l in lanes:
                            ps = (psA, psB)[m % 2]
                            if m == 0:
                                pe.wait_ge(gTb_ready, nth(l))
                                pe.wait_ge(gT_ready, nth(l, G_M1))
                            if m >= 2:
                                pe.wait_ge((m1_h, m1_o)[m % 2], nth(l, 0))
                            pe.matmul(ps[l][:, :], k65[:, a:a + P], xT[l][:, :], start=True, stop=False)
                            pe.matmul(ps[l][:, :], sel_bf[:, P * m:P * (m + 1)], gTb[l][:, :],
                                      start=False, stop=True).then_inc(m1_z, 1)
                    for l in lanes:
                        pe.wait_ge(m1_h, nth(l, 1))
                        pe.wait_ge(m1_o, nth(l, 1))
                        for t in range(TILES):
                            o = psA[l][:, D * t:D * (t + 1)]
                            for m in range(MT):
                                a = C128["w2_1"][0] + D * m
                                pe.matmul(o, tile(hid[l][:, m, :], t), k128[:, a:a + D], start=(m == 0), stop=False)
                            last = pe.matmul(o, tile(gT[l][:, :], t), c32("b2_1"), start=False, stop=True)
                        last.then_inc(m1_z, 1)

                    turn(lambda l: nth(l, LN_A2), X_A2, xn, ln_out)
                    for l in lanes:
                        pe.wait_ge(x_ready, nth(l, X_A2))
                        pe.matmul(psB[l][0:64, :], c64("q2"), xT[l][0:64, :], start=True, stop=True).then_inc(a2_q, 1)
                        for t in range(TILES):
                            last = pe.matmul(tile(psA[l], t), tile(xT[l][0:64, :], t), c64("kv2"), start=True, stop=True)
                        last.then_inc(a2_kv, 1)
                    for l in lanes:
                        pe.wait_ge(a2_qe, nth(l))
                        pe.wait_ge(a2_kf, nth(l))
                        pe.wait_ge(a2_v, nth(l))
                        for t in range(TILES):
                            last = pe.matmul(psB[l][0:64, KV2 * t:KV2 * (t + 1)], kf[l][:, 0, t, :], v_sb[l][:, t, :],
                                             start=True, stop=True)
                        last.then_inc(a2_s, 1)
                    for l in lanes:
                        pe.wait_ge(a2_qf, nth(l))
                        pe.wait_ge(a2_sm, nth(l))
                        for t in range(TILES):
                            last = pe.matmul(psA[l][:, KV2 * t:KV2 * (t + 1)], tile(fm2[l], t), kvm[l][:, t, :],
                                             start=True, stop=True)
                        last.then_inc(a2_n, 1)
                    turn(lambda l: nth(l, 1), X_IN2, aff, ln_affine)
                    for l in lanes:
                        pe.wait_ge(x_ready, nth(l, X_IN2))
                        pe.matmul(psB[l][0:64, :], c64("w1_2a"), xT[l][0:64, :], start=True, stop=True).then_inc(a2_z, 1)
                    for l in lanes:
                        pe.wait_ge(a2_g, nth(l))
                        for t in range(TILES):
                            last = pe.matmul(psA[l][:, D * t:D * (t + 1)], tile(fm[l], t), c65("w2_2a"),
                                             start=True, stop=True)
                        last.then_inc(a2_y, 1)

                    turn(lambda l: nth(l, LN_M2), X_M2, xn, ln_out)
                    route(G_M2, X_M2, "route2", E2)
                    turn_gates(G_M2, gate, E2)
                    for m in range(MT):
                        a = C65["w1_2"][0] + P * m
                        for l in lanes:
                            if m == 0:
                                pe.wait_ge(gT_ready, nth(l, G_M2))
                            else:
                                pe.wait_ge(m2_h, nth(l, m - 1))
                            pe.matmul(psA[l][:, :], k65[:, a:a + P], xT[l][:, :], start=True, stop=True).then_inc(m2_z, 1)
                            if m:
                                pe.wait_ge(m2_hg, nth(l, m - 1))
                            pe.matmul(psB[l][:, :], cc("sel2", E2)[:, P * m:P * (m + 1)], gT[l][0:E2, :],
                                      start=True, stop=True).then_inc(m2_g, 1)
                    for l in lanes:
                        pe.wait_ge(m2_hg, nth(l, MT - 1))
                        for t in range(TILES):
                            o = psA[l][:, D * t:D * (t + 1)]
                            for m in range(MT):
                                a = C128["w2_2"][0] + D * m
                                pe.matmul(o, tile(hid[l][:, m, :], t), k128[:, a:a + D], start=(m == 0), stop=False)
                            last = pe.matmul(o, tile(gT[l][0:E2, :], t), c32("b2_2", E2), start=False, stop=True)
                        last.then_inc(m2_o, 1)

                    turn(lambda l: nth(l, LN_A3), X_A3, xn, ln_out)
                    for l in lanes:
                        pe.wait_ge(x_ready, nth(l, X_A3))
                        pe.matmul(psA[l][:, :], b1_3[:, :], xT[l][0:64, :], start=True, stop=True)
                        pe.matmul(psB[l][:, :], b2_3[:, :], xT[l][0:64, :], start=True, stop=True).then_inc(a3_p, 1)
                    for l in lanes:
                        pe.wait_ge(a3_c, 2 * (l + 1))
                        for t in range(TILES):
                            o = psA[l][:, D * t:D * (t + 1)]
                            pe.matmul(o, tile(big_a[l], t), c_cos[:, :], start=True, stop=False)
                            pe.matmul(o, tile(big_b[l], t), c_sin[:, :], start=False, stop=False)
                            last = pe.matmul(o, tile(xT[l][0:64, :], t), diag3[:, :], start=False, stop=True)
                        last.then_inc(a3_y, 1)

                    turn(lambda l: nth(l, LN_M3), X_M3, xn, ln_out)
                    for l in lanes:
                        pe.wait_ge(x_ready, nth(l, X_M3))
                        pe.matmul(psB[l][0:G3, :], c65("proj3"), xT[l][:, :], start=True, stop=True).then_inc(m3_z, 1)

                    def weights3(p):
                        for l in lanes:
                            if p == 0:
                                pe.wait_ge(m3_g, nth(l))
                                pe.wait_ge(m3_sx, nth(l))
                            else:
                                pe.wait_ge(m3_s, nth(l, p - 1))
                            pe.matmul(psA[l][:, :], w3_rows[:, P * p:P * (p + 1)], big3[l],
                                      start=True, stop=True).then_inc(m3_w, 1)

                    def gather3(p):
                        for l in lanes:
                            pe.wait_ge(m3_p, nth(l, p))
                            a = D - 2 * p
                            pe.matmul(psB[l][0:64, :], pick3[:, a:a + D], pr[l][:, p % 2, :],
                                      start=(p == 0), stop=(p == PAIRS - 1)).then_inc(m3_used, 1)

                    big3 = [gTb[l][0:G3, :] for l in lanes]
                    weights3(0)
                    for p in range(PAIRS):
                        if p + 1 < PAIRS:
                            weights3(p + 1)
                        gather3(p)
                    for l in lanes:
                        pe.wait_ge(m3_ys, nth(l))
                        for t in range(TILES):
                            last = pe.transpose(psA[l][:, D * t:D * (t + 1)], tile(fm2[l], t), cc("ident", 64)[:, 0:64])
                        last.then_inc(m3_t, 1)

                @block.vector
                def _(dve):
                    V = nc.vector

                    def norm(use, src, ready, at):
                        for l in lanes:
                            dve.wait_ge(ready, nth(l, at))
                            V.tensor_reduce(stat[l][:, 0, :], src[l][:, :, :], X, ALU.add).then_inc(ln_sum, 1)
                        for l in lanes:
                            dve.wait_ge(ln_sum, nth(l, use))
                            V.scalar_tensor_tensor(cen[l][:, :, :], spread(stat[l][:, 0, :], D), -1.0 / D,
                                                   src[l][:, :, :], ALU.mult, ALU.add).then_inc(ln_cen, 1)
                        for l in lanes:
                            dve.wait_ge(ln_sq, nth(l, use))
                            V.tensor_reduce(stat[l][:, 1, :], sq[l][:, :, :], X, ALU.add).then_inc(ln_var, 1)
                        for l in lanes:
                            dve.wait_ge(ln_rstd, nth(l, use))
                            V.tensor_tensor(xn[l][:, :, :], cen[l][:, :, :], spread(stat[l][:, 3, :], D),
                                            ALU.mult).then_inc(ln_out, 1)

                    gcount = [0]

                    def gstep_all(emit):
                        for l in lanes:
                            if gcount[0]:
                                dve.wait_ge(gstep, nth(l, gcount[0] - 1))
                            emit(l).then_inc(gstep, 1)
                        gcount[0] += 1

                    def first_of(E, scores, peak, onehot):
                        def w(b, l):
                            return b[l][:, :, 0:E]
                        gstep_all(lambda l: V.tensor_reduce(gs[l][:, peak, :], w(scores, l), X, ALU.max))
                        gstep_all(lambda l: V.tensor_tensor(w(ge, l), w(scores, l), spread(gs[l][:, peak, :], E), ALU.is_equal))
                        gstep_all(lambda l: V.tensor_tensor(w(gk, l), w(ge, l), rank(E), ALU.mult))
                        gstep_all(lambda l: V.tensor_reduce(gs[l][:, 2, :], w(gk, l), X, ALU.max))
                        gstep_all(lambda l: V.tensor_tensor(w(onehot, l), w(gk, l), spread(gs[l][:, 2, :], E), ALU.is_equal))

                    def copy_logits(use, E):
                        for l in lanes:
                            dve.wait_ge(logits, nth(l, use))
                            V.tensor_copy(lg[l][:, :, 0:E], psB[l][:, 0:TILES * E].rearrange("p (t e) -> p t e", e=E)
                                          ).then_inc(gstep, 1)
                        gcount[0] += 1

                    def top2(use, E):
                        def w(b, l):
                            return b[l][:, :, 0:E]
                        copy_logits(use, E)
                        first_of(E, lg, 0, oh1)
                        gstep_all(lambda l: V.scalar_tensor_tensor(w(lg, l), w(oh1, l), -BIG, w(lg, l), ALU.mult, ALU.add))
                        first_of(E, lg, 1, oh2)
                        gstep_all(lambda l: V.tensor_tensor(gs[l][:, 3, :], gs[l][:, 1, :], gs[l][:, 0, :], ALU.subtract))
                        turn = {G_M0: 0, G_M2: 1}[use]
                        for l in lanes:
                            dve.wait_ge(g_exp, nth(l, turn))
                        gstep_all(lambda l: V.tensor_scalar(gs[l][:, 5, :], gs[l][:, 4, :], 1.0, None, ALU.add))
                        gstep_all(lambda l: V.reciprocal(gs[l][:, 6, :], gs[l][:, 5, :]))
                        gstep_all(lambda l: V.tensor_tensor(gs[l][:, 7, :], gs[l][:, 6, :], gs[l][:, 4, :], ALU.mult))
                        gstep_all(lambda l: V.tensor_tensor(w(ge, l), w(oh1, l), spread(gs[l][:, 6, :], E), ALU.mult))
                        gstep_all(lambda l: V.tensor_tensor(w(gk, l), w(oh2, l), spread(gs[l][:, 7, :], E), ALU.mult))
                        for l in lanes:
                            dve.wait_ge(gstep, nth(l, gcount[0] - 1))
                            V.tensor_tensor(w(gate, l), w(ge, l), w(gk, l), ALU.add).then_inc(g_done, 1)

                    def add_psum(done, at, use):
                        for l in lanes:
                            dve.wait_ge(done, at(l))
                            V.tensor_tensor(h[l][:, :, :], rows(psA[l]), h[l][:, :, :], ALU.add).then_inc(h_new, 1)

                    for l in lanes:
                        src = emb[:, bass.ds(it * (LANES * TILES) + l * TILES, TILES), :]
                        kp = keep[:, bass.ds(it * (LANES * TILES) + l * TILES, TILES)]
                        V.tensor_tensor(h[l][:, :, :], src, kp[:, :, None].broadcast_to([P, TILES, D]),
                                        ALU.mult).then_inc(h_new, 1)

                    norm(LN_A0, h, h_new, H_EMB)
                    for l in lanes:
                        dve.wait_ge(a0_rv, nth(l))
                        V.tensor_copy(v_sb[l][:, :, 0:D], rows(psA[l])).then_inc(a0_v, 1)
                    for l in lanes:
                        dve.wait_ge(a0_s, nth(l))
                        V.tensor_tensor(big_a[l][:, :].rearrange("p (t s) -> p t s", t=TILES),
                                        psB[l][:, :].rearrange("p (t s) -> p t s", t=TILES),
                                        cc("decay")[:, None, :].broadcast_to([P, TILES, P]), ALU.mult).then_inc(a0_p, 1)
                    add_psum(a0_o, lambda l: nth(l), H_A0)

                    norm(LN_M0, h, h_new, H_A0)
                    top2(G_M0, E0)
                    for q in range(E0 // 2):
                        for l in lanes:
                            dve.wait_ge(m0_o, nth(l, q))
                            if q == 0:
                                dve.wait_ge(g_done, nth(l, G_M0))
                            else:
                                dve.wait_ge(m0_acc, nth(l, q - 1))
                            for e in (2 * q, 2 * q + 1):
                                for t in range(TILES):
                                    at = 256 * (e % 2) + D * t
                                    base = xn if e == 0 else y
                                    last = V.scalar_tensor_tensor(y[l][:, t, :], psB[l][:, at:at + D],
                                                                  gate[l][:, t, e:e + 1], base[l][:, t, :],
                                                                  ALU.mult, ALU.add)
                                if e % 2 == 0:
                                    last.then_inc(m0_half, 1)
                                    dve.wait_ge(m0_half, nth(l, q))
                            last.then_inc(m0_acc, 1)
                    for l in lanes:
                        dve.wait_ge(m0_b, nth(l))
                        dve.wait_ge(m0_acc, nth(l, E0 // 2 - 1))
                        V.tensor_tensor(y[l][:, :, :], rows(psA[l]), y[l][:, :, :], ALU.add).then_inc(y_new, 1)
                    norm(LN_IN0, y, y_new, Y_IN0)
                    for l in lanes:
                        dve.wait_ge(ln_affine, nth(l, 0))
                        V.tensor_tensor(h[l][:, :, :], aff[l][:, :, :], h[l][:, :, :], ALU.add).then_inc(h_new, 1)

                    norm(LN_A1, h, h_new, H_M0)
                    for l in lanes:
                        dve.wait_ge(a1_qk, nth(l))
                        V.tensor_copy(fm2[l][:, :], psB[l][0:64, :]).then_inc(a1_k, 1)
                    for l in lanes:
                        dve.wait_ge(a1_v, nth(l))
                        V.tensor_copy(v_sb[l][:, :, 0:D], rows(psA[l])).then_inc(a1_vs, 1)
                    block1 = cc("block")[:, None, :].broadcast_to([P, TILES, P])
                    for l in lanes:
                        dve.wait_ge(a1_s, nth(l))
                        for ps, dst in ((psA, big_a), (psB, big_b)):
                            V.tensor_tensor(dst[l][:, :].rearrange("p (t m) -> p t m", t=TILES),
                                            ps[l][:, :].rearrange("p (t m) -> p t m", t=TILES), block1,
                                            ALU.mult).then_inc(a1_m, 1)
                    for l in lanes:
                        for hh, src in enumerate((big_a, big_b)):
                            dve.wait_ge(a1_m, 2 * l + hh + 1)
                            V.tensor_reduce(s8[l][:, TILES * hh:TILES * (hh + 1), :],
                                            src[l][:, :].rearrange("p (t g j) -> p t j g", t=TILES, j=BS1),
                                            X, ALU.add).then_inc(a1_e8, 1)
                    for l in lanes:
                        dve.wait_ge(a1_e8, 2 * (l + 1))
                        V.tensor_reduce(s8s[l][:, 0, :], s8[l][:, :, :], X, ALU.max).then_inc(a1_step, 1)

                    def spread8(l, i):
                        return s8s[l][:, i, :][:, :, None].broadcast_to([P, H1 * TILES, BS1])
                    for l in lanes:
                        dve.wait_ge(a1_step, nth(l, 0))
                        V.tensor_tensor(s8b[l][:, :, :], s8[l][:, :, :], spread8(l, 0), ALU.subtract).then_inc(a1_step, 1)
                    for l in lanes:
                        dve.wait_ge(a1_exp, nth(l))
                        V.tensor_reduce(s8s[l][:, 1, :], s8b[l][:, :, :], X, ALU.add).then_inc(a1_step, 1)
                    for l in lanes:
                        dve.wait_ge(a1_step, nth(l, 2))
                        V.reciprocal(s8s[l][:, 2, :], s8s[l][:, 1, :]).then_inc(a1_step, 1)
                    for l in lanes:
                        dve.wait_ge(a1_step, nth(l, 3))
                        V.tensor_tensor(s8[l][:, :, :], s8b[l][:, :, :], spread8(l, 2), ALU.mult).then_inc(a1_step, 1)
                    add_psum(a1_o, lambda l: nth(l), H_A1)

                    norm(LN_M1, h, h_new, H_A1)
                    copy_logits(G_M1, E1)
                    first_of(E1, lg, 0, oh1)
                    for l in lanes:
                        dve.wait_ge(gstep, nth(l, gcount[0] - 1))
                        V.tensor_copy(gs[l][:, 7, 0:1], gs[l][:, 2, 0:1]).then_inc(g_done, 1)
                    for l in lanes:
                        dve.wait_ge(gT_ready, nth(l, G_M1))
                        V.tensor_scalar(gTb[l][:, :], gT[l][:, :], -1.0, BIG, ALU.add, ALU.mult).then_inc(gTb_ready, 1)
                    for m in range(1, MT, 2):
                        for l in lanes:
                            dve.wait_ge(m1_z, nth(l, m))
                            V.tensor_scalar(hid[l][:, m, :], psB[l][:, :], 0.0, None, ALU.max).then_inc(m1_o, 1)
                    for l in lanes:
                        dve.wait_ge(m1_z, nth(l, MT))
                        V.scalar_tensor_tensor(h[l][:, :, :], rows(psA[l]), 0.0, h[l][:, :, :], ALU.max,
                                               ALU.add).then_inc(h_new, 1)

                    norm(LN_A2, h, h_new, H_M1)
                    for l in lanes:
                        dve.wait_ge(a2_ke, nth(l))
                        kv = psA[l][:, :].rearrange("p (t c) -> p t c", t=TILES)
                        V.tensor_copy(v_sb[l][:, :, 0:D], kv[:, :, D:2 * D]).then_inc(a2_v, 1)
                        V.scalar_tensor_tensor(kf[l][:, 0, :, :], kf[l][:, 0, :, :], 1.0, kf[l][:, 1, :, :],
                                               ALU.min, ALU.add).then_inc(a2_kf, 1)
                        V.scalar_tensor_tensor(fm2[l][:, :], fm2[l][:, :], 1.0, big_a[l][0:64, :],
                                               ALU.min, ALU.add).then_inc(a2_qf, 1)
                    heads = cc("heads", 64)[:, None, :].broadcast_to([64, TILES, KV2])
                    for l in lanes:
                        dve.wait_ge(a2_s, nth(l))
                        V.tensor_tensor(kvm[l][:, :, :], psB[l][0:64, 0:TILES * KV2].rearrange("p (t c) -> p t c", c=KV2),
                                        heads, ALU.mult).then_inc(a2_sm, 1)
                    for l in lanes:
                        dve.wait_ge(a2_n, nth(l))
                        nd = psA[l][:, 0:TILES * KV2].rearrange("p (t c) -> p t c", c=KV2)
                        V.tensor_scalar(lg[l][:, :, 0:H2], nd[:, :, D:KV2], DEN_EPS, None, ALU.add).then_inc(a2_step, 1)
                    for l in lanes:
                        dve.wait_ge(a2_step, nth(l, 0))
                        V.reciprocal(lg[l][:, :, 8:8 + H2], lg[l][:, :, 0:H2]).then_inc(a2_step, 1)
                    for l in lanes:
                        dve.wait_ge(a2_step, nth(l, 1))
                        for t in range(TILES):
                            num = psA[l][:, KV2 * t:KV2 * t + D].rearrange("p (h m) -> p h m", m=D2)
                            z = lg[l][:, t, 8:8 + H2][:, :, None].broadcast_to([P, H2, D2])
                            last = V.tensor_tensor(y[l][:, t, :].rearrange("p (h m) -> p h m", m=D2), num, z, ALU.mult)
                        last.then_inc(a2_step, 1)
                    for l in lanes:
                        dve.wait_ge(a2_step, nth(l, 2))
                        V.tensor_tensor(y[l][:, :, :], y[l][:, :, :], xn[l][:, :, :], ALU.add).then_inc(y_new, 1)
                    norm(LN_IN2, y, y_new, Y_IN2)
                    for l in lanes:
                        dve.wait_ge(a2_y, nth(l))
                        V.tensor_tensor(y[l][:, :, :], rows(psA[l]), aff[l][:, :, :], ALU.add).then_inc(y_new, 1)
                    norm(LN_OUT2, y, y_new, Y_OUT2)
                    for l in lanes:
                        dve.wait_ge(ln_affine, nth(l, 2))
                        V.tensor_tensor(h[l][:, :, :], aff[l][:, :, :], h[l][:, :, :], ALU.add).then_inc(h_new, 1)

                    norm(LN_M2, h, h_new, H_A2)
                    top2(G_M2, E2)
                    for m in range(MT):
                        for l in lanes:
                            dve.wait_ge(m2_h, nth(l, m))
                            dve.wait_ge(m2_g, nth(l, m))
                            V.tensor_tensor(hid[l][:, m, :], psB[l][:, :], hid[l][:, m, :], ALU.mult).then_inc(m2_hg, 1)
                    for l in lanes:
                        dve.wait_ge(m2_o, nth(l))
                        dve.wait_ge(m2_res, nth(l))
                        V.tensor_tensor(h[l][:, :, :], rows(psA[l]), y[l][:, :, :], ALU.add).then_inc(h_new, 1)

                    norm(LN_A3, h, h_new, H_M2)
                    for l in lanes:
                        dve.wait_ge(a3_p, nth(l))
                        for ps, wave, dst in ((psA, cosines, big_a), (psB, sines, big_b)):
                            V.tensor_tensor(dst[l][:, :].rearrange("p (t s) -> p t s", t=TILES),
                                            ps[l][:, :].rearrange("p (t s) -> p t s", t=TILES),
                                            wave[:, None, :].broadcast_to([P, TILES, P]), ALU.mult).then_inc(a3_m, 1)
                    for l in lanes:
                        dve.wait_ge(a3_w, nth(l))
                        V.tensor_tensor_scan(hid[l][:, 0, :], decay3[:, :], big_c[l][:, :], 0.0,
                                             ALU.mult, ALU.add).then_inc(a3_z, 1)
                    add_psum(a3_y, lambda l: nth(l), H_A3)

                    norm(LN_M3, h, h_new, H_A3)
                    for l in lanes:
                        dve.wait_ge(m3_z, nth(l))
                        V.tensor_scalar(gTb[l][0:G3, :], psB[l][0:G3, :], GATE_MIN, None, ALU.is_gt).then_inc(m3_g, 1)
                    for p in range(PAIRS):
                        for l in lanes:
                            dve.wait_ge(m3_s, nth(l, p))
                            if p == 0:
                                dve.wait_ge(m3_sx, nth(l))
                            if p >= 2:
                                dve.wait_ge(m3_used, nth(l, p - 2))
                            V.tensor_tensor(pr[l][:, p % 2, :], sg[l][:, p % 2, :], sx[l][:, :], ALU.mult).then_inc(m3_p, 1)
                    for l in lanes:
                        dve.wait_ge(m3_used, nth(l, PAIRS - 1))
                        V.tensor_scalar(fm2[l][:, :], psB[l][0:64, :], c64("scale3"), None, ALU.mult).then_inc(m3_ys, 1)
                    for l in lanes:
                        dve.wait_ge(m3_t, nth(l))
                        V.tensor_tensor(h[l][:, :, :], rows(psA[l]), h[l][:, :, :], ALU.add).then_inc(h_new, 1)

            nc.sync.sem_clear(range(sems[sems_setup].num, sems[-1].num + 1))
            nc.all_engine_barrier()


def shape_constants():
    import numpy as np
    c = np.zeros((P, CC["_"][1]), np.float32)

    def put(name, a):
        s, e = CC[name]
        a = np.asarray(a, np.float32)
        c[0:a.shape[0], s:e] = a

    i = np.arange(P)
    put("ident", np.eye(P))
    gap = i[None, :] - i[:, None]
    put("decay", np.where(gap >= 0, np.exp(gap * np.log(np.float64(0.96875))), 0.0))
    put("block", i[:, None] // BS1 == i[None, :] // BS1)
    j = np.arange(D)
    head = np.arange(H2)
    put("heads", np.concatenate([j[:, None] // D2 == j[None, :] // D2, j[:, None] // D2 == head[None, :]], 1))
    for name, E in (("rank0", E0), ("rank1", E1), ("rank2", E2)):
        put(name, np.tile(E - np.arange(E), (P, 1)))
    put("time", np.tile(i, (P, 1)))
    put("later", np.tile(i > 0, (P, 1)))
    put("sign", np.where(i < D, 1.0, -1.0)[:, None])
    hid = np.arange(HID)
    put("sel2", np.arange(E2)[:, None] == hid[None, :] // F2)
    put("exp1", np.arange(E1)[:, None] == hid[None, :] // F1)
    put("pick3", np.arange(2 * D)[None, :] == D + i[:, None] // D)
    return c


def kernel(**inputs):
    import numpy as np
    import concourse.bacc as bacc
    from concourse.bass_utils import run_bass_kernel_spmd

    a = {k: np.asarray(v) for k, v in inputs.items()}

    def row(x):
        return x.reshape(1, -1)

    def with_bias(w, b):
        return np.concatenate([w, row(b)], 0)

    zero = np.zeros((1, D), np.float32)
    w65 = np.concatenate([
        with_bias(a["L0_ffn_gate_w"], a["L0_ffn_gate_b"]),
        with_bias(a["L0_ffn_w1"].transpose(1, 0, 2).reshape(D, E0 * F0), a["L0_ffn_b1"]),
        with_bias(a["L1_attn_Wv"].T, a["L1_attn_bv"]),
        with_bias(a["L1_ffn_router_w"].T, a["L1_ffn_router_b"]),
        with_bias(a["L1_ffn_W1"].transpose(1, 0, 2).reshape(D, HID), a["L1_ffn_b1"]),
        with_bias(a["L2_attn_W2"].T, a["L2_attn_b2"]),
        with_bias(a["L2_ffn_router_w"].T, np.zeros(E2, np.float32)),
        with_bias(a["L2_ffn_w1"].transpose(1, 0, 2).reshape(D, HID), a["L2_ffn_b1"]),
        np.concatenate([with_bias(a["L3_ffn_proj_w"].T, a["L3_ffn_proj_b"])] * SPLIT, 1),
    ], 1)
    qkv = a["L2_attn_Wqkv"]
    w64 = np.concatenate([
        a["L0_attn_Wq"], a["L0_attn_Wk"], a["L0_attn_Wv"].T,
        qkv[0:D].T, qkv[D:3 * D].T, a["L2_attn_W1"].T, a["L2_attn_b1"].reshape(D, 1),
        a["L3_attn_B_re"], a["L3_attn_B_im"], a["L3_attn_gamma_log"].reshape(D, 1),
        a["L3_attn_D"].reshape(D, 1), a["L3_ffn_scale"].reshape(D, 1),
    ], 1)
    c_re, c_im = a["L3_attn_C_re"].T, a["L3_attn_C_im"].T
    nu, theta = a["L3_attn_nu_log"].reshape(D, 1), a["L3_attn_theta_log"].reshape(D, 1)
    w3 = a["L3_ffn_weight"][0].transpose(0, 2, 1).reshape(P, 256)
    w128 = np.concatenate([
        a["L0_ffn_w2"].transpose(1, 0, 2).reshape(F0, E0 * D),
        a["L1_ffn_W2"].reshape(MT, P, D).transpose(1, 0, 2).reshape(P, MT * D),
        a["L2_ffn_w2"].reshape(MT, P, D).transpose(1, 0, 2).reshape(P, MT * D),
        np.concatenate([c_re, c_im], 0), np.concatenate([c_im, c_re], 0),
        np.concatenate([nu, nu], 0), np.concatenate([theta, theta], 0), w3,
    ], 1)

    def per_head(w, b):
        return np.concatenate([w.reshape(H1, D1, D), b.reshape(H1, D1, 1)], 2).transpose(1, 0, 2).reshape(D1, H1 * 65)

    def rows32(x):
        return np.concatenate([x, np.zeros((32 - x.shape[0], x.shape[1]), np.float32)], 0)

    w32 = np.concatenate([
        per_head(a["L1_attn_Wq"], a["L1_attn_bq"]), per_head(a["L1_attn_Wk"], a["L1_attn_bk"]),
        a["L1_attn_P"], rows32(a["L0_ffn_b2"]), a["L1_ffn_b2"], rows32(a["L2_ffn_b2"]),
    ], 1)
    wrow = np.concatenate([row(a[n]) for n in ("L0_ffn_gamma", "L0_ffn_beta", "L2_attn_ln1_g", "L2_attn_ln1_b",
                                               "L2_attn_ln2_g", "L2_attn_ln2_b")], 1)
    arrays = {
        "ids": np.ascontiguousarray(a["x"].T), "emb_w": np.ascontiguousarray(a["L0_tok_W"].T),
        "w65": w65, "w64": w64, "w128": w128, "w32": w32, "wrow": wrow, "consts": shape_constants(),
    }
    nc = bacc.Bacc("TRN2", target_bir_lowering=False, num_devices=1)
    aps = {n: nc.dram_tensor(n, list(v.shape), mybir.dt.from_np(v.dtype), kind="ExternalInput").ap()
           for n, v in arrays.items()}
    out = nc.dram_tensor("out", [NSEQ, P, D], mybir.dt.float32, kind="ExternalOutput").ap()
    tower(nc, aps["ids"], aps["emb_w"], aps["w65"], aps["w64"], aps["w128"], aps["w32"], aps["wrow"],
          aps["consts"], None, out.rearrange("(i l t) p d -> i l t p d", i=PASSES, l=LANES))
    r = run_bass_kernel_spmd(nc, [arrays], core_ids=[0])
    return r.results[0]["out"]
```

```python
import concourse.bass as bass
from concourse import mybir
from contextlib import ExitStack

P = 128
D = 64
LANES = 4
TILES = 4
NT = TILES * P
NSEQ = 32
PASSES = NSEQ // (LANES * TILES)

E0, F0 = 16, 128
E1, F1 = 32, 16
E2, F2 = 8, 64
E3 = 8
HID = 512
MT = HID // P
H1, D1, BS1 = 2, 32, 8
H2, D2 = 8, 8
KV2 = D + H2
PAIRS = D // 2
SPLIT = 3
G3 = SPLIT * E3
N_LN = 11
NT_USES = 9
BIG = 1.0e30
LN_EPS = 1e-5
DEN_EPS = 1e-6
GATE_MIN = 2.0 ** -24
LOG2E = 1.4426950408889634
MAGIC = 12582912.0
LN2_HI, LN2_LO = 0.693359375, -2.12194440e-4
PI = 3.141592653589793
TWO_PI_1 = 6.28125
TWO_PI_2 = 0.00193500518798828125
TWO_PI_3 = 2.0 * PI - TWO_PI_1 - TWO_PI_2
HALF_PI = PI / 2.0
QUANT = 6144.0

def columns(widths):
    at, out = 0, {}
    for name, width in widths:
        out[name] = (at, at + width)
        at += width
    out["_"] = (0, at)
    return out


C65 = columns([("gate0", E0), ("wv1", D), ("route1", E1), ("w2_2a", D), ("route2", E2), ("proj3", G3)])
CUP = columns([("w1_0", E0 * F0), ("w1_1", HID), ("w1_2", HID)])
N_UP = CUP["_"][1]
C64 = columns([("wq0", D), ("wk0", D), ("wv0", D), ("q2", D), ("kv2", 2 * D), ("w1_2a", D),
               ("b1_2a", 1), ("b_re", D), ("b_im", D), ("gamma3", 1), ("d3", 1)])
C128 = columns([("w2_0", E0 * D), ("w2_1", MT * D), ("w2_2", MT * D), ("c_a", D), ("c_b", D),
                ("nu", 1), ("theta", 1), ("w3", 256), ("b1_0", E0), ("b1_1", MT), ("b1_2", MT),
                ("scale3", 1)])
C32 = columns([("qb1", H1 * 65), ("kb1", H1 * 65), ("p1", D1), ("b2_0", D), ("b2_1", D), ("b2_2", D)])
CROW = columns([("g0", D), ("be0", D), ("g2a", D), ("be2a", D), ("g2b", D), ("be2b", D)])
CC = columns([("ident", P), ("decay", P), ("block", P), ("heads", KV2), ("rank0", E0),
              ("rank1", E1), ("rank2", E2), ("time", P), ("later", P), ("sign", 1)])
CB = columns([("sel2", MT * P), ("exp1", MT * P), ("pick3", 2 * D)])
XS_USES = 4


def nth(lane, use=0):
    return use * LANES + lane + 1


def tower(nc, ids, emb_w, w65, wup, w64, w128, w32, wrow, consts, binary, out):
    F32, BF16, I32, U32 = mybir.dt.float32, mybir.dt.bfloat16, mybir.dt.int32, mybir.dt.uint32
    F32R = mybir.dt.float32r
    ACT = mybir.ActivationFunctionType
    ALU = mybir.AluOpType
    X = mybir.AxisListType.X

    with ExitStack() as ctx:
        def sb(name, shape, dt=F32):
            return ctx.enter_context(nc.sbuf_tensor(name, shape, dt))

        def per_lane(name, shape, dt=F32):
            return [sb(f"{name}{l}", shape, dt) for l in range(LANES)]

        def sem(name):
            s = ctx.enter_context(nc.semaphore(name))
            sems.append(s)
            return s

        sems = []
        lanes = range(LANES)

        k65 = sb("k65", [65, C65["_"][1]])
        k64 = sb("k64", [64, C64["_"][1]])
        k128 = sb("k128", [P, C128["_"][1]])
        k32 = sb("k32", [32, C32["_"][1]])
        krow = sb("krow", [P, CROW["_"][1]])
        kc = sb("kc", [P, CC["_"][1]])

        def c65(name):
            a, b = C65[name]
            return k65[:, a:b]

        def c64(name):
            a, b = C64[name]
            return k64[:, a:b]

        def c128(name):
            a, b = C128[name]
            return k128[:, a:b]

        def c32(name, rows=32):
            a, b = C32[name]
            return k32[0:rows, a:b]

        def crow(name):
            a, b = CROW[name]
            return krow[:, None, a:b].broadcast_to([P, TILES, D])

        def cc(name, rows=P):
            a, b = CC[name]
            return kc[0:rows, a:b]

        def rank(E):
            return cc({E0: "rank0", E1: "rank1", E2: "rank2"}[E])[:, None, :].broadcast_to([P, TILES, E])

        ident = cc("ident")
        ids_sb = sb("ids_sb", [P, NSEQ], I32)
        ids_f = sb("ids_f", [P, NSEQ])
        keep = sb("keep", [P, NSEQ])
        emb = sb("emb", [P, NSEQ, D])

        score0 = sb("score0", [64, D])
        qp1 = sb("qp1", [65, D])
        kp1 = sb("kp1", [65, D])
        b_sc = sb("b_sc", [64, 2, D])
        b_f = sb("b_f", [P, 2, P])
        b_hi = sb("b_hi", [P, 2 * P], F32R)
        b_lo = sb("b_lo", [P, 2 * P], F32R)
        up_hi = sb("up_hi", [P, N_UP], F32R)
        up_lo = sb("up_lo", [P, N_UP], F32R)
        c_cos = sb("c_cos", [P, D])
        c_sin = sb("c_sin", [P, D])
        diag3 = sb("diag3", [64, D])
        cosines = sb("cosines", [P, P])
        sines = sb("sines", [P, P])
        decay3 = sb("decay3", [P, NT])
        w3_rows = sb("w3_rows", [P, PAIRS * P], BF16)
        kb = sb("kb", [P, CB["_"][1]], BF16)

        def cb(name, rows):
            a, b = CB[name]
            return kb[0:rows, a:b]

        sel1, sel2, pick3 = cb("exp1", E1), cb("sel2", SPLIT * E2), cb("pick3", P)
        neg_half = sb("neg_half", [P, TILES])
        ln_logs = sb("ln_logs", [P, 3])
        ex = sb("ex", [P, 6, 3])
        ex_i = sb("ex_i", [P, 3], I32)
        th = sb("th", [P, 8])

        h = per_lane("h", [P, TILES, D])
        xn = per_lane("xn", [P, TILES, D])
        y = per_lane("y", [P, TILES, D])
        aff = per_lane("aff", [P, TILES, D])
        sq = aff
        stat = per_lane("stat", [P, 4, TILES])
        xT = per_lane("xT", [65, NT])
        xs = per_lane("xs", [P, NT], F32R)
        fm = per_lane("fm", [65, NT])
        fm2 = per_lane("fm2", [P, NT])
        cen = [fm2[l][:, 0:TILES * D].rearrange("p (t d) -> p t d", t=TILES) for l in lanes]
        v_sb = per_lane("v_sb", [P, TILES, KV2])
        big_a = per_lane("big_a", [P, NT])
        big_b = per_lane("big_b", [P, NT])
        big_c = per_lane("big_c", [P, NT])
        hid = per_lane("hid", [P, MT, NT])
        lg, ge, gk, oh1, oh2 = (
            [big[l][:, P * i:P * (i + 1)].rearrange("p (t e) -> p t e", e=E1) for l in lanes]
            for big, i in ((big_a, 0), (big_a, 1), (big_a, 2), (big_a, 3), (big_b, 0)))
        kvm = per_lane("kvm", [64, TILES, KV2])
        gate = per_lane("gate", [P, TILES, E1])
        gs = per_lane("gs", [P, 8, TILES])
        gT = per_lane("gT", [E1, NT])
        gTb = per_lane("gTb", [P, NT], BF16)
        g3 = per_lane("g3", [P, TILES, SPLIT * E2])
        gh = per_lane("gh", [P, TILES, E2], BF16)
        s8 = per_lane("s8", [P, H1 * TILES, BS1])
        s8b = per_lane("s8b", [P, H1 * TILES, BS1])
        s8s = per_lane("s8s", [P, 4, H1 * TILES])
        kf = [hid[l][:, 3, :].rearrange("p (b t d) -> p b t d", b=2, t=TILES) for l in lanes]
        sg = [hid[l][:, 0, :].bitcast(BF16).rearrange("p (b n) -> p b n", b=2) for l in lanes]
        pr = [hid[l][:, 1, :].bitcast(BF16).rearrange("p (b n) -> p b n", b=2) for l in lanes]
        sx = [hid[l][:, 2, :].bitcast(BF16)[:, 0:NT] for l in lanes]

        ph = hid[0][:, 0:2, :].rearrange("p a (b s) -> p (a b) s", s=P)
        w3_hi, w3_mid, w3_lo = (hid[0][:, 2, 128 * i:128 * (i + 1)].bitcast(BF16) for i in range(3))
        w3_r1, w3_r2 = (hid[0][:, 3, 256 * i:256 * (i + 1)] for i in range(2))
        up_raw = [hid[2][:, :, :].rearrange("p a n -> p (a n)"),
                  hid[3][:, 0:2, :].rearrange("p a n -> p (a n)")]
        up_cut = (0, 4 * NT, N_UP)
        kb_raw = hid[1][:, :, :].rearrange("p a n -> p (a n)")[:, 0:CB["_"][1]]

        psA = [ctx.enter_context(nc.psum_tensor(f"psA{l}", [P, NT], F32)) for l in lanes]
        psB = [ctx.enter_context(nc.psum_tensor(f"psB{l}", [P, NT], F32)) for l in lanes]

        w3_bounce = nc.dram_tensor("w3_bounce", [SPLIT, E3, PAIRS * P], BF16).ap()

        ids_in = sem("ids_in")
        weights_in = sem("weights_in")
        gathered = sem("gathered")
        ids_ready = sem("ids_ready")
        v_chain = sem("v_chain")
        folded = sem("folded")
        unfolded = sem("unfolded")
        angles = sem("angles")
        waves = sem("waves")
        halves = sem("halves")
        w3_split = sem("w3_split")
        w3_out = sem("w3_out")
        w3_in = sem("w3_in")
        b_scaled = sem("b_scaled")
        up_in = sem("up_in")
        up_rounded = sem("up_rounded")
        b_rounded = sem("b_rounded")
        N_WEIGHTS = 7

        with nc.Block() as block:
            @block.sync
            def _(sp):
                sp.dma_start(ids_sb[:, :], ids).then_inc(ids_in, 16)
                sp.dma_start(k64[:, :], w64).then_inc(weights_in, 16)
                sp.dma_start(kc[:, :], consts).then_inc(weights_in, 16)
                sp.dma_start(kb_raw, binary).then_inc(weights_in, 16)
                sp.dma_start(k65[:, :], w65).then_inc(weights_in, 16)
                for i in range(2):
                    for half in (slice(0, D), slice(D, P)):
                        sp.dma_start(up_raw[i][half, :], wup[:, up_cut[i]:up_cut[i + 1]]).then_inc(up_in, 16)
                sp.wait_ge(w3_split, 3)
                for s, part in enumerate((w3_hi, w3_mid, w3_lo)):
                    sp.dma_start(w3_bounce[s].rearrange("e (c x) -> (e c) x", x=256),
                                 part[:, :]).then_inc(w3_out, 16)
                sp.wait_ge(w3_out, 16 * SPLIT)
                for l in lanes:
                    sp.dma_start(w3_rows[32 * l:32 * l + G3, :],
                                 w3_bounce.rearrange("s e x -> (s e) x")).then_inc(w3_in, 16)
                sp.wait_ge(w3_in, 16 * LANES)

            @block.gpsimd
            def _(pool):
                pool.wait_ge(ids_in, 16)
                for s in range(NSEQ):
                    pool.indirect_dma_start(
                        emb[:, s, :], None, emb_w,
                        bass.IndirectOffsetOnAxis(ap=ids_sb[:, s:s + 1].bitcast(U32), axis=0)
                    ).then_inc(gathered, 16)
                pool.wait_ge(gathered, 16 * NSEQ)

            @block.tensor
            def _(pe):
                pe.wait_ge(weights_in, 16 * N_WEIGHTS)
                pe.matmul(psA[0][0:64, 0:D], c64("wq0"), c64("wk0"), start=True, stop=True)
                qb = c32("qb1").rearrange("e (h i) -> e h i", h=H1)
                kw = c32("kb1").rearrange("e (h i) -> e h i", h=H1)
                for hh in range(H1):
                    pe.matmul(psA[1][0:65, D1 * hh:D1 * (hh + 1)], qb[:, hh, :], c32("p1"),
                              start=True, stop=True)
                for hh in range(H1):
                    pe.matmul(psA[2][0:65, D1 * hh:D1 * (hh + 1)], kw[:, hh, :], c32("p1"),
                              start=True, stop=True).then_inc(folded, 1)
                pe.wait_ge(b_scaled, 2)
                pe.transpose(psA[3][0:64, 0:64], b_sc[:, 0, :], cc("ident", 64)[:, 0:64])
                pe.transpose(psA[3][0:64, 64:128], b_sc[:, 1, :], cc("ident", 64)[:, 0:64]).then_inc(folded, 1)

            @block.scalar
            def _(act):
                act.dma_start(k128[:, :], w128).then_inc(weights_in, 16)
                act.dma_start(k32[:, :], w32).then_inc(weights_in, 16)
                act.dma_start(krow[:, :], wrow.broadcast_to([P, CROW["_"][1]])).then_inc(weights_in, 16)
                act.wait_ge(weights_in, 16 * N_WEIGHTS)
                act.activation(kb[:, :], kb_raw, ACT.Copy)
                act.wait_ge(folded, 2)
                act.activation(score0[:, :], psA[0][0:64, 0:D], ACT.Copy)
                act.activation(qp1[:, :], psA[1][0:65, 0:D], ACT.Copy, scale=float(D1) ** -0.5)
                act.activation(kp1[:, :], psA[2][0:65, 0:D], ACT.Copy)
                act.wait_ge(up_in, 64)
                for i in range(2):
                    act.activation(up_hi[:, up_cut[i]:up_cut[i + 1]], up_raw[i], ACT.Copy).then_inc(up_rounded, 1)
                act.wait_ge(angles, 2)
                act.activation(sines[:, :], ph[:, 5, :], ACT.Sin)
                act.activation(cosines[:, :], ph[:, 7, :], ACT.Sin)

            @block.vector
            def _(dve):
                count = [0]

                def then(ins):
                    count[0] += 1
                    ins.then_inc(v_chain, 1)
                    dve.wait_ge(v_chain, count[0])

                V = nc.vector
                V.memset(neg_half[:, :], -0.5)
                for l in lanes:
                    V.memset(xT[l][64:65, :], 1.0)
                    V.memset(fm[l][64:65, :], 1.0)
                    V.memset(v_sb[l][:, :, D:KV2], 1.0)
                dve.wait_ge(ids_in, 16)
                then(V.tensor_copy(ids_f[:, :], ids_sb[:, :]))
                V.tensor_scalar(keep[:, :], ids_f[:, :], 0.0, None, ALU.not_equal)
                dve.wait_ge(weights_in, 16 * N_WEIGHTS)

                w3 = c128("w3")
                then(V.tensor_copy(w3_hi[:, :], w3))
                then(V.tensor_tensor(w3_r1[:, :], w3, w3_hi[:, :], ALU.subtract))
                then(V.tensor_copy(w3_mid[:, :], w3_r1[:, :]))
                then(V.tensor_tensor(w3_r2[:, :], w3_r1[:, :], w3_mid[:, :], ALU.subtract))
                V.tensor_copy(w3_lo[:, :], w3_r2[:, :]).then_inc(w3_split, 3)

                def exponential(dst, src, n):
                    x, r, k, p = (ex[:, i, 0:n] for i in range(4))
                    then(V.tensor_scalar(x, src, -87.0, 88.0, ALU.max, ALU.min))
                    then(V.tensor_scalar(k, x, LOG2E, MAGIC, ALU.mult, ALU.add))
                    then(V.tensor_scalar(k, k, MAGIC, None, ALU.subtract))
                    then(V.scalar_tensor_tensor(r, k, -LN2_HI, x, ALU.mult, ALU.add))
                    then(V.scalar_tensor_tensor(r, k, -LN2_LO, r, ALU.mult, ALU.add))
                    then(V.tensor_scalar(p, r, 1.0 / 5040.0, 1.0 / 720.0, ALU.mult, ALU.add))
                    for c in (1.0 / 120.0, 1.0 / 24.0, 1.0 / 6.0, 0.5, 1.0, 1.0):
                        then(V.tensor_tensor(p, p, r, ALU.mult))
                        then(V.tensor_scalar(p, p, c, None, ALU.add))
                    then(V.tensor_scalar(ex_i[:, 0:n], k, 127.0, None, ALU.add))
                    then(V.tensor_scalar(ex_i[:, 0:n], ex_i[:, 0:n], 23, None, ALU.logical_shift_left))
                    then(V.tensor_tensor(dst, p, ex_i[:, 0:n].bitcast(F32), ALU.mult))

                V.tensor_copy(ln_logs[:, 0:2], k128[:, C128["nu"][0]:C128["theta"][1]])
                V.memset(ln_logs[64:128, 2:3], 0.0)
                then(V.tensor_copy(ln_logs[0:64, 2:3], c64("gamma3")))
                exponential(ex[:, 4, :], ln_logs[:, :], 3)
                for part, name in enumerate(("b_re", "b_im")):
                    V.tensor_scalar(b_sc[:, part, :], c64(name), ex[0:64, 4, 2:3], None,
                                    ALU.mult).then_inc(b_scaled, 1)
                then(V.tensor_scalar(th[:, 0:1], ex[:, 4, 0:1], -1.0, None, ALU.mult))
                then(V.tensor_copy(th[:, 1:2], ex[:, 4, 1:2]))
                exponential(th[:, 2:3], th[:, 0:1], 1)
                later = cc("later")[:, None, :].broadcast_to([P, TILES, P])
                V.tensor_scalar(decay3[:, :].rearrange("p (t s) -> p t s", t=TILES), later,
                                th[:, 2:3], None, ALU.mult)
                then(V.tensor_scalar(th[:, 3:4], th[:, 1:2], 0.5 / PI, MAGIC, ALU.mult, ALU.add))
                then(V.tensor_scalar(th[:, 3:4], th[:, 3:4], MAGIC, None, ALU.subtract))
                for c in (TWO_PI_1, TWO_PI_2, TWO_PI_3):
                    then(V.scalar_tensor_tensor(th[:, 1:2], th[:, 3:4], -c, th[:, 1:2], ALU.mult, ALU.add))
                then(V.tensor_scalar(th[:, 4:5], th[:, 1:2], QUANT, None, ALU.add))
                then(V.tensor_scalar(th[:, 4:5], th[:, 4:5], QUANT, None, ALU.subtract))
                then(V.tensor_tensor(th[:, 5:6], th[:, 1:2], th[:, 4:5], ALU.subtract))
                then(V.tensor_scalar(ph[:, 0, :], cc("time"), th[:, 4:5], None, ALU.mult))
                then(V.tensor_scalar(ph[:, 1, :], ph[:, 0, :], 0.5 / PI, MAGIC, ALU.mult, ALU.add))
                then(V.tensor_scalar(ph[:, 1, :], ph[:, 1, :], MAGIC, None, ALU.subtract))
                then(V.tensor_scalar(ph[:, 2, :], cc("time"), th[:, 5:6], None, ALU.mult))
                for c in (TWO_PI_1, TWO_PI_2, TWO_PI_3):
                    then(V.scalar_tensor_tensor(ph[:, 0, :], ph[:, 1, :], -c, ph[:, 0, :], ALU.mult, ALU.add))
                then(V.tensor_tensor(ph[:, 3, :], ph[:, 0, :], ph[:, 2, :], ALU.add))
                V.tensor_scalar(ph[:, 5, :], ph[:, 3, :], -3.1415925, 3.1415925, ALU.max, ALU.min).then_inc(angles, 1)
                then(V.tensor_scalar(ph[:, 6, :], ph[:, 3, :], HALF_PI, None, ALU.add))
                then(V.tensor_scalar(ph[:, 4, :], ph[:, 6, :], PI, -2.0 * PI, ALU.is_gt, ALU.mult))
                then(V.tensor_tensor(ph[:, 6, :], ph[:, 6, :], ph[:, 4, :], ALU.add))
                V.tensor_scalar(ph[:, 7, :], ph[:, 6, :], -3.1415925, 3.1415925, ALU.max, ALU.min).then_inc(angles, 1)
                V.tensor_scalar(c_cos[:, :], c128("c_a"), cc("sign"), None, ALU.mult)
                V.tensor_scalar(c_sin[:, :], c128("c_b"), -1.0, None, ALU.mult)
                V.tensor_scalar(diag3[:, :], cc("ident", 64)[:, 0:64], c64("d3"), None, ALU.mult)
                for i in range(2):
                    dve.wait_ge(up_rounded, i + 1)
                    cut = slice(up_cut[i], up_cut[i + 1])
                    V.tensor_tensor(up_lo[:, cut], up_raw[i], up_hi[:, cut].bitcast(F32), ALU.subtract)
                dve.wait_ge(folded, 3)
                for half in (slice(0, D), slice(D, P)):
                    V.tensor_copy(b_f[half, 0, :], psA[3][0:64, 0:P])
                    V.tensor_copy(b_f[half, 1, 0:D], psA[3][0:64, D:P])
                    V.tensor_scalar(b_f[half, 1, D:P], psA[3][0:64, 0:D], -1.0, None, ALU.mult).then_inc(b_rounded, 1)
                dve.wait_ge(b_rounded, 2)
                bf = b_f[:, :, :].rearrange("p a n -> p (a n)")
                V.tensor_copy(b_hi[:, :], bf).then_inc(b_rounded, 1)
                dve.wait_ge(b_rounded, 3)
                V.tensor_tensor(b_lo[:, :], bf, b_hi[:, :].bitcast(F32), ALU.subtract)

        first = sems[0].num
        nc.sync.sem_clear(range(first, sems[-1].num + 1))
        nc.all_engine_barrier()

        sems_setup = len(sems)
        h_new = sem("h_new")
        y_new = sem("y_new")
        y_part = sem("y_part")
        ln_sum = sem("ln_sum")
        ln_cen = sem("ln_cen")
        ln_sq = sem("ln_sq")
        ln_var = sem("ln_var")
        ln_vare = sem("ln_vare")
        ln_rstd = sem("ln_rstd")
        ln_out = sem("ln_out")
        ln_scaled = sem("ln_scaled")
        ln_affine = sem("ln_affine")
        x_turned = sem("x_turned")
        x_ready = sem("x_ready")
        xs_hi = sem("xs_hi")
        xs_ready = sem("xs_ready")
        logits = sem("logits")
        gstep = sem("gstep")
        g_sum = sem("g_sum")
        gsplit = sem("gsplit")
        g_exp = sem("g_exp")
        g_done = sem("g_done")
        g_turned = sem("g_turned")
        gT_ready = sem("gT_ready")
        gTb_ready = sem("gTb_ready")
        a0_rv = sem("a0_rv")
        a0_r = sem("a0_r")
        a0_v = sem("a0_v")
        a0_s = sem("a0_s")
        a0_p = sem("a0_p")
        a0_o = sem("a0_o")
        m0_z = sem("m0_z")
        m0_h = sem("m0_h")
        m0_o = sem("m0_o")
        m0_prod = sem("m0_prod")
        m0_acc = sem("m0_acc")
        m0_b = sem("m0_b")
        a1_qk = sem("a1_qk")
        a1_q = sem("a1_q")
        a1_k = sem("a1_k")
        a1_v = sem("a1_v")
        a1_vs = sem("a1_vs")
        a1_s = sem("a1_s")
        a1_m = sem("a1_m")
        a1_e8 = sem("a1_e8")
        a1_step = sem("a1_step")
        a1_exp = sem("a1_exp")
        a1_full = sem("a1_full")
        a1_turned = sem("a1_turned")
        a1_aT = sem("a1_aT")
        a1_o = sem("a1_o")
        m1_z = sem("m1_z")
        m1_h = sem("m1_h")
        m1_o = sem("m1_o")
        a2_q = sem("a2_q")
        a2_kv = sem("a2_kv")
        a2_qe = sem("a2_qe")
        a2_ke = sem("a2_ke")
        a2_qf = sem("a2_qf")
        a2_kf = sem("a2_kf")
        a2_v = sem("a2_v")
        a2_s = sem("a2_s")
        a2_sm = sem("a2_sm")
        a2_n = sem("a2_n")
        a2_step = sem("a2_step")
        a2_z = sem("a2_z")
        a2_g = sem("a2_g")
        a2_y = sem("a2_y")
        m2_z = sem("m2_z")
        m2_h = sem("m2_h")
        m2_g = sem("m2_g")
        m2_hg = sem("m2_hg")
        m2_o = sem("m2_o")
        m2_res = sem("m2_res")
        a3_p = sem("a3_p")
        a3_m = sem("a3_m")
        a3_w = sem("a3_w")
        a3_z = sem("a3_z")
        a3_c = sem("a3_c")
        a3_y = sem("a3_y")
        m3_sx = sem("m3_sx")
        m3_z = sem("m3_z")
        m3_g = sem("m3_g")
        m3_w = sem("m3_w")
        m3_s = sem("m3_s")
        m3_p = sem("m3_p")
        m3_used = sem("m3_used")
        m3_ys = sem("m3_ys")
        m3_t = sem("m3_t")
        stored = sem("stored")

        (LN_A0, LN_M0, LN_IN0, LN_A1, LN_M1, LN_A2, LN_IN2, LN_OUT2, LN_M2, LN_A3, LN_M3) = range(N_LN)
        (H_EMB, H_A0, H_M0, H_A1, H_M1, H_A2, H_M2, H_A3, H_OUT) = range(9)
        (X_A0, X_M0, X_A1, X_M1, X_A2, X_IN2, X_M2, X_A3, X_M3) = range(NT_USES)
        XS_M0, XS_M1, XS_M2, XS_A3 = range(XS_USES)
        G_M0, G_M1, G_M2 = range(3)
        Y_IN0, Y_IN2, Y_OUT2 = range(3)
        TOP2_DIFF, TOP2_STEPS, TOP1_STEPS = 12, 18, 6

        def rows(ap):
            return ap[:, 0:TILES * D].rearrange("p (t d) -> p t d", t=TILES)

        def half3(l):
            return slice(D * (l % 2), D * (l % 2) + D)

        def prod(l, q):
            return (big_a, big_b)[q % 2][l][:, :]

        def spread(stat_ap, n):
            return stat_ap[:, :, None].broadcast_to([P, TILES, n])

        with nc.Fori(0, PASSES) as it:
            with nc.Block() as block:

                @block.sync
                def _(sp):
                    for l in lanes:
                        sp.wait_ge(h_new, nth(l, H_OUT))
                        sp.dma_start(out[it, l].rearrange("t p d -> p t d"), h[l][:, :, :]).then_inc(stored, 16)
                    sp.wait_ge(stored, 16 * LANES)

                @block.gpsimd
                def _(pool):
                    G = nc.gpsimd

                    def rstd(use):
                        for l in lanes:
                            pool.wait_ge(ln_var, nth(l, use))
                            G.tensor_scalar(stat[l][:, 2, :], stat[l][:, 1, :], 1.0 / D, LN_EPS,
                                            ALU.mult, ALU.add).then_inc(ln_vare, 1)
                        for l in lanes:
                            pool.wait_ge(ln_vare, nth(l, use))
                            G.tensor_tensor(stat[l][:, 3, :], stat[l][:, 2, :], neg_half[:, :],
                                            ALU.pow).then_inc(ln_rstd, 1)

                    def affine(ln, use, gamma, beta):
                        for l in lanes:
                            pool.wait_ge(ln_out, nth(l, ln))
                            G.tensor_tensor(aff[l][:, :, :], xn[l][:, :, :], crow(gamma), ALU.mult).then_inc(ln_scaled, 1)
                        for l in lanes:
                            pool.wait_ge(ln_scaled, nth(l, use))
                            G.tensor_tensor(aff[l][:, :, :], aff[l][:, :, :], crow(beta), ALU.add).then_inc(ln_affine, 1)

                    rstd(LN_A0)
                    rstd(LN_M0)
                    for q in range(E0 // 2):
                        for l in lanes:
                            pool.wait_ge(m0_prod, nth(l, q))
                            if q:
                                pool.wait_ge(m0_acc, nth(l, q - 1))
                                G.tensor_tensor(big_c[l][:, :], prod(l, q), big_c[l][:, :], ALU.add).then_inc(m0_acc, 1)
                            else:
                                G.tensor_copy(big_c[l][:, :], prod(l, q)).then_inc(m0_acc, 1)
                    rstd(LN_IN0)
                    affine(LN_IN0, 0, "g0", "be0")
                    rstd(LN_A1)
                    block1 = cc("block").rearrange("p (g j) -> p g j", j=BS1)[:, None, :, :].broadcast_to(
                        [P, TILES, P // BS1, BS1])
                    for l in lanes:
                        pool.wait_ge(a1_step, nth(l, 4))
                        for hh, dst in enumerate((big_a, big_b)):
                            w = s8[l][:, TILES * hh:TILES * (hh + 1), None, :].broadcast_to([P, TILES, P // BS1, BS1])
                            G.tensor_tensor(dst[l][:, :].rearrange("p (t g j) -> p t g j", t=TILES, j=BS1),
                                            w, block1, ALU.mult).then_inc(a1_full, 1)
                    rstd(LN_M1)
                    rstd(LN_A2)
                    rstd(LN_IN2)
                    affine(LN_IN2, 1, "g2a", "be2a")
                    rstd(LN_OUT2)
                    affine(LN_OUT2, 2, "g2b", "be2b")
                    rstd(LN_M2)
                    for l in lanes:
                        pool.wait_ge(ln_out, nth(l, LN_M2))
                        G.tensor_tensor(y[l][:, :, :], h[l][:, :, :], xn[l][:, :, :], ALU.add).then_inc(m2_res, 1)
                    rstd(LN_A3)
                    for l in lanes:
                        pool.wait_ge(a3_m, 2 * (l + 1))
                        G.tensor_tensor(big_c[l][:, :], big_a[l][:, :], big_b[l][:, :], ALU.add).then_inc(a3_w, 1)
                    for l in lanes:
                        pool.wait_ge(a3_z, nth(l))
                        for wave, dst in ((cosines, big_a), (sines, big_b)):
                            G.tensor_tensor(dst[l][:, :].rearrange("p (t s) -> p t s", t=TILES),
                                            hid[l][:, 0, :].rearrange("p (t s) -> p t s", t=TILES),
                                            wave[:, None, :].broadcast_to([P, TILES, P]), ALU.mult).then_inc(a3_c, 1)
                    rstd(LN_M3)

                @block.scalar
                def _(act):
                    def squares(use):
                        for l in lanes:
                            act.wait_ge(ln_cen, nth(l, use))
                            act.activation(sq[l][:, :, :], cen[l][:, :, :], ACT.Square).then_inc(ln_sq, 1)

                    def turned(use):
                        for l in lanes:
                            act.wait_ge(x_turned, nth(l, use))
                            act.activation(xT[l][0:64, :], psA[l][0:64, :], ACT.Copy).then_inc(x_ready, 1)

                    def turned_parts(use):
                        for l in lanes:
                            act.wait_ge(x_turned, nth(l, use))
                            act.activation(xs[l][0:64, :], psA[l][0:64, :], ACT.Copy).then_inc(xs_hi, 1)
                            act.activation(xT[l][0:64, :], psA[l][0:64, :], ACT.Copy).then_inc(x_ready, 1)

                    def gate_exp(use):
                        for l in lanes:
                            act.wait_ge(gstep, nth(l, use * (TOP2_STEPS + TOP1_STEPS) + TOP2_DIFF))
                            act.activation(gs[l][:, 4, :], gs[l][:, 3, :], ACT.Exp).then_inc(g_exp, 1)

                    def gates_turned(use, E):
                        for l in lanes:
                            act.wait_ge(g_turned, nth(l, use))
                            act.activation(gT[l][0:E, :], psA[l][0:E, :], ACT.Copy).then_inc(gT_ready, 1)

                    squares(LN_A0)
                    turned(X_A0)
                    for l in lanes:
                        act.wait_ge(a0_rv, nth(l))
                        act.activation(fm[l][0:64, :], psB[l][0:64, :], ACT.Copy).then_inc(a0_r, 1)
                    squares(LN_M0)
                    turned_parts(X_M0)
                    gate_exp(0)
                    gates_turned(G_M0, E0)
                    for e in range(E0):
                        for l in lanes:
                            act.wait_ge(m0_z, nth(l, e))
                            if e >= 4:
                                act.wait_ge(m0_o, nth(l, e // 2 - 2))
                            act.activation(hid[l][:, e % 4, :], psA[l][:, :], ACT.Relu,
                                           bias=c128("b1_0")[:, e:e + 1]).then_inc(m0_h, 1)
                    squares(LN_IN0)
                    squares(LN_A1)
                    turned(X_A1)
                    for l in lanes:
                        act.wait_ge(a1_qk, nth(l))
                        act.activation(fm[l][0:64, :], psA[l][0:64, :], ACT.Copy).then_inc(a1_q, 1)
                    for l in lanes:
                        act.wait_ge(a1_step, nth(l, 1))
                        act.activation(s8b[l][:, :, :], s8b[l][:, :, :], ACT.Exp).then_inc(a1_exp, 1)
                    for l in lanes:
                        act.wait_ge(a1_turned, nth(l))
                        act.activation(hid[l][:, 0, :], psA[l][:, :], ACT.Copy)
                        act.activation(hid[l][:, 1, :], psB[l][:, :], ACT.Copy).then_inc(a1_aT, 1)
                    squares(LN_M1)
                    turned_parts(X_M1)
                    gates_turned(G_M1, E1)
                    for m in range(0, MT, 2):
                        for l in lanes:
                            act.wait_ge(m1_z, nth(l, m))
                            act.activation(hid[l][:, m, :], psA[l][:, :], ACT.Relu,
                                           bias=c128("b1_1")[:, m:m + 1]).then_inc(m1_h, 1)
                    squares(LN_A2)
                    turned(X_A2)
                    for l in lanes:
                        act.wait_ge(a2_q, nth(l))
                        act.activation(fm2[l][0:64, :], psB[l][0:64, :], ACT.Exp)
                        act.activation(big_a[l][0:64, :], psB[l][0:64, :], ACT.Relu).then_inc(a2_qe, 1)
                        act.wait_ge(a2_kv, nth(l))
                        kv = psA[l][:, :].rearrange("p (t c) -> p t c", t=TILES)
                        act.activation(kf[l][:, 0, :, :], kv[:, :, 0:D], ACT.Exp)
                        act.activation(kf[l][:, 1, :, :], kv[:, :, 0:D], ACT.Relu).then_inc(a2_ke, 1)
                    squares(LN_IN2)
                    turned(X_IN2)
                    for l in lanes:
                        act.wait_ge(a2_z, nth(l))
                        act.activation(fm[l][0:64, :], psB[l][0:64, :], ACT.Gelu, bias=c64("b1_2a")).then_inc(a2_g, 1)
                    squares(LN_OUT2)
                    squares(LN_M2)
                    turned_parts(X_M2)
                    gate_exp(1)
                    for l in lanes:
                        act.wait_ge(g_turned, nth(l, G_M2))
                        act.activation(gT[l][0:E2, :], psA[l][0:E2, :], ACT.Copy)
                        act.activation(gTb[l][0:SPLIT * E2, :], psA[l][0:SPLIT * E2, :], ACT.Copy).then_inc(gT_ready, 1)
                    for m in range(MT):
                        for l in lanes:
                            act.wait_ge(m2_z, nth(l, m))
                            act.activation(hid[l][:, m, :], psA[l][:, :], ACT.Gelu,
                                           bias=c128("b1_2")[:, m:m + 1]).then_inc(m2_h, 1)
                    squares(LN_A3)
                    turned_parts(X_A3)
                    squares(LN_M3)
                    for l in lanes:
                        act.wait_ge(x_turned, nth(l, X_M3))
                        act.activation(xT[l][0:64, :], psA[l][0:64, :], ACT.Copy).then_inc(x_ready, 1)
                        act.activation(sx[l][0:64, :], psA[l][0:64, :], ACT.Sign)
                        act.activation(sx[l][64:128, :], psA[l][0:64, :], ACT.Sign).then_inc(m3_sx, 1)
                    for p in range(PAIRS):
                        for l in lanes:
                            act.wait_ge(m3_w, nth(l, p))
                            if p >= 2:
                                act.wait_ge(m3_p, nth(l, p - 2))
                            act.activation(sg[l][:, p % 2, :], psA[l][:, :], ACT.Sign).then_inc(m3_s, 1)

                @block.tensor
                def _(pe):
                    def turn(ln, use, src, ready):
                        for l in lanes:
                            pe.wait_ge(ready, ln(l))
                            for t in range(TILES):
                                last = pe.transpose(psA[l][0:64, P * t:P * (t + 1)], src[l][:, t, :], ident)
                            last.then_inc(x_turned, 1)

                    def tile(ap, t):
                        return ap[:, P * t:P * (t + 1)]

                    def up(out, name, col, l):
                        a = CUP[name][0] + P * col
                        pe.matmul(out, up_hi[:, a:a + P], xs[l][:, :], start=True, stop=False)
                        return pe.matmul(out, up_lo[:, a:a + P], xs[l][:, :], start=False, stop=(name != "w1_1"))

                    def route(use, x_use, name, E):
                        for l in lanes:
                            pe.wait_ge(x_ready, nth(l, x_use))
                            for t in range(TILES):
                                last = pe.matmul(psB[l][:, E * t:E * (t + 1)], tile(xT[l], t), c65(name),
                                                 start=True, stop=True)
                            last.then_inc(logits, 1)

                    def turn_gates(use, src, E):
                        for l in lanes:
                            pe.wait_ge(g_done, nth(l, use))
                            for t in range(TILES):
                                last = pe.transpose(psA[l][0:E, P * t:P * (t + 1)], src[l][:, t, 0:E], ident)
                            last.then_inc(g_turned, 1)

                    turn(lambda l: nth(l, LN_A0), X_A0, xn, ln_out)
                    for l in lanes:
                        pe.wait_ge(x_ready, nth(l, X_A0))
                        pe.matmul(psB[l][0:64, :], score0[:, :], xT[l][0:64, :], start=True, stop=True)
                        for t in range(TILES):
                            last = pe.matmul(psA[l][:, D * t:D * (t + 1)], tile(xT[l][0:64, :], t), c64("wv0"),
                                             start=True, stop=True)
                        last.then_inc(a0_rv, 1)
                    for l in lanes:
                        pe.wait_ge(a0_r, nth(l))
                        for t in range(TILES):
                            last = pe.matmul(tile(psB[l], t), tile(xT[l][0:64, :], t), tile(fm[l][0:64, :], t),
                                             start=True, stop=True)
                        last.then_inc(a0_s, 1)
                    for l in lanes:
                        pe.wait_ge(a0_v, nth(l))
                        pe.wait_ge(a0_p, nth(l))
                        for t in range(TILES):
                            last = pe.matmul(psA[l][:, D * t:D * (t + 1)], tile(big_a[l], t), v_sb[l][:, t, 0:D],
                                             start=True, stop=True)
                        last.then_inc(a0_o, 1)

                    turn(lambda l: nth(l, LN_M0), X_M0, xn, ln_out)
                    route(G_M0, X_M0, "gate0", E0)
                    turn_gates(G_M0, gate, E0)

                    def up0(e):
                        for l in lanes:
                            if e == 0:
                                pe.wait_ge(gT_ready, nth(l, G_M0))
                            else:
                                pe.wait_ge(m0_h, nth(l, e - 1))
                            up(psA[l][:, :], "w1_0", e, l).then_inc(m0_z, 1)

                    def down0(q):
                        for l in lanes:
                            pe.wait_ge(m0_h, nth(l, 2 * q + 1))
                            if q:
                                pe.wait_ge(m0_prod, nth(l, q - 1))
                            for e in (2 * q, 2 * q + 1):
                                a = C128["w2_0"][0] + D * e
                                for t in range(TILES):
                                    at = 256 * (e % 2) + D * t
                                    last = pe.matmul(psB[l][:, at:at + D], tile(hid[l][:, e % 4, :], t),
                                                     k128[:, a:a + D], start=True, stop=True)
                            last.then_inc(m0_o, 1)

                    up0(0)
                    up0(1)
                    for q in range(E0 // 2):
                        for e in (2 * q + 2, 2 * q + 3):
                            if e < E0:
                                up0(e)
                        down0(q)
                    for l in lanes:
                        for t in range(TILES):
                            last = pe.matmul(psA[l][:, D * t:D * (t + 1)], tile(gT[l][0:E0, :], t),
                                             c32("b2_0", E0), start=True, stop=True)
                        last.then_inc(m0_b, 1)

                    turn(lambda l: nth(l, LN_A1), X_A1, xn, ln_out)
                    for l in lanes:
                        pe.wait_ge(x_ready, nth(l, X_A1))
                        pe.matmul(psA[l][0:64, :], qp1[:, :], xT[l][:, :], start=True, stop=True)
                        pe.matmul(psB[l][0:64, :], kp1[:, :], xT[l][:, :], start=True, stop=True).then_inc(a1_qk, 1)
                    for l in lanes:
                        pe.wait_ge(a1_q, nth(l))
                        for t in range(TILES):
                            last = pe.matmul(psA[l][:, D * t:D * (t + 1)], tile(xT[l], t), c65("wv1"),
                                             start=True, stop=True)
                        last.then_inc(a1_v, 1)
                    for l in lanes:
                        pe.wait_ge(a1_k, nth(l))
                        pe.wait_ge(a1_vs, nth(l))
                        for hh, ps in enumerate((psA, psB)):
                            r = slice(D1 * hh, D1 * (hh + 1))
                            for t in range(TILES):
                                last = pe.matmul(tile(ps[l], t), tile(fm[l][r, :], t), tile(fm2[l][r, :], t),
                                                 start=True, stop=True)
                        last.then_inc(a1_s, 1)
                    for l in lanes:
                        pe.wait_ge(a1_full, 2 * (l + 1))
                        pe.wait_ge(a1_m, 2 * (l + 1))
                        for ps, src in ((psA, big_a), (psB, big_b)):
                            for t in range(TILES):
                                last = pe.transpose(tile(ps[l], t), tile(src[l], t), ident)
                        last.then_inc(a1_turned, 1)
                    for l in lanes:
                        pe.wait_ge(a1_aT, nth(l))
                        for t in range(TILES):
                            for hh in range(H1):
                                c = D1 * hh
                                last = pe.matmul(psA[l][:, D * t + c:D * t + c + D1], tile(hid[l][:, hh, :], t),
                                                 v_sb[l][:, t, c:c + D1], start=True, stop=True)
                        last.then_inc(a1_o, 1)

                    turn(lambda l: nth(l, LN_M1), X_M1, xn, ln_out)
                    route(G_M1, X_M1, "route1", E1)
                    turn_gates(G_M1, oh1, E1)
                    for m in range(MT):
                        for l in lanes:
                            ps = (psA, psB)[m % 2]
                            if m == 0:
                                pe.wait_ge(gTb_ready, nth(l))
                                pe.wait_ge(gT_ready, nth(l, G_M1))
                            if m >= 2:
                                pe.wait_ge((m1_h, m1_o)[m % 2], nth(l, 0))
                            up(ps[l][:, :], "w1_1", m, l)
                            pe.matmul(ps[l][:, :], sel1[:, P * m:P * (m + 1)], gTb[l][0:E1, :],
                                      start=False, stop=True).then_inc(m1_z, 1)
                    for l in lanes:
                        pe.wait_ge(m1_h, nth(l, 1))
                        pe.wait_ge(m1_o, nth(l, 1))
                        for t in range(TILES):
                            o = psA[l][:, D * t:D * (t + 1)]
                            for m in range(MT):
                                a = C128["w2_1"][0] + D * m
                                pe.matmul(o, tile(hid[l][:, m, :], t), k128[:, a:a + D], start=(m == 0), stop=False)
                            last = pe.matmul(o, tile(gT[l][:, :], t), c32("b2_1"), start=False, stop=True)
                        last.then_inc(m1_z, 1)

                    turn(lambda l: nth(l, LN_A2), X_A2, xn, ln_out)
                    for l in lanes:
                        pe.wait_ge(x_ready, nth(l, X_A2))
                        pe.matmul(psB[l][0:64, :], c64("q2"), xT[l][0:64, :], start=True, stop=True).then_inc(a2_q, 1)
                        for t in range(TILES):
                            last = pe.matmul(tile(psA[l], t), tile(xT[l][0:64, :], t), c64("kv2"), start=True, stop=True)
                        last.then_inc(a2_kv, 1)
                    for l in lanes:
                        pe.wait_ge(a2_qe, nth(l))
                        pe.wait_ge(a2_kf, nth(l))
                        pe.wait_ge(a2_v, nth(l))
                        for t in range(TILES):
                            last = pe.matmul(psB[l][0:64, KV2 * t:KV2 * (t + 1)], kf[l][:, 0, t, :], v_sb[l][:, t, :],
                                             start=True, stop=True)
                        last.then_inc(a2_s, 1)
                    for l in lanes:
                        pe.wait_ge(a2_qf, nth(l))
                        pe.wait_ge(a2_sm, nth(l))
                        for t in range(TILES):
                            last = pe.matmul(psA[l][:, KV2 * t:KV2 * (t + 1)], tile(fm2[l][0:64, :], t), kvm[l][:, t, :],
                                             start=True, stop=True)
                        last.then_inc(a2_n, 1)
                    turn(lambda l: nth(l, 1), X_IN2, aff, ln_affine)
                    for l in lanes:
                        pe.wait_ge(x_ready, nth(l, X_IN2))
                        pe.matmul(psB[l][0:64, :], c64("w1_2a"), xT[l][0:64, :], start=True, stop=True).then_inc(a2_z, 1)
                    for l in lanes:
                        pe.wait_ge(a2_g, nth(l))
                        for t in range(TILES):
                            last = pe.matmul(psA[l][:, D * t:D * (t + 1)], tile(fm[l], t), c65("w2_2a"),
                                             start=True, stop=True)
                        last.then_inc(a2_y, 1)

                    turn(lambda l: nth(l, LN_M2), X_M2, xn, ln_out)
                    route(G_M2, X_M2, "route2", E2)
                    for l in lanes:
                        pe.wait_ge(g_done, nth(l, G_M2))
                        for t in range(TILES):
                            last = pe.transpose(psA[l][0:SPLIT * E2, P * t:P * (t + 1)], g3[l][:, t, :], ident)
                        last.then_inc(g_turned, 1)
                    for m in range(MT):
                        for l in lanes:
                            if m == 0:
                                pe.wait_ge(gT_ready, nth(l, G_M2))
                            else:
                                pe.wait_ge(m2_h, nth(l, m - 1))
                            up(psA[l][:, :], "w1_2", m, l).then_inc(m2_z, 1)
                            if m:
                                pe.wait_ge(m2_hg, nth(l, m - 1))
                            pe.matmul(psB[l][:, :], sel2[:, P * m:P * (m + 1)], gTb[l][0:SPLIT * E2, :],
                                      start=True, stop=True).then_inc(m2_g, 1)
                    for l in lanes:
                        pe.wait_ge(m2_hg, nth(l, MT - 1))
                        for t in range(TILES):
                            o = psA[l][:, D * t:D * (t + 1)]
                            for m in range(MT):
                                a = C128["w2_2"][0] + D * m
                                pe.matmul(o, tile(hid[l][:, m, :], t), k128[:, a:a + D], start=(m == 0), stop=False)
                            last = pe.matmul(o, tile(gT[l][0:E2, :], t), c32("b2_2", E2), start=False, stop=True)
                        last.then_inc(m2_o, 1)

                    turn(lambda l: nth(l, LN_A3), X_A3, xn, ln_out)
                    for l in lanes:
                        pe.wait_ge(x_ready, nth(l, X_A3))
                        pe.wait_ge(xs_ready, nth(l, XS_A3))
                        for i, ps in enumerate((psA, psB)):
                            pe.matmul(ps[l][:, :], b_hi[:, P * i:P * (i + 1)], xs[l][:, :], start=True, stop=False)
                            last = pe.matmul(ps[l][:, :], b_lo[:, P * i:P * (i + 1)], xs[l][:, :],
                                             start=False, stop=True)
                        last.then_inc(a3_p, 1)
                    for l in lanes:
                        pe.wait_ge(a3_c, 2 * (l + 1))
                        for t in range(TILES):
                            o = psA[l][:, D * t:D * (t + 1)]
                            pe.matmul(o, tile(big_a[l], t), c_cos[:, :], start=True, stop=False)
                            pe.matmul(o, tile(big_b[l], t), c_sin[:, :], start=False, stop=False)
                            last = pe.matmul(o, tile(xT[l][0:64, :], t), diag3[:, :], start=False, stop=True)
                        last.then_inc(a3_y, 1)

                    turn(lambda l: nth(l, LN_M3), X_M3, xn, ln_out)
                    for l in lanes:
                        pe.wait_ge(x_ready, nth(l, X_M3))
                        pe.matmul(psB[l][0:G3, :], c65("proj3"), xT[l][:, :], start=True, stop=True).then_inc(m3_z, 1)

                    def weights3(p):
                        for l in lanes:
                            if p == 0:
                                pe.wait_ge(m3_g, nth(l))
                                pe.wait_ge(m3_sx, nth(l))
                            else:
                                pe.wait_ge(m3_s, nth(l, p - 1))
                            pe.matmul(psA[l][:, :], w3_rows[32 * l:32 * l + G3, P * p:P * (p + 1)], big3[l],
                                      start=True, stop=True).then_inc(m3_w, 1)

                    def gather3(p):
                        for l in lanes:
                            pe.wait_ge(m3_p, nth(l, p))
                            a = D - 2 * p
                            pe.matmul(psB[l][half3(l), :], pick3[:, a:a + D], pr[l][:, p % 2, :],
                                      start=(p == 0), stop=(p == PAIRS - 1)).then_inc(m3_used, 1)

                    big3 = [gTb[l][32 * l:32 * l + G3, :] for l in lanes]
                    weights3(0)
                    for p in range(PAIRS):
                        if p + 1 < PAIRS:
                            weights3(p + 1)
                        gather3(p)
                    for l in lanes:
                        pe.wait_ge(m3_ys, nth(l))
                        for t in range(TILES):
                            last = pe.transpose(psA[l][:, D * t:D * (t + 1)], tile(fm2[l][0:64, :], t), cc("ident", 64)[:, 0:64])
                        last.then_inc(m3_t, 1)

                @block.vector
                def _(dve):
                    V = nc.vector

                    def norm(use, src, ready, at):
                        for l in lanes:
                            dve.wait_ge(ready, nth(l, at))
                            V.tensor_reduce(stat[l][:, 0, :], src[l][:, :, :], X, ALU.add).then_inc(ln_sum, 1)
                        for l in lanes:
                            dve.wait_ge(ln_sum, nth(l, use))
                            V.scalar_tensor_tensor(cen[l][:, :, :], spread(stat[l][:, 0, :], D), -1.0 / D,
                                                   src[l][:, :, :], ALU.mult, ALU.add).then_inc(ln_cen, 1)
                        for l in lanes:
                            dve.wait_ge(ln_sq, nth(l, use))
                            V.tensor_reduce(stat[l][:, 1, :], sq[l][:, :, :], X, ALU.add).then_inc(ln_var, 1)
                        for l in lanes:
                            dve.wait_ge(ln_rstd, nth(l, use))
                            V.tensor_tensor(xn[l][:, :, :], cen[l][:, :, :], spread(stat[l][:, 3, :], D),
                                            ALU.mult).then_inc(ln_out, 1)

                    def low_parts(use):
                        for l in lanes:
                            dve.wait_ge(xs_hi, nth(l, use))
                            dve.wait_ge(x_ready, nth(l, (X_M0, X_M1, X_M2, X_A3)[use]))
                            V.tensor_tensor(xs[l][D:P, :], psA[l][0:D, :], xs[l][0:D, :].bitcast(F32),
                                            ALU.subtract).then_inc(xs_ready, 1)

                    gcount = [0]

                    def gstep_all(emit):
                        for l in lanes:
                            if gcount[0]:
                                dve.wait_ge(gstep, nth(l, gcount[0] - 1))
                            emit(l).then_inc(gstep, 1)
                        gcount[0] += 1

                    def first_of(E, scores, peak, onehot):
                        def w(b, l):
                            return b[l][:, :, 0:E]
                        gstep_all(lambda l: V.tensor_reduce(gs[l][:, peak, :], w(scores, l), X, ALU.max))
                        gstep_all(lambda l: V.tensor_tensor(w(ge, l), w(scores, l), spread(gs[l][:, peak, :], E), ALU.is_equal))
                        gstep_all(lambda l: V.tensor_tensor(w(gk, l), w(ge, l), rank(E), ALU.mult))
                        gstep_all(lambda l: V.tensor_reduce(gs[l][:, 2, :], w(gk, l), X, ALU.max))
                        gstep_all(lambda l: V.tensor_tensor(w(onehot, l), w(gk, l), spread(gs[l][:, 2, :], E), ALU.is_equal))

                    def copy_logits(use, E):
                        for l in lanes:
                            dve.wait_ge(logits, nth(l, use))
                            V.tensor_copy(lg[l][:, :, 0:E], psB[l][:, 0:TILES * E].rearrange("p (t e) -> p t e", e=E)
                                          ).then_inc(gstep, 1)
                        gcount[0] += 1

                    def top2(use, E):
                        def w(b, l):
                            return b[l][:, :, 0:E]
                        copy_logits(use, E)
                        first_of(E, lg, 0, oh1)
                        gstep_all(lambda l: V.scalar_tensor_tensor(w(lg, l), w(oh1, l), -BIG, w(lg, l), ALU.mult, ALU.add))
                        first_of(E, lg, 1, oh2)
                        gstep_all(lambda l: V.tensor_tensor(gs[l][:, 3, :], gs[l][:, 1, :], gs[l][:, 0, :], ALU.subtract))
                        turn = {G_M0: 0, G_M2: 1}[use]
                        for l in lanes:
                            dve.wait_ge(g_exp, nth(l, turn))
                        gstep_all(lambda l: V.tensor_scalar(gs[l][:, 5, :], gs[l][:, 4, :], 1.0, None, ALU.add))
                        gstep_all(lambda l: V.reciprocal(gs[l][:, 6, :], gs[l][:, 5, :]))
                        gstep_all(lambda l: V.tensor_tensor(gs[l][:, 7, :], gs[l][:, 6, :], gs[l][:, 4, :], ALU.mult))
                        gstep_all(lambda l: V.tensor_tensor(w(ge, l), w(oh1, l), spread(gs[l][:, 6, :], E), ALU.mult))
                        gstep_all(lambda l: V.tensor_tensor(w(gk, l), w(oh2, l), spread(gs[l][:, 7, :], E), ALU.mult))
                        for l in lanes:
                            dve.wait_ge(gstep, nth(l, gcount[0] - 1))
                            if use == G_M2:
                                V.tensor_tensor(g3[l][:, :, 0:E2], w(ge, l), w(gk, l), ALU.add).then_inc(g_sum, 1)
                                dve.wait_ge(g_sum, nth(l))
                            else:
                                V.tensor_tensor(w(gate, l), w(ge, l), w(gk, l), ALU.add).then_inc(g_done, 1)

                    def add_psum(done, at, use):
                        for l in lanes:
                            dve.wait_ge(done, at(l))
                            V.tensor_tensor(h[l][:, :, :], rows(psA[l]), h[l][:, :, :], ALU.add).then_inc(h_new, 1)

                    for l in lanes:
                        src = emb[:, bass.ds(it * (LANES * TILES) + l * TILES, TILES), :]
                        kp = keep[:, bass.ds(it * (LANES * TILES) + l * TILES, TILES)]
                        V.tensor_tensor(h[l][:, :, :], src, kp[:, :, None].broadcast_to([P, TILES, D]),
                                        ALU.mult).then_inc(h_new, 1)

                    norm(LN_A0, h, h_new, H_EMB)
                    for l in lanes:
                        dve.wait_ge(a0_rv, nth(l))
                        V.tensor_copy(v_sb[l][:, :, 0:D], rows(psA[l])).then_inc(a0_v, 1)
                    for l in lanes:
                        dve.wait_ge(a0_s, nth(l))
                        V.tensor_tensor(big_a[l][:, :].rearrange("p (t s) -> p t s", t=TILES),
                                        psB[l][:, :].rearrange("p (t s) -> p t s", t=TILES),
                                        cc("decay")[:, None, :].broadcast_to([P, TILES, P]), ALU.mult).then_inc(a0_p, 1)
                    add_psum(a0_o, lambda l: nth(l), H_A0)

                    norm(LN_M0, h, h_new, H_A0)
                    low_parts(XS_M0)
                    top2(G_M0, E0)
                    for q in range(E0 // 2):
                        for l in lanes:
                            dve.wait_ge(m0_o, nth(l, q))
                            if q == 0:
                                dve.wait_ge(g_done, nth(l, G_M0))
                            if q >= 2:
                                dve.wait_ge(m0_acc, nth(l, q - 2))
                            g = gate[l][:, :, 2 * q:2 * q + 2].rearrange("p t e -> p e t")
                            V.tensor_tensor(prod(l, q).rearrange("p (e t d) -> p e t d", e=2, t=TILES),
                                            psB[l][:, :].rearrange("p (e t d) -> p e t d", e=2, t=TILES),
                                            g[:, :, :, None].broadcast_to([P, 2, TILES, D]), ALU.mult).then_inc(m0_prod, 1)
                    for l in lanes:
                        dve.wait_ge(m0_acc, nth(l, E0 // 2 - 1))
                        V.tensor_tensor(y[l][:, :, :], rows(big_c[l]), xn[l][:, :, :], ALU.add).then_inc(y_part, 1)
                    for l in lanes:
                        dve.wait_ge(y_part, nth(l, 0))
                        odd = big_c[l][:, TILES * D:].rearrange("p (t d) -> p t d", t=TILES)
                        V.tensor_tensor(y[l][:, :, :], odd, y[l][:, :, :], ALU.add).then_inc(y_part, 1)
                    for l in lanes:
                        dve.wait_ge(m0_b, nth(l))
                        dve.wait_ge(y_part, nth(l, 1))
                        V.tensor_tensor(y[l][:, :, :], rows(psA[l]), y[l][:, :, :], ALU.add).then_inc(y_new, 1)
                    norm(LN_IN0, y, y_new, Y_IN0)
                    for l in lanes:
                        dve.wait_ge(ln_affine, nth(l, 0))
                        V.tensor_tensor(h[l][:, :, :], aff[l][:, :, :], h[l][:, :, :], ALU.add).then_inc(h_new, 1)

                    norm(LN_A1, h, h_new, H_M0)
                    for l in lanes:
                        dve.wait_ge(a1_qk, nth(l))
                        V.tensor_copy(fm2[l][0:64, :], psB[l][0:64, :]).then_inc(a1_k, 1)
                    for l in lanes:
                        dve.wait_ge(a1_v, nth(l))
                        V.tensor_copy(v_sb[l][:, :, 0:D], rows(psA[l])).then_inc(a1_vs, 1)
                    block1 = cc("block")[:, None, :].broadcast_to([P, TILES, P])
                    for l in lanes:
                        dve.wait_ge(a1_s, nth(l))
                        for ps, dst in ((psA, big_a), (psB, big_b)):
                            V.tensor_tensor(dst[l][:, :].rearrange("p (t m) -> p t m", t=TILES),
                                            ps[l][:, :].rearrange("p (t m) -> p t m", t=TILES), block1,
                                            ALU.mult).then_inc(a1_m, 1)
                    for l in lanes:
                        for hh, src in enumerate((big_a, big_b)):
                            dve.wait_ge(a1_m, 2 * l + hh + 1)
                            V.tensor_reduce(s8[l][:, TILES * hh:TILES * (hh + 1), :],
                                            src[l][:, :].rearrange("p (t g j) -> p t j g", t=TILES, j=BS1),
                                            X, ALU.add).then_inc(a1_e8, 1)
                    for l in lanes:
                        dve.wait_ge(a1_e8, 2 * (l + 1))
                        V.tensor_reduce(s8s[l][:, 0, :], s8[l][:, :, :], X, ALU.max).then_inc(a1_step, 1)

                    def spread8(l, i):
                        return s8s[l][:, i, :][:, :, None].broadcast_to([P, H1 * TILES, BS1])
                    for l in lanes:
                        dve.wait_ge(a1_step, nth(l, 0))
                        V.tensor_tensor(s8b[l][:, :, :], s8[l][:, :, :], spread8(l, 0), ALU.subtract).then_inc(a1_step, 1)
                    for l in lanes:
                        dve.wait_ge(a1_exp, nth(l))
                        V.tensor_reduce(s8s[l][:, 1, :], s8b[l][:, :, :], X, ALU.add).then_inc(a1_step, 1)
                    for l in lanes:
                        dve.wait_ge(a1_step, nth(l, 2))
                        V.reciprocal(s8s[l][:, 2, :], s8s[l][:, 1, :]).then_inc(a1_step, 1)
                    for l in lanes:
                        dve.wait_ge(a1_step, nth(l, 3))
                        V.tensor_tensor(s8[l][:, :, :], s8b[l][:, :, :], spread8(l, 2), ALU.mult).then_inc(a1_step, 1)
                    add_psum(a1_o, lambda l: nth(l), H_A1)

                    norm(LN_M1, h, h_new, H_A1)
                    low_parts(XS_M1)
                    copy_logits(G_M1, E1)
                    first_of(E1, lg, 0, oh1)
                    for l in lanes:
                        dve.wait_ge(gstep, nth(l, gcount[0] - 1))
                        V.tensor_copy(gs[l][:, 7, 0:1], gs[l][:, 2, 0:1]).then_inc(g_done, 1)
                    for l in lanes:
                        dve.wait_ge(gT_ready, nth(l, G_M1))
                        V.tensor_scalar(gTb[l][0:E1, :], gT[l][:, :], -1.0, BIG, ALU.add, ALU.mult).then_inc(gTb_ready, 1)
                    for m in range(1, MT, 2):
                        for l in lanes:
                            dve.wait_ge(m1_z, nth(l, m))
                            V.tensor_scalar(hid[l][:, m, :], psB[l][:, :], c128("b1_1")[:, m:m + 1], 0.0,
                                            ALU.add, ALU.max).then_inc(m1_o, 1)
                    for l in lanes:
                        dve.wait_ge(m1_z, nth(l, MT))
                        V.scalar_tensor_tensor(h[l][:, :, :], rows(psA[l]), 0.0, h[l][:, :, :], ALU.max,
                                               ALU.add).then_inc(h_new, 1)

                    norm(LN_A2, h, h_new, H_M1)
                    for l in lanes:
                        dve.wait_ge(a2_ke, nth(l))
                        kv = psA[l][:, :].rearrange("p (t c) -> p t c", t=TILES)
                        V.tensor_copy(v_sb[l][:, :, 0:D], kv[:, :, D:2 * D]).then_inc(a2_v, 1)
                        V.scalar_tensor_tensor(kf[l][:, 0, :, :], kf[l][:, 0, :, :], 1.0, kf[l][:, 1, :, :],
                                               ALU.min, ALU.add).then_inc(a2_kf, 1)
                        V.scalar_tensor_tensor(fm2[l][0:64, :], fm2[l][0:64, :], 1.0, big_a[l][0:64, :],
                                               ALU.min, ALU.add).then_inc(a2_qf, 1)
                    heads = cc("heads", 64)[:, None, :].broadcast_to([64, TILES, KV2])
                    for l in lanes:
                        dve.wait_ge(a2_s, nth(l))
                        V.tensor_tensor(kvm[l][:, :, :], psB[l][0:64, 0:TILES * KV2].rearrange("p (t c) -> p t c", c=KV2),
                                        heads, ALU.mult).then_inc(a2_sm, 1)
                    for l in lanes:
                        dve.wait_ge(a2_n, nth(l))
                        nd = psA[l][:, 0:TILES * KV2].rearrange("p (t c) -> p t c", c=KV2)
                        V.tensor_scalar(lg[l][:, :, 0:H2], nd[:, :, D:KV2], DEN_EPS, None, ALU.add).then_inc(a2_step, 1)
                    for l in lanes:
                        dve.wait_ge(a2_step, nth(l, 0))
                        V.reciprocal(lg[l][:, :, 8:8 + H2], lg[l][:, :, 0:H2]).then_inc(a2_step, 1)
                    for l in lanes:
                        dve.wait_ge(a2_step, nth(l, 1))
                        for t in range(TILES):
                            num = psA[l][:, KV2 * t:KV2 * t + D].rearrange("p (h m) -> p h m", m=D2)
                            z = lg[l][:, t, 8:8 + H2][:, :, None].broadcast_to([P, H2, D2])
                            last = V.tensor_tensor(y[l][:, t, :].rearrange("p (h m) -> p h m", m=D2), num, z, ALU.mult)
                        last.then_inc(a2_step, 1)
                    for l in lanes:
                        dve.wait_ge(a2_step, nth(l, 2))
                        V.tensor_tensor(y[l][:, :, :], y[l][:, :, :], xn[l][:, :, :], ALU.add).then_inc(y_new, 1)
                    norm(LN_IN2, y, y_new, Y_IN2)
                    for l in lanes:
                        dve.wait_ge(a2_y, nth(l))
                        V.tensor_tensor(y[l][:, :, :], rows(psA[l]), aff[l][:, :, :], ALU.add).then_inc(y_new, 1)
                    norm(LN_OUT2, y, y_new, Y_OUT2)
                    for l in lanes:
                        dve.wait_ge(ln_affine, nth(l, 2))
                        V.tensor_tensor(h[l][:, :, :], aff[l][:, :, :], h[l][:, :, :], ALU.add).then_inc(h_new, 1)

                    norm(LN_M2, h, h_new, H_A2)
                    low_parts(XS_M2)
                    top2(G_M2, E2)
                    parts = [g3[l][:, :, :].rearrange("p t (s e) -> p s t e", s=SPLIT) for l in lanes]
                    for l in lanes:
                        V.tensor_copy(gh[l][:, :, :], parts[l][:, 0]).then_inc(gsplit, 1)
                    for l in lanes:
                        dve.wait_ge(gsplit, nth(l, 0))
                        V.tensor_tensor(parts[l][:, 1], parts[l][:, 0], gh[l][:, :, :], ALU.subtract).then_inc(gsplit, 1)
                    for l in lanes:
                        dve.wait_ge(gsplit, nth(l, 1))
                        V.tensor_copy(gh[l][:, :, :], parts[l][:, 1]).then_inc(gsplit, 1)
                    for l in lanes:
                        dve.wait_ge(gsplit, nth(l, 2))
                        V.tensor_tensor(parts[l][:, 2], parts[l][:, 1], gh[l][:, :, :], ALU.subtract).then_inc(g_done, 1)
                    for m in range(MT):
                        for l in lanes:
                            dve.wait_ge(m2_h, nth(l, m))
                            dve.wait_ge(m2_g, nth(l, m))
                            V.tensor_tensor(hid[l][:, m, :], psB[l][:, :], hid[l][:, m, :], ALU.mult).then_inc(m2_hg, 1)
                    for l in lanes:
                        dve.wait_ge(m2_o, nth(l))
                        dve.wait_ge(m2_res, nth(l))
                        V.tensor_tensor(h[l][:, :, :], rows(psA[l]), y[l][:, :, :], ALU.add).then_inc(h_new, 1)

                    norm(LN_A3, h, h_new, H_M2)
                    low_parts(XS_A3)
                    for l in lanes:
                        dve.wait_ge(a3_p, nth(l))
                        for ps, wave, dst in ((psA, cosines, big_a), (psB, sines, big_b)):
                            V.tensor_tensor(dst[l][:, :].rearrange("p (t s) -> p t s", t=TILES),
                                            ps[l][:, :].rearrange("p (t s) -> p t s", t=TILES),
                                            wave[:, None, :].broadcast_to([P, TILES, P]), ALU.mult).then_inc(a3_m, 1)
                    for l in lanes:
                        dve.wait_ge(a3_w, nth(l))
                        V.tensor_tensor_scan(hid[l][:, 0, :], decay3[:, :], big_c[l][:, :], 0.0,
                                             ALU.mult, ALU.add).then_inc(a3_z, 1)
                    add_psum(a3_y, lambda l: nth(l), H_A3)

                    norm(LN_M3, h, h_new, H_A3)
                    for l in lanes:
                        dve.wait_ge(m3_z, nth(l))
                        V.tensor_scalar(gTb[l][32 * l:32 * l + G3, :], psB[l][0:G3, :], GATE_MIN, None, ALU.is_gt).then_inc(m3_g, 1)
                    for p in range(PAIRS):
                        for l in lanes:
                            dve.wait_ge(m3_s, nth(l, p))
                            if p == 0:
                                dve.wait_ge(m3_sx, nth(l))
                            if p >= 2:
                                dve.wait_ge(m3_used, nth(l, p - 2))
                            V.tensor_tensor(pr[l][:, p % 2, :], sg[l][:, p % 2, :], sx[l][:, :], ALU.mult).then_inc(m3_p, 1)
                    for l in lanes:
                        dve.wait_ge(m3_used, nth(l, PAIRS - 1))
                        V.tensor_scalar(fm2[l][0:64, :], psB[l][half3(l), :], c128("scale3")[half3(l), :], None, ALU.mult).then_inc(m3_ys, 1)
                    for l in lanes:
                        dve.wait_ge(m3_t, nth(l))
                        V.tensor_tensor(h[l][:, :, :], rows(psA[l]), h[l][:, :, :], ALU.add).then_inc(h_new, 1)

            nc.sync.sem_clear(range(sems[sems_setup].num, sems[-1].num + 1))
            nc.all_engine_barrier()


def shape_constants():
    import numpy as np
    c = np.zeros((P, CC["_"][1]), np.float32)
    b = np.zeros((P, CB["_"][1]), np.float32)

    def put(name, a):
        into, (s, e) = (c, CC[name]) if name in CC else (b, CB[name])
        a = np.asarray(a, np.float32)
        into[0:a.shape[0], s:e] = a

    i = np.arange(P)
    put("ident", np.eye(P))
    gap = i[None, :] - i[:, None]
    put("decay", np.where(gap >= 0, np.exp(gap * np.log(np.float64(0.96875))), 0.0))
    put("block", i[:, None] // BS1 == i[None, :] // BS1)
    j = np.arange(D)
    head = np.arange(H2)
    put("heads", np.concatenate([j[:, None] // D2 == j[None, :] // D2, j[:, None] // D2 == head[None, :]], 1))
    for name, E in (("rank0", E0), ("rank1", E1), ("rank2", E2)):
        put(name, np.tile(E - np.arange(E), (P, 1)))
    put("time", np.tile(i, (P, 1)))
    put("later", np.tile(i > 0, (P, 1)))
    put("sign", np.where(i < D, 1.0, -1.0)[:, None])
    hid = np.arange(HID)
    put("sel2", np.arange(SPLIT * E2)[:, None] % E2 == hid[None, :] // F2)
    put("exp1", np.arange(E1)[:, None] == hid[None, :] // F1)
    put("pick3", np.arange(2 * D)[None, :] == D + i[:, None] // D)
    return c, b


def kernel(**inputs):
    import numpy as np
    import concourse.bacc as bacc
    from concourse.bass_utils import run_bass_kernel_spmd

    a = {k: np.asarray(v) for k, v in inputs.items()}

    def row(x):
        return x.reshape(1, -1)

    def with_bias(w, b):
        return np.concatenate([w, row(b)], 0)

    zero = np.zeros((1, D), np.float32)
    w65 = np.concatenate([
        with_bias(a["L0_ffn_gate_w"], a["L0_ffn_gate_b"]),
        with_bias(a["L1_attn_Wv"].T, a["L1_attn_bv"]),
        with_bias(a["L1_ffn_router_w"].T, a["L1_ffn_router_b"]),
        with_bias(a["L2_attn_W2"].T, a["L2_attn_b2"]),
        with_bias(a["L2_ffn_router_w"].T, np.zeros(E2, np.float32)),
        np.concatenate([with_bias(a["L3_ffn_proj_w"].T, a["L3_ffn_proj_b"])] * SPLIT, 1),
    ], 1)
    wup = np.concatenate([a[n].transpose(1, 0, 2).reshape(D, -1) for n in ("L0_ffn_w1", "L1_ffn_W1", "L2_ffn_w1")], 1)
    scale3 = a["L3_ffn_scale"].reshape(D, 1)
    qkv = a["L2_attn_Wqkv"]
    w64 = np.concatenate([
        a["L0_attn_Wq"], a["L0_attn_Wk"], a["L0_attn_Wv"].T,
        qkv[0:D].T, qkv[D:3 * D].T, a["L2_attn_W1"].T, a["L2_attn_b1"].reshape(D, 1),
        a["L3_attn_B_re"], a["L3_attn_B_im"], a["L3_attn_gamma_log"].reshape(D, 1),
        a["L3_attn_D"].reshape(D, 1),
    ], 1)
    c_re, c_im = a["L3_attn_C_re"].T, a["L3_attn_C_im"].T
    nu, theta = a["L3_attn_nu_log"].reshape(D, 1), a["L3_attn_theta_log"].reshape(D, 1)
    w3 = a["L3_ffn_weight"][0].transpose(0, 2, 1).reshape(P, 256)
    w128 = np.concatenate([
        a["L0_ffn_w2"].transpose(1, 0, 2).reshape(F0, E0 * D),
        a["L1_ffn_W2"].reshape(MT, P, D).transpose(1, 0, 2).reshape(P, MT * D),
        a["L2_ffn_w2"].reshape(MT, P, D).transpose(1, 0, 2).reshape(P, MT * D),
        np.concatenate([c_re, c_im], 0), np.concatenate([c_im, c_re], 0),
        np.concatenate([nu, nu], 0), np.concatenate([theta, theta], 0), w3,
        a["L0_ffn_b1"].T, a["L1_ffn_b1"].reshape(MT, P).T, a["L2_ffn_b1"].reshape(MT, P).T,
        np.concatenate([scale3, scale3], 0),
    ], 1)

    def per_head(w, b):
        return np.concatenate([w.reshape(H1, D1, D), b.reshape(H1, D1, 1)], 2).transpose(1, 0, 2).reshape(D1, H1 * 65)

    def rows32(x):
        return np.concatenate([x, np.zeros((32 - x.shape[0], x.shape[1]), np.float32)], 0)

    w32 = np.concatenate([
        per_head(a["L1_attn_Wq"], a["L1_attn_bq"]), per_head(a["L1_attn_Wk"], a["L1_attn_bk"]),
        a["L1_attn_P"], rows32(a["L0_ffn_b2"]), a["L1_ffn_b2"], rows32(a["L2_ffn_b2"]),
    ], 1)
    wrow = np.concatenate([row(a[n]) for n in ("L0_ffn_gamma", "L0_ffn_beta", "L2_attn_ln1_g", "L2_attn_ln1_b",
                                               "L2_attn_ln2_g", "L2_attn_ln2_b")], 1)
    consts, binary = shape_constants()
    arrays = {
        "ids": np.ascontiguousarray(a["x"].T), "emb_w": np.ascontiguousarray(a["L0_tok_W"].T),
        "w65": w65, "wup": wup, "w64": w64, "w128": w128, "w32": w32, "wrow": wrow, "consts": consts, "binary": binary,
    }
    nc = bacc.Bacc("TRN2", target_bir_lowering=False, num_devices=1)
    aps = {n: nc.dram_tensor(n, list(v.shape), mybir.dt.from_np(v.dtype), kind="ExternalInput").ap()
           for n, v in arrays.items()}
    out = nc.dram_tensor("out", [NSEQ, P, D], mybir.dt.float32, kind="ExternalOutput").ap()
    tower(nc, aps["ids"], aps["emb_w"], aps["w65"], aps["wup"], aps["w64"], aps["w128"], aps["w32"], aps["wrow"],
          aps["consts"], aps["binary"], out.rearrange("(i l t) p d -> i l t p d", i=PASSES, l=LANES))
    r = run_bass_kernel_spmd(nc, [arrays], core_ids=[0])
    return r.results[0]["out"]
```

```python
import concourse.bass as bass
from concourse import mybir
from contextlib import ExitStack

P = 128
D = 64
LANES = 4
TILES = 4
NT = TILES * P
NSEQ = 32
PASS_SEQ = LANES * TILES
PASSES = NSEQ // PASS_SEQ
GROUPS = 2
GROUP_LANES = LANES // GROUPS
GROUP_TILES = GROUP_LANES * TILES
PLACES = (2, 20, 37.5, 60, 80, 95, 105, 125, 144, 160,
          181, 203, 219, 227, 250, 272, 300, 312, 340, 368)
ISSUE = ((-21.7, -8.8, 27.9, 62.3, 99.1, 106.4, 112, 132.6, 149.8, 167.3,
          178.9, 218.3, 237.2, 247.6, 266.5, 299, 346.9, 356.4, 363.7, 393.1),
         (-16.6, 7.7, 42.2, 79.2, 110.8, 118.2, 125.3, 141.3, 166, 180.1,
          194.7, 210.8, 225.3, 232, 264.9, 291.4, 332.7, 356, 363.7, 391.9))

E0, F0 = 16, 128
E1, F1 = 32, 16
E2, F2 = 8, 64
E3 = 8
HID = 512
MT = HID // P
H1, D1, BS1 = 2, 32, 8
H2, D2 = 8, 8
KV2 = D + H2
PAIRS = D // 2
SPLIT = 3
G3 = SPLIT * E3
BIG = 1.0e30
LN_EPS = 1e-5
DEN_EPS = 1e-6
GATE_MIN = 2.0 ** -24
LOG2E = 1.4426950408889634
MAGIC = 12582912.0
LN2_HI, LN2_LO = 0.693359375, -2.12194440e-4
PI = 3.141592653589793
TWO_PI_1 = 6.28125
TWO_PI_2 = 0.00193500518798828125
TWO_PI_3 = 2.0 * PI - TWO_PI_1 - TWO_PI_2
HALF_PI = PI / 2.0
QUANT = 6144.0

def columns(widths):
    at, out = 0, {}
    for name, width in widths:
        out[name] = (at, at + width)
        at += width
    out["_"] = (0, at)
    return out


C65 = columns([("wv1", D), ("w2_2a", D), ("proj3", G3)])
CUP = columns([("w1_0", E0 * F0), ("w1_1", HID), ("w1_2", HID), ("route0", E0), ("route1", E1), ("route2", E2)])
N_UP = CUP["_"][1]
C64 = columns([("wq0", D), ("wk0", D), ("wv0", D), ("q2", D), ("kv2", 2 * D), ("w1_2a", D),
               ("b1_2a", 1), ("b_re", D), ("b_im", D)])
C128 = columns([("w2_0", E0 * D), ("w2_1", MT * D), ("w2_2", MT * D), ("c_a", D), ("c_b", D),
                ("w3", 256), ("b1_0", E0), ("b1_1", MT), ("b1_2", MT),
                ("scale3", 1)])
C32 = columns([("qb1", H1 * 65), ("kb1", H1 * 65), ("p1", D1), ("b2_0", D), ("b2_1", D), ("b2_2", D)])
CROW = columns([("g0", D), ("be0", D), ("g2a", D), ("be2a", D), ("g2b", D), ("be2b", D),
                ("bias0", E0), ("bias1", E1), ("d3", D)])
CC = columns([("ident", P), ("decay", P), ("block", P), ("heads", KV2), ("rank0", E0),
              ("rank1", E1), ("rank2", E2), ("time", P), ("later", P), ("sign", 1)])
CB = columns([("sel2", MT * P), ("exp1", MT * P), ("pick3", 3 * D)])


def nth(lane, use=0):
    return use * GROUP_LANES + lane % GROUP_LANES + 1


def tower(nc, ids, emb_w, logs, w65, wup, w64, w128, w32, wrow, consts, binary, out):
    F32, BF16, I32, U32 = mybir.dt.float32, mybir.dt.bfloat16, mybir.dt.int32, mybir.dt.uint32
    F32R = mybir.dt.float32r
    ACT = mybir.ActivationFunctionType
    ALU = mybir.AluOpType
    X = mybir.AxisListType.X

    with ExitStack() as ctx:
        def sb(name, shape, dt=F32):
            return ctx.enter_context(nc.sbuf_tensor(name, shape, dt))

        def per_lane(name, shape, dt=F32):
            return [sb(f"{name}{l}", shape, dt) for l in range(LANES)]

        def per_group(name, shape, dt=F32):
            return [sb(f"{name}{g}", shape, dt) for g in range(GROUPS)]

        def sem(name):
            s = ctx.enter_context(nc.semaphore(name))
            sems.append(s)
            return s

        sems = []
        lanes = range(LANES)

        k65 = sb("k65", [65, C65["_"][1]])
        k64 = sb("k64", [64, C64["_"][1]])
        k128 = sb("k128", [P, C128["_"][1]])
        k32 = sb("k32", [32, C32["_"][1]])
        krow = sb("krow", [P, CROW["_"][1]])
        kc = sb("kc", [P, CC["_"][1]])

        def c65(name):
            a, b = C65[name]
            return k65[:, a:b]

        def c64(name):
            a, b = C64[name]
            return k64[:, a:b]

        def c128(name):
            a, b = C128[name]
            return k128[:, a:b]

        def c32(name, rows=32):
            a, b = C32[name]
            return k32[0:rows, a:b]

        def crow(name):
            a, b = CROW[name]
            return krow[:, None, a:b].broadcast_to([P, TILES, b - a])

        def cc(name, rows=P):
            a, b = CC[name]
            return kc[0:rows, a:b]

        def rank(E):
            return cc({E0: "rank0", E1: "rank1", E2: "rank2"}[E])[:, None, :].broadcast_to([P, GROUP_TILES, E])

        ident = cc("ident")
        ids_sb = sb("ids_sb", [P, NSEQ + PASS_SEQ], I32)
        ids_next = [sb(f"ids_next{g}", [P, GROUP_TILES], I32) for g in range(GROUPS)]
        ids_f = sb("ids_f", [P, NSEQ])
        keep = sb("keep", [P, NSEQ])
        emb = sb("emb", [P, PASS_SEQ, D])

        score0 = sb("score0", [64, D])
        qkp1 = sb("qkp1", [65, 2 * D])
        b_sc = sb("b_sc", [64, 2, D])
        b_f = sb("b_f", [P, 2, P])
        b_hi = sb("b_hi", [P, 2 * P], F32R)
        b_lo = sb("b_lo", [P, 2 * P], F32R)
        up_hi = sb("up_hi", [P, N_UP], F32R)
        up_lo = sb("up_lo", [P, N_UP], F32R)
        c_cos = sb("c_cos", [P, D])
        c_sin = sb("c_sin", [P, D])
        cosines = sb("cosines", [P, P])
        sines = sb("sines", [P, P])
        decay3 = sb("decay3", [P, NT])
        w3_rows = sb("w3_rows", [P, PAIRS * P], BF16)
        kb = sb("kb", [P, CB["_"][1]], BF16)

        def cb(name, rows):
            a, b = CB[name]
            return kb[0:rows, a:b]

        sel1, sel2, pick3 = cb("exp1", E1), cb("sel2", SPLIT * E2), cb("pick3", P)
        ln_logs = sb("ln_logs", [P, 3])
        ex = sb("ex", [P, 6, 3])
        ex_i = sb("ex_i", [P, 3], I32)
        th = sb("th", [P, 8])

        h = per_lane("h", [P, TILES, D])
        xn = per_lane("xn", [P, TILES, D])
        y = per_lane("y", [P, TILES, D])
        aff = per_lane("aff", [P, TILES, D])
        halves_stat = per_group("halves_stat", [P, GROUP_TILES, 6])
        stat = per_group("stat", [P, GROUP_TILES, 2])
        var_eps = per_group("var_eps", [P, GROUP_TILES])
        inv_std = per_group("inv_std", [P, GROUP_TILES])
        neg_half = sb("neg_half", [P, TILES])
        xT = per_lane("xT", [65, NT])
        xs = per_lane("xs", [P, NT], F32R)
        fm = per_lane("fm", [65, NT])
        fm2 = per_lane("fm2", [P, NT])
        v_sb = per_lane("v_sb", [P, TILES, KV2])
        big_a = per_lane("big_a", [P, NT])
        big_b = per_lane("big_b", [P, NT])
        big_c = per_lane("big_c", [P, NT])
        hid = per_lane("hid", [P, MT, NT])
        lg, gk, ge, oh1, oh2 = (
            [big[GROUP_LANES * g + i][:, GROUP_TILES * E1 * j:GROUP_TILES * E1 * (j + 1)].rearrange(
                "p (t e) -> p t e", e=E1) for g in range(GROUPS)]
            for big, i, j in ((big_a, 0, 0), (big_a, 0, 1), (big_a, 1, 0), (big_a, 1, 1), (big_b, 0, 0)))
        kvm = per_lane("kvm", [64, TILES, KV2])
        gate = per_group("gate", [P, GROUP_TILES, E0])
        gs = per_group("gs", [P, 8, GROUP_TILES])
        gT = per_lane("gT", [E1, NT])
        gTb = per_lane("gTb", [P, NT], BF16)
        g3 = per_group("g3", [P, GROUP_TILES, SPLIT * E2])
        gh = per_group("gh", [P, GROUP_TILES, E2], BF16)
        s8 = per_group("s8", [P, H1 * GROUP_TILES, BS1])
        s8b = per_group("s8b", [P, H1 * GROUP_TILES, BS1])
        s8s = per_group("s8s", [P, 3, H1 * GROUP_TILES])
        kf = [hid[l][:, 3, :].rearrange("p (b t d) -> p b t d", b=2, t=TILES) for l in lanes]
        sg = [hid[l][:, 0, :].bitcast(BF16).rearrange("p (b n) -> p b n", b=2) for l in lanes]
        pr = [hid[l][:, 1, :].bitcast(BF16).rearrange("p (b n) -> p b n", b=2) for l in lanes]
        sx = [hid[l][:, 2, :].bitcast(BF16)[:, 0:NT] for l in lanes]

        ph = hid[0][:, 0:2, :].rearrange("p a (b s) -> p (a b) s", s=P)
        w3_hi, w3_mid, w3_lo = (hid[0][:, 2, 128 * i:128 * (i + 1)].bitcast(BF16) for i in range(3))
        w3_r1, w3_r2 = (hid[0][:, 3, 256 * i:256 * (i + 1)] for i in range(2))
        up_raw = [hid[2][:, :, :].rearrange("p a n -> p (a n)"),
                  hid[3][:, :, :].rearrange("p a n -> p (a n)")[:, 0:N_UP - MT * NT]]
        up_cut = (0, MT * NT, N_UP)
        kb_raw = hid[1][:, :, :].rearrange("p a n -> p (a n)")[:, 0:CB["_"][1]]

        psA = [ctx.enter_context(nc.psum_tensor(f"psA{l}", [P, NT], F32)) for l in lanes]
        psB = [ctx.enter_context(nc.psum_tensor(f"psB{l}", [P, NT], F32)) for l in lanes]

        w3_bounce = nc.dram_tensor("w3_bounce", [SPLIT, E3, PAIRS * P], BF16).ap()

        ids_in = sem("ids_in")
        weights_in = sem("weights_in")
        gathered = sem("gathered")
        logs_in = sem("logs_in")
        rows_cleared = sem("rows_cleared")
        ones_set = sem("ones_set")
        consts_in = sem("consts_in")
        v_chain = sem("v_chain")
        folded = sem("folded")
        angles = sem("angles")
        w3_split = sem("w3_split")
        w3_out = sem("w3_out")
        w3_in = sem("w3_in")
        b_scaled = sem("b_scaled")
        up_in = sem("up_in")
        up_rounded = sem("up_rounded")
        b_rounded = sem("b_rounded")
        N_WEIGHTS = 6

        with nc.Block() as block:
            @block.sync
            def _(sp):
                sp.dma_start(ids_sb[:, 0:NSEQ], ids).then_inc(ids_in, 16)
                sp.dma_start(ln_logs[:, :], logs).then_inc(logs_in, 16)
                sp.dma_start(kc[:, :], consts).then_inc(consts_in, 16)
                sp.dma_start(k64[:, :], w64).then_inc(weights_in, 16)
                sp.dma_start(kb_raw, binary).then_inc(weights_in, 16)
                sp.dma_start(k65[:, :], w65).then_inc(weights_in, 16)
                for i in range(2):
                    for half in (slice(0, D), slice(D, P)):
                        sp.dma_start(up_raw[i][half, :], wup[:, up_cut[i]:up_cut[i + 1]]).then_inc(up_in, 16)
                sp.wait_ge(w3_split, 3)
                for s, part in enumerate((w3_hi, w3_mid, w3_lo)):
                    sp.dma_start(w3_bounce[s].rearrange("e (c x) -> (e c) x", x=256),
                                 part[:, :]).then_inc(w3_out, 16)
                sp.wait_ge(w3_out, 16 * SPLIT)
                sp.wait_ge(rows_cleared, 1)
                sp.dma_start(w3_rows[0:G3, :], w3_bounce.rearrange("s e x -> (s e) x")).then_inc(w3_in, 16)
                sp.wait_ge(w3_in, 16)

            @block.gpsimd
            def _(pool):
                pool.wait_ge(ids_in, 16)
                for s in range(PASS_SEQ):
                    pool.indirect_dma_start(
                        emb[:, s, :], None, emb_w,
                        bass.IndirectOffsetOnAxis(ap=ids_sb[:, s:s + 1].bitcast(U32), axis=0)
                    ).then_inc(gathered, 16)
                for l in lanes:
                    nc.gpsimd.memset(xT[l][64:65, :], 1.0).then_inc(ones_set, 1)
                    nc.gpsimd.memset(fm[l][64:65, :], 1.0).then_inc(ones_set, 1)
                pool.wait_ge(ones_set, 2 * LANES)
                nc.gpsimd.memset(w3_rows[:, :], 0.0).then_inc(rows_cleared, 1)
                nc.gpsimd.memset(neg_half[:, :], -0.5)
                for l in lanes:
                    nc.gpsimd.memset(v_sb[l][:, :, D:KV2], 1.0)
                    nc.gpsimd.memset(gTb[l][:, :], 0.0)
                pool.wait_ge(gathered, 16 * PASS_SEQ)

            @block.tensor
            def _(pe):
                pe.wait_ge(consts_in, 16)
                pe.wait_ge(weights_in, 16 * N_WEIGHTS)
                pe.matmul(psA[0][0:64, 0:D], c64("wq0"), c64("wk0"), start=True, stop=True)
                qb = c32("qb1").rearrange("e (h i) -> e h i", h=H1)
                kw = c32("kb1").rearrange("e (h i) -> e h i", h=H1)
                for hh in range(H1):
                    pe.matmul(psA[1][0:65, D1 * hh:D1 * (hh + 1)], qb[:, hh, :], c32("p1"),
                              start=True, stop=True)
                for hh in range(H1):
                    pe.matmul(psA[2][0:65, D1 * hh:D1 * (hh + 1)], kw[:, hh, :], c32("p1"),
                              start=True, stop=True).then_inc(folded, 1)
                pe.wait_ge(b_scaled, 2)
                pe.transpose(psA[3][0:64, 0:64], b_sc[:, 0, :], cc("ident", 64)[:, 0:64])
                pe.transpose(psA[3][0:64, 64:128], b_sc[:, 1, :], cc("ident", 64)[:, 0:64]).then_inc(folded, 1)

            @block.scalar
            def _(act):
                act.dma_start(k128[:, :], w128).then_inc(weights_in, 16)
                act.dma_start(k32[:, :], w32).then_inc(weights_in, 16)
                act.dma_start(krow[:, :], wrow.broadcast_to([P, CROW["_"][1]])).then_inc(weights_in, 16)
                act.wait_ge(weights_in, 16 * N_WEIGHTS)
                act.activation(kb[:, :], kb_raw, ACT.Copy)
                act.wait_ge(folded, 2)
                act.activation(score0[:, :], psA[0][0:64, 0:D], ACT.Copy)
                act.activation(qkp1[:, 0:D], psA[1][0:65, 0:D], ACT.Copy, scale=float(D1) ** -0.5)
                act.activation(qkp1[:, D:], psA[2][0:65, 0:D], ACT.Copy)
                act.wait_ge(up_in, 64)
                for i in range(2):
                    act.activation(up_hi[:, up_cut[i]:up_cut[i + 1]], up_raw[i], ACT.Copy).then_inc(up_rounded, 1)
                act.wait_ge(angles, 2)
                act.activation(sines[:, :], ph[:, 5, :], ACT.Sin)
                act.activation(cosines[:, :], ph[:, 7, :], ACT.Sin)

            @block.vector
            def _(dve):
                count = [0]

                def then(ins):
                    count[0] += 1
                    ins.then_inc(v_chain, 1)
                    dve.wait_ge(v_chain, count[0])

                V = nc.vector
                V.memset(ids_sb[:, NSEQ:], 0)
                dve.wait_ge(ids_in, 16)
                then(V.tensor_copy(ids_f[:, :], ids_sb[:, 0:NSEQ]))
                V.tensor_scalar(keep[:, :], ids_f[:, :], 0.0, None, ALU.not_equal)
                def exponential(dst, src, n):
                    x, r, k, p = (ex[:, i, 0:n] for i in range(4))
                    then(V.tensor_scalar(x, src, -87.0, 88.0, ALU.max, ALU.min))
                    then(V.tensor_scalar(k, x, LOG2E, MAGIC, ALU.mult, ALU.add))
                    then(V.tensor_scalar(k, k, MAGIC, None, ALU.subtract))
                    then(V.scalar_tensor_tensor(r, k, -LN2_HI, x, ALU.mult, ALU.add))
                    then(V.scalar_tensor_tensor(r, k, -LN2_LO, r, ALU.mult, ALU.add))
                    then(V.tensor_scalar(p, r, 1.0 / 5040.0, 1.0 / 720.0, ALU.mult, ALU.add))
                    for c in (1.0 / 120.0, 1.0 / 24.0, 1.0 / 6.0, 0.5, 1.0, 1.0):
                        then(V.tensor_tensor(p, p, r, ALU.mult))
                        then(V.tensor_scalar(p, p, c, None, ALU.add))
                    then(V.tensor_scalar(ex_i[:, 0:n], k, 127.0, None, ALU.add))
                    then(V.tensor_scalar(ex_i[:, 0:n], ex_i[:, 0:n], 23, None, ALU.logical_shift_left))
                    then(V.tensor_tensor(dst, p, ex_i[:, 0:n].bitcast(F32), ALU.mult))

                dve.wait_ge(logs_in, 16)
                exponential(ex[:, 4, :], ln_logs[:, :], 3)
                then(V.tensor_scalar(th[:, 0:1], ex[:, 4, 0:1], -1.0, None, ALU.mult))
                then(V.tensor_copy(th[:, 1:2], ex[:, 4, 1:2]))
                exponential(th[:, 2:3], th[:, 0:1], 1)
                dve.wait_ge(consts_in, 16)
                later = cc("later")[:, None, :].broadcast_to([P, TILES, P])
                V.tensor_scalar(decay3[:, :].rearrange("p (t s) -> p t s", t=TILES), later,
                                th[:, 2:3], None, ALU.mult)
                then(V.tensor_scalar(th[:, 3:4], th[:, 1:2], 0.5 / PI, MAGIC, ALU.mult, ALU.add))
                then(V.tensor_scalar(th[:, 3:4], th[:, 3:4], MAGIC, None, ALU.subtract))
                for c in (TWO_PI_1, TWO_PI_2, TWO_PI_3):
                    then(V.scalar_tensor_tensor(th[:, 1:2], th[:, 3:4], -c, th[:, 1:2], ALU.mult, ALU.add))
                then(V.tensor_scalar(th[:, 4:5], th[:, 1:2], QUANT, None, ALU.add))
                then(V.tensor_scalar(th[:, 4:5], th[:, 4:5], QUANT, None, ALU.subtract))
                then(V.tensor_tensor(th[:, 5:6], th[:, 1:2], th[:, 4:5], ALU.subtract))
                then(V.tensor_scalar(ph[:, 0, :], cc("time"), th[:, 4:5], None, ALU.mult))
                then(V.tensor_scalar(ph[:, 1, :], ph[:, 0, :], 0.5 / PI, MAGIC, ALU.mult, ALU.add))
                then(V.tensor_scalar(ph[:, 1, :], ph[:, 1, :], MAGIC, None, ALU.subtract))
                then(V.tensor_scalar(ph[:, 2, :], cc("time"), th[:, 5:6], None, ALU.mult))
                for c in (TWO_PI_1, TWO_PI_2, TWO_PI_3):
                    then(V.scalar_tensor_tensor(ph[:, 0, :], ph[:, 1, :], -c, ph[:, 0, :], ALU.mult, ALU.add))
                then(V.tensor_tensor(ph[:, 3, :], ph[:, 0, :], ph[:, 2, :], ALU.add))
                V.tensor_scalar(ph[:, 5, :], ph[:, 3, :], -3.1415925, 3.1415925, ALU.max, ALU.min).then_inc(angles, 1)
                then(V.tensor_scalar(ph[:, 6, :], ph[:, 3, :], HALF_PI, None, ALU.add))
                then(V.tensor_scalar(ph[:, 4, :], ph[:, 6, :], PI, -2.0 * PI, ALU.is_gt, ALU.mult))
                then(V.tensor_tensor(ph[:, 6, :], ph[:, 6, :], ph[:, 4, :], ALU.add))
                V.tensor_scalar(ph[:, 7, :], ph[:, 6, :], -3.1415925, 3.1415925, ALU.max, ALU.min).then_inc(angles, 1)
                dve.wait_ge(weights_in, 16 * N_WEIGHTS)

                w3 = c128("w3")
                then(V.tensor_copy(w3_hi[:, :], w3))
                then(V.tensor_tensor(w3_r1[:, :], w3, w3_hi[:, :], ALU.subtract))
                then(V.tensor_copy(w3_mid[:, :], w3_r1[:, :]))
                then(V.tensor_tensor(w3_r2[:, :], w3_r1[:, :], w3_mid[:, :], ALU.subtract))
                V.tensor_copy(w3_lo[:, :], w3_r2[:, :]).then_inc(w3_split, 3)
                for part, name in enumerate(("b_re", "b_im")):
                    V.tensor_scalar(b_sc[:, part, :], c64(name), ex[0:64, 4, 2:3], None,
                                    ALU.mult).then_inc(b_scaled, 1)
                V.tensor_scalar(c_cos[:, :], c128("c_a"), cc("sign"), None, ALU.mult)
                V.tensor_scalar(c_sin[:, :], c128("c_b"), -1.0, None, ALU.mult)
                for i in range(2):
                    dve.wait_ge(up_rounded, i + 1)
                    cut = slice(up_cut[i], up_cut[i + 1])
                    V.tensor_tensor(up_lo[:, cut], up_raw[i], up_hi[:, cut].bitcast(F32), ALU.subtract)
                dve.wait_ge(folded, 3)
                for half in (slice(0, D), slice(D, P)):
                    V.tensor_copy(b_f[half, 0, :], psA[3][0:64, 0:P])
                    V.tensor_copy(b_f[half, 1, 0:D], psA[3][0:64, D:P])
                    V.tensor_scalar(b_f[half, 1, D:P], psA[3][0:64, 0:D], -1.0, None, ALU.mult).then_inc(b_rounded, 1)
                dve.wait_ge(b_rounded, 2)
                bf = b_f[:, :, :].rearrange("p a n -> p (a n)")
                V.tensor_copy(b_hi[:, :], bf).then_inc(b_rounded, 1)
                dve.wait_ge(b_rounded, 3)
                V.tensor_tensor(b_lo[:, :], bf, b_hi[:, :].bitcast(F32), ALU.subtract)

        first = sems[0].num
        nc.sync.sem_clear(range(first, sems[-1].num + 1))
        nc.all_engine_barrier()

        prefetched = [sem(f"prefetched_{g}") for g in range(GROUPS)]
        sems_setup = len(sems)

        def signal(name):
            return [sem(f"{name}_{g}") for g in range(GROUPS)]

        h_new = signal("h_new")
        y_part = signal("y_part")
        y_new = signal("y_new")
        norm_halves = signal("norm_halves")
        norm_var = signal("norm_var")
        norm_cen = signal("norm_cen")
        norm_out = signal("norm_out")
        scaled = signal("scaled")
        affined = signal("affined")
        x_turned = signal("x_turned")
        x_ready = signal("x_ready")
        xs_high = signal("xs_high")
        xs_ready = signal("xs_ready")
        logits = signal("logits")
        g_turned = signal("g_turned")
        gT_ready = signal("gT_ready")
        gTb_ready = signal("gTb_ready")
        norm_eps = signal("norm_eps")
        norm_rstd = signal("norm_rstd")
        ids_moved = signal("ids_moved")
        gating = signal("gating")
        gate_exp = signal("gate_exp")
        pe_step = signal("pe_step")
        act_step = signal("act_step")
        dve_step = signal("dve_step")
        pool_step = signal("pool_step")
        m0_z = signal("m0_z")
        m0_h = signal("m0_h")
        m0_o = signal("m0_o")
        m0_prod = signal("m0_prod")
        m0_acc = signal("m0_acc")
        m0_b = signal("m0_b")
        m1_z = signal("m1_z")
        m1_even = signal("m1_even")
        m1_odd = signal("m1_odd")
        m2_z = signal("m2_z")
        m2_h = signal("m2_h")
        m2_g = signal("m2_g")
        m2_hg = signal("m2_hg")
        m2_o = signal("m2_o")
        m2_res = signal("m2_res")
        m3_x = signal("m3_x")
        m3_z = signal("m3_z")
        m3_g = signal("m3_g")
        m3_w = signal("m3_w")
        m3_s = signal("m3_s")
        m3_p = signal("m3_p")
        m3_sum = signal("m3_sum")
        m3_y = signal("m3_y")
        m3_t = signal("m3_t")
        stored = sem("stored")

        (LN_A0, LN_M0, LN_IN0, LN_A1, LN_M1, LN_A2, LN_IN2, LN_OUT2, LN_M2, LN_A3, LN_M3) = range(11)
        (H_EMB, H_A0, H_M0, H_A1, H_M1, H_A2, H_M2, H_A3, H_OUT) = range(9)
        (X_A0, X_M0, X_A1, X_M1, X_A2, X_IN2, X_M2, X_A3, X_M3) = range(9)
        XT_A0, XT_A1, XT_A2, XT_IN2, XT_M3 = range(5)
        XS_M0, XS_M1, XS_M2, XS_A3 = range(4)
        G_M0, G_M1, G_M2 = range(3)
        Y_IN0, Y_IN2, Y_OUT2 = range(3)
        AFF_IN0, AFF_IN2, AFF_OUT2 = range(3)
        (PE_RV0, PE_S0, PE_O0, PE_QK1, PE_V1, PE_S1, PE_T1, PE_O1, PE_Q2, PE_KV2, PE_S2, PE_N2, PE_Z2, PE_Y2,
         PE_B3, PE_Y3) = range(16)
        AC_R0, AC_Q1, AC_EXP1, AC_T1, AC_Q2, AC_K2, AC_G2 = range(7)
        (DV_V0, DV_P0, DV_K1, DV_V1, DV_BLOCK1, DV_FOLD1, DV_MAX1, DV_SUB1, DV_SUM1, DV_REC1, DV_W1,
         DV_KV2, DV_Q2, DV_S2, DV_DEN2, DV_REC2, DV_O2, DV_TURN3, DV_SCAN3) = range(19)
        PL_W1, PL_SCALED3, PL_RES3, PL_SUM3, PL_TURN3 = range(5)
        TOP2_DIFF, TOP2_STEPS, TOP1_STEPS, SPLIT_STEPS = 12, 19, 6, 4
        GATING_AT = {G_M0: 0, G_M1: TOP2_STEPS, G_M2: TOP2_STEPS + TOP1_STEPS}
        GATING_END = {G_M0: TOP2_STEPS, G_M1: TOP2_STEPS + TOP1_STEPS,
                      G_M2: 2 * TOP2_STEPS + TOP1_STEPS + SPLIT_STEPS}

        (AT_A0, AT_M0, AT_IN0, AT_A1, AT_M1, AT_A2, AT_IN2, AT_OUT2, AT_M2, AT_A3, AT_M3, AT_OUT) = (
            2, 20, 95, 105, 144, 181, 203, 219, 227, 272, 300, 368)
        MEAN, RSTD, CENTRE, OUT, TURN, COPY, LOW, ROUTE, GATES = 1, 1.5, 1.5, 4, 5, 6, 7, 7, 8
        GATES_TURN, GATES_COPY = 16.5, 17.5
        GATING_STEP = 0.4
        M0_STEP, M1_STEP, M2_STEP, M3_STEP = 3, 3, 4.5, 1.6
        LATER = 0.6

        def issue(g, place):
            i = max(1, min(sum(p <= place for p in PLACES), len(PLACES) - 1))
            (p, q), (a, b) = PLACES[i - 1:i + 1], ISSUE[g][i - 1:i + 1]
            return a + (place - p) * (b - a) / (q - p)

        def in_order(programs):
            due = {g: issue(g, next(program)) for g, program in enumerate(programs)}
            while due:
                g = min(due, key=lambda i: (due[i], i))
                place = next(programs[g], None)
                if place is None:
                    del due[g]
                else:
                    due[g] = issue(g, place)

        def lanes_of(g):
            return range(GROUP_LANES * g, GROUP_LANES * (g + 1))

        def part(ap, l):
            i = l % GROUP_LANES
            return ap[:, TILES * i:TILES * (i + 1)]

        def rows(ap):
            return ap[:, 0:TILES * D].rearrange("p (t d) -> p t d", t=TILES)

        def tile(ap, t):
            return ap[:, P * t:P * (t + 1)]

        def prod(l, q):
            return (big_a, big_b)[q % 2][l][:, :]

        def spread(ap, n):
            return ap[:, :, None].broadcast_to([P, ap.shape[1], n])

        with nc.Fori(0, PASSES) as it:
            with nc.Block() as block:

                @block.sync
                def _(sp):
                    for g in range(GROUPS):
                        for l in lanes_of(g):
                            sp.wait_ge(h_new[g], nth(l, H_OUT))
                            sp.dma_start(out[it, l].rearrange("t p d -> p t d"), h[l][:, :, :]).then_inc(stored, 16)
                    sp.wait_ge(stored, 16 * LANES)

                @block.gpsimd
                def _(pool):
                    G = nc.gpsimd

                    def program(g):
                        own = lanes_of(g)

                        def rstd(at, use):
                            for l in own:
                                yield at + RSTD + LATER * (l - own[0])
                                pool.wait_ge(norm_var[g], nth(l, use))
                                G.tensor_scalar(part(var_eps[g], l), part(stat[g], l)[:, :, 1], LN_EPS, None,
                                                ALU.add).then_inc(norm_eps[g], 1)
                                pool.wait_ge(norm_eps[g], nth(l, use))
                                G.tensor_tensor(part(inv_std[g], l), part(var_eps[g], l), neg_half[:, :],
                                                ALU.pow).then_inc(norm_rstd[g], 1)

                        def affine(at, ln, use, gamma, beta):
                            for l in own:
                                yield at + OUT + 1 + LATER * (l - own[0])
                                pool.wait_ge(norm_out[g], nth(l, ln))
                                G.tensor_tensor(aff[l][:, :, :], xn[l][:, :, :], crow(gamma), ALU.mult).then_inc(scaled[g], 1)
                            for l in own:
                                pool.wait_ge(scaled[g], nth(l, use))
                                G.tensor_tensor(aff[l][:, :, :], aff[l][:, :, :], crow(beta), ALU.add).then_inc(affined[g], 1)

                        yield from rstd(AT_A0, LN_A0)
                        yield from rstd(AT_M0, LN_M0)
                        for q in range(1, E0 // 2):
                            for l in own:
                                yield AT_M0 + GATES_COPY + M0_STEP * (2 * q + 3) + 4 + LATER * (l - own[0])
                                pool.wait_ge(m0_prod[g], nth(l, q))
                                if q == 1:
                                    G.tensor_tensor(big_c[l][:, :], prod(l, 0), prod(l, 1), ALU.add).then_inc(m0_acc[g], 1)
                                else:
                                    pool.wait_ge(m0_acc[g], nth(l, q - 2))
                                    G.tensor_tensor(big_c[l][:, :], prod(l, q), big_c[l][:, :], ALU.add).then_inc(m0_acc[g], 1)
                        yield from rstd(AT_IN0, LN_IN0)
                        yield from affine(AT_IN0, LN_IN0, AFF_IN0, "g0", "be0")
                        yield from rstd(AT_A1, LN_A1)
                        block1 = cc("block").rearrange("p (g j) -> p g j", j=BS1)[:, None, :, :].broadcast_to(
                            [P, TILES, P // BS1, BS1])
                        for l in own:
                            yield AT_A1 + 27 + LATER * (l - own[0])
                            pool.wait_ge(dve_step[g], nth(l, DV_W1))
                            for hh, dst in enumerate((big_a, big_b)):
                                at = TILES * (H1 * (l % GROUP_LANES) + hh)
                                w = s8[g][:, at:at + TILES, None, :].broadcast_to([P, TILES, P // BS1, BS1])
                                last = G.tensor_tensor(dst[l][:, :].rearrange("p (t g j) -> p t g j", t=TILES, j=BS1),
                                                       w, block1, ALU.mult)
                            last.then_inc(pool_step[g], 1)
                        yield from rstd(AT_M1, LN_M1)
                        yield from rstd(AT_A2, LN_A2)
                        yield from rstd(AT_IN2, LN_IN2)
                        yield from affine(AT_IN2, LN_IN2, AFF_IN2, "g2a", "be2a")
                        yield from rstd(AT_OUT2, LN_OUT2)
                        yield from affine(AT_OUT2, LN_OUT2, AFF_OUT2, "g2b", "be2b")
                        yield from rstd(AT_M2, LN_M2)
                        for l in own:
                            yield AT_M2 + TURN + LATER * (l - own[0])
                            pool.wait_ge(norm_out[g], nth(l, LN_M2))
                            G.tensor_tensor(y[l][:, :, :], h[l][:, :, :], xn[l][:, :, :], ALU.add).then_inc(m2_res[g], 1)
                        yield from rstd(AT_A3, LN_A3)
                        for l in own:
                            yield AT_A3 + OUT + 1 + LATER * (l - own[0])
                            pool.wait_ge(norm_out[g], nth(l, LN_A3))
                            G.tensor_tensor(y[l][:, :, :], xn[l][:, :, :], crow("d3"), ALU.mult).then_inc(pool_step[g], 1)
                        for l in own:
                            yield AT_A3 + OUT + 2 + LATER * (l - own[0])
                            pool.wait_ge(pool_step[g], nth(l, PL_SCALED3))
                            G.tensor_tensor(y[l][:, :, :], y[l][:, :, :], h[l][:, :, :], ALU.add).then_inc(pool_step[g], 1)
                        for l in own:
                            yield AT_A3 + 14 + LATER * (l - own[0])
                            pool.wait_ge(dve_step[g], nth(l, DV_TURN3))
                            G.tensor_tensor(big_c[l][:, :], big_a[l][:, :], big_b[l][:, :], ALU.add).then_inc(pool_step[g], 1)
                        for l in own:
                            yield AT_A3 + 18 + LATER * (l - own[0])
                            pool.wait_ge(dve_step[g], nth(l, DV_SCAN3))
                            for wave, dst in ((cosines, big_a), (sines, big_b)):
                                last = G.tensor_tensor(dst[l][:, :].rearrange("p (t s) -> p t s", t=TILES),
                                                       hid[l][:, 0, :].rearrange("p (t s) -> p t s", t=TILES),
                                                       wave[:, None, :].broadcast_to([P, TILES, P]), ALU.mult)
                            last.then_inc(pool_step[g], 1)
                        yield from rstd(AT_M3, LN_M3)
                        yield AT_M3 + 10
                        pool.wait_ge(h_new[g], nth(own[-1], H_EMB))
                        ahead = it * PASS_SEQ + (PASS_SEQ + GROUP_TILES * g)
                        G.tensor_copy(ids_next[g][:, :], ids_sb[:, bass.ds(ahead, GROUP_TILES)]).then_inc(ids_moved[g], 1)
                        pool.wait_ge(ids_moved[g], 1)
                        for i in range(GROUP_TILES):
                            yield AT_M3 + 12 + 4 * i
                            G.indirect_dma_start(
                                emb[:, GROUP_TILES * g + i, :], None, emb_w,
                                bass.IndirectOffsetOnAxis(ap=ids_next[g][:, i:i + 1].bitcast(U32), axis=0)
                            ).then_inc(prefetched[g], 16)
                        yield AT_OUT
                        pool.wait_ge(prefetched[g], it * (16 * GROUP_TILES) + 16 * GROUP_TILES)

                    in_order([program(g) for g in range(GROUPS)])

                @block.scalar
                def _(act):
                    def program(g):
                        own = lanes_of(g)

                        def turned(at, use):
                            for l in own:
                                yield at + COPY + LATER * (l - own[0])
                                act.wait_ge(x_turned[g], nth(l, use))
                                act.activation(xT[l][0:64, :], psA[l][0:64, :], ACT.Copy).then_inc(x_ready[g], 1)

                        def turned_parts(at, use):
                            for l in own:
                                yield at + COPY + LATER * (l - own[0])
                                act.wait_ge(x_turned[g], nth(l, use))
                                act.activation(xs[l][0:64, :], psA[l][0:64, :], ACT.Copy).then_inc(xs_high[g], 1)

                        def exp_of_difference(at, use, turn):
                            yield at + GATES + GATING_STEP * (TOP2_DIFF + 1)
                            act.wait_ge(gating[g], GATING_AT[use] + TOP2_DIFF + 1)
                            act.activation(gs[g][:, 4, :], gs[g][:, 3, :], ACT.Exp).then_inc(gate_exp[g], 1)

                        def gates_turned(at, use, E):
                            for l in own:
                                yield at + GATES_COPY + LATER * (l - own[0])
                                act.wait_ge(g_turned[g], nth(l, use))
                                act.activation(gT[l][0:E, :], psA[l][0:E, :], ACT.Copy).then_inc(gT_ready[g], 1)

                        yield from turned(AT_A0, X_A0)
                        for l in own:
                            yield AT_A0 + 9 + LATER * (l - own[0])
                            act.wait_ge(pe_step[g], nth(l, PE_RV0))
                            act.activation(fm[l][0:64, :], psB[l][0:64, :], ACT.Copy).then_inc(act_step[g], 1)
                        yield from turned_parts(AT_M0, X_M0)
                        yield from exp_of_difference(AT_M0, G_M0, 0)
                        yield from gates_turned(AT_M0, G_M0, E0)
                        for e in range(E0):
                            for l in own:
                                yield AT_M0 + GATES_COPY + M0_STEP * (e + 1) + LATER * (l - own[0])
                                act.wait_ge(m0_z[g], nth(l, e))
                                if e >= 4:
                                    act.wait_ge(m0_o[g], nth(l, e // 2 - 2))
                                act.activation(hid[l][:, e % 4, :], psA[l][:, :], ACT.Relu,
                                               bias=c128("b1_0")[:, e:e + 1]).then_inc(m0_h[g], 1)
                        yield from turned(AT_A1, X_A1)
                        for l in own:
                            yield AT_A1 + 9 + LATER * (l - own[0])
                            act.wait_ge(pe_step[g], nth(l, PE_QK1))
                            act.activation(fm[l][0:64, :], psA[l][0:64, :], ACT.Copy).then_inc(act_step[g], 1)
                        yield AT_A1 + 24
                        act.wait_ge(dve_step[g], nth(own[-1], DV_SUB1))
                        act.activation(s8b[g][:, :, :], s8b[g][:, :, :], ACT.Exp).then_inc(act_step[g], GROUP_LANES)
                        for l in own:
                            yield AT_A1 + 33 + LATER * (l - own[0])
                            act.wait_ge(pe_step[g], nth(l, PE_T1))
                            act.activation(hid[l][:, 0, :], psA[l][:, :], ACT.Copy)
                            act.activation(hid[l][:, 1, :], psB[l][:, :], ACT.Copy).then_inc(act_step[g], 1)
                        yield from turned_parts(AT_M1, X_M1)
                        for l in own:
                            yield AT_M1 + 14 + LATER * (l - own[0])
                            act.wait_ge(g_turned[g], nth(l, G_M1))
                            act.activation(gT[l][0:E1, :], psA[l][0:E1, :], ACT.Copy).then_inc(gT_ready[g], 1)
                        for m in range(0, MT, 2):
                            for l in own:
                                yield AT_M1 + 18 + M1_STEP * m + LATER * (l - own[0])
                                act.wait_ge(m1_z[g], nth(l, m))
                                act.activation(hid[l][:, m, :], psA[l][:, :], ACT.Relu,
                                               bias=c128("b1_1")[:, m:m + 1]).then_inc(m1_even[g], 1)
                        yield from turned(AT_A2, X_A2)
                        for l in own:
                            yield AT_A2 + 9 + LATER * (l - own[0])
                            act.wait_ge(pe_step[g], nth(l, PE_Q2))
                            act.activation(fm2[l][0:64, :], psB[l][0:64, :], ACT.Exp)
                            act.activation(big_a[l][0:64, :], psB[l][0:64, :], ACT.Relu).then_inc(act_step[g], 1)
                        for l in own:
                            yield AT_A2 + 11 + LATER * (l - own[0])
                            act.wait_ge(pe_step[g], nth(l, PE_KV2))
                            kv = psA[l][:, :].rearrange("p (t c) -> p t c", t=TILES)
                            act.activation(kf[l][:, 0, :, :], kv[:, :, 0:D], ACT.Exp)
                            act.activation(kf[l][:, 1, :, :], kv[:, :, 0:D], ACT.Relu).then_inc(act_step[g], 1)
                        for l in own:
                            yield AT_IN2 + 8 + LATER * (l - own[0])
                            act.wait_ge(x_turned[g], nth(l, X_IN2))
                            act.activation(xT[l][0:64, :], psA[l][0:64, :], ACT.Copy).then_inc(x_ready[g], 1)
                        for l in own:
                            yield AT_IN2 + 11 + LATER * (l - own[0])
                            act.wait_ge(pe_step[g], nth(l, PE_Z2))
                            act.activation(fm[l][0:64, :], psB[l][0:64, :], ACT.Gelu, bias=c64("b1_2a")).then_inc(act_step[g], 1)
                        yield from turned_parts(AT_M2, X_M2)
                        yield from exp_of_difference(AT_M2, G_M2, 1)
                        for l in own:
                            yield AT_M2 + GATES_COPY + 1 + LATER * (l - own[0])
                            act.wait_ge(g_turned[g], nth(l, G_M2))
                            act.activation(gT[l][0:E2, :], psA[l][0:E2, :], ACT.Copy)
                            act.activation(gTb[l][0:SPLIT * E2, :], psA[l][0:SPLIT * E2, :], ACT.Copy).then_inc(gT_ready[g], 1)
                        for m in range(MT):
                            for l in own:
                                yield AT_M2 + 22.5 + M2_STEP * m + LATER * (l - own[0])
                                act.wait_ge(m2_z[g], nth(l, m))
                                act.activation(hid[l][:, m, :], psA[l][:, :], ACT.Gelu,
                                               bias=c128("b1_2")[:, m:m + 1]).then_inc(m2_h[g], 1)
                        yield from turned_parts(AT_A3, X_A3)
                        for l in own:
                            yield AT_M3 + COPY + LATER * (l - own[0])
                            act.wait_ge(x_turned[g], nth(l, X_M3))
                            act.activation(xT[l][0:64, :], psA[l][0:64, :], ACT.Copy).then_inc(x_ready[g], 1)
                            act.activation(sx[l][0:64, :], psA[l][0:64, :], ACT.Sign)
                            act.activation(sx[l][64:128, :], psA[l][0:64, :], ACT.Sign).then_inc(m3_x[g], 1)
                        for p in range(PAIRS):
                            for l in own:
                                yield AT_M3 + 11 + M3_STEP * p + LATER * (l - own[0])
                                act.wait_ge(m3_w[g], nth(l, p))
                                if p >= 2:
                                    act.wait_ge(m3_p[g], nth(l, p - 2))
                                act.activation(sg[l][:, p % 2, :], psA[l][:, :], ACT.Sign).then_inc(m3_s[g], 1)

                    in_order([program(g) for g in range(GROUPS)])

                @block.tensor
                def _(pe):
                    def program(g):
                        own = lanes_of(g)

                        def turn(at, src, ready, value):
                            for l in own:
                                yield at + LATER * (l - own[0])
                                pe.wait_ge(ready, value(l))
                                for t in range(TILES):
                                    last = pe.transpose(psA[l][0:64, P * t:P * (t + 1)], src[l][:, t, :], ident)
                                last.then_inc(x_turned[g], 1)

                        def turn_norm(at, ln):
                            yield from turn(at + TURN, xn, norm_out[g], lambda l: nth(l, ln))

                        def up(out, name, col, l):
                            a = CUP[name][0] + P * col
                            pe.matmul(out, up_hi[:, a:a + P], xs[l][:, :], start=True, stop=False)
                            return pe.matmul(out, up_lo[:, a:a + P], xs[l][:, :], start=False, stop=(name != "w1_1"))

                        def route(at, use, name, E):
                            for l in own:
                                yield at + ROUTE + LATER * (l - own[0])
                                pe.wait_ge(xs_ready[g], nth(l, use))
                                a = CUP[name][0]
                                for t in range(TILES):
                                    o = psB[l][:, E * t:E * (t + 1)]
                                    pe.matmul(o, tile(xs[l], t), up_hi[:, a:a + E], start=True, stop=False)
                                    last = pe.matmul(o, tile(xs[l], t), up_lo[:, a:a + E], start=False, stop=True)
                                last.then_inc(logits[g], 1)

                        def turn_gates(at, use, src, E):
                            yield at
                            pe.wait_ge(gating[g], GATING_END[use])
                            for l in own:
                                for t in range(TILES):
                                    last = pe.transpose(psA[l][0:E, P * t:P * (t + 1)], part(src[g], l)[:, t, 0:E], ident)
                                last.then_inc(g_turned[g], 1)

                        yield from turn_norm(AT_A0, LN_A0)
                        for l in own:
                            yield AT_A0 + 7 + LATER * (l - own[0])
                            pe.wait_ge(x_ready[g], nth(l, XT_A0))
                            pe.matmul(psB[l][0:64, :], score0[:, :], xT[l][0:64, :], start=True, stop=True)
                            for t in range(TILES):
                                last = pe.matmul(psA[l][:, D * t:D * (t + 1)], tile(xT[l][0:64, :], t), c64("wv0"),
                                                 start=True, stop=True)
                            last.then_inc(pe_step[g], 1)
                        for l in own:
                            yield AT_A0 + 11 + LATER * (l - own[0])
                            pe.wait_ge(act_step[g], nth(l, AC_R0))
                            for t in range(TILES):
                                last = pe.matmul(tile(psB[l], t), tile(xT[l][0:64, :], t), tile(fm[l][0:64, :], t),
                                                 start=True, stop=True)
                            last.then_inc(pe_step[g], 1)
                        for l in own:
                            yield AT_A0 + 15 + LATER * (l - own[0])
                            pe.wait_ge(dve_step[g], nth(l, DV_P0))
                            for t in range(TILES):
                                last = pe.matmul(psA[l][:, D * t:D * (t + 1)], tile(big_a[l], t), v_sb[l][:, t, 0:D],
                                                 start=True, stop=True)
                            last.then_inc(pe_step[g], 1)

                        yield from turn_norm(AT_M0, LN_M0)
                        yield from route(AT_M0, XS_M0, "route0", E0)
                        yield from turn_gates(AT_M0 + GATES_TURN, G_M0, gate, E0)

                        def up0(at, e):
                            for l in own:
                                yield at + LATER * (l - own[0])
                                if e == 0:
                                    pe.wait_ge(gT_ready[g], nth(l, G_M0))
                                    pe.wait_ge(xs_ready[g], nth(l, XS_M0))
                                else:
                                    pe.wait_ge(m0_h[g], nth(l, e - 1))
                                up(psA[l][:, :], "w1_0", e, l).then_inc(m0_z[g], 1)

                        def down0(at, q):
                            for l in own:
                                yield at + LATER * (l - own[0])
                                pe.wait_ge(m0_h[g], nth(l, 2 * q + 1))
                                if q:
                                    pe.wait_ge(m0_prod[g], nth(l, q - 1))
                                for e in (2 * q, 2 * q + 1):
                                    a = C128["w2_0"][0] + D * e
                                    for t in range(TILES):
                                        to = 256 * (e % 2) + D * t
                                        last = pe.matmul(psB[l][:, to:to + D], tile(hid[l][:, e % 4, :], t),
                                                         k128[:, a:a + D], start=True, stop=True)
                                last.then_inc(m0_o[g], 1)

                        for e in range(E0 + 2):
                            at = AT_M0 + GATES_COPY + M0_STEP * e
                            if e < E0:
                                yield from up0(at + 1, e)
                            if e >= 3 and e % 2:
                                yield from down0(at + 2, (e - 3) // 2)
                        for l in own:
                            for t in range(TILES):
                                last = pe.matmul(psA[l][:, D * t:D * (t + 1)], tile(gT[l][0:E0, :], t),
                                                 c32("b2_0", E0), start=True, stop=True)
                            last.then_inc(m0_b[g], 1)

                        yield from turn_norm(AT_A1, LN_A1)
                        for l in own:
                            yield AT_A1 + 7 + LATER * (l - own[0])
                            pe.wait_ge(x_ready[g], nth(l, XT_A1))
                            pe.matmul(psA[l][:, :], qkp1[:, :], xT[l][:, :], start=True, stop=True).then_inc(pe_step[g], 1)
                        for l in own:
                            yield AT_A1 + 8 + LATER * (l - own[0])
                            for t in range(TILES):
                                last = pe.matmul(psB[l][:, D * t:D * (t + 1)], tile(xT[l], t), c65("wv1"),
                                                 start=True, stop=True)
                            last.then_inc(pe_step[g], 1)
                        for l in own:
                            yield AT_A1 + 13 + LATER * (l - own[0])
                            pe.wait_ge(act_step[g], nth(l, AC_Q1))
                            pe.wait_ge(dve_step[g], nth(l, DV_V1))
                            for hh, ps in enumerate((psA, psB)):
                                r = slice(D1 * hh, D1 * (hh + 1))
                                for t in range(TILES):
                                    last = pe.matmul(tile(ps[l], t), tile(fm[l][r, :], t), tile(fm2[l][r, :], t),
                                                     start=True, stop=True)
                            last.then_inc(pe_step[g], 1)
                        for l in own:
                            yield AT_A1 + 30 + LATER * (l - own[0])
                            pe.wait_ge(pool_step[g], nth(l, PL_W1))
                            for ps, src in ((psA, big_a), (psB, big_b)):
                                for t in range(TILES):
                                    last = pe.transpose(tile(ps[l], t), tile(src[l], t), ident)
                            last.then_inc(pe_step[g], 1)
                        for l in own:
                            yield AT_A1 + 35 + LATER * (l - own[0])
                            pe.wait_ge(act_step[g], nth(l, AC_T1))
                            for t in range(TILES):
                                for hh in range(H1):
                                    c = D1 * hh
                                    last = pe.matmul(psA[l][:, D * t + c:D * t + c + D1], tile(hid[l][:, hh, :], t),
                                                     v_sb[l][:, t, c:c + D1], start=True, stop=True)
                            last.then_inc(pe_step[g], 1)

                        yield from turn_norm(AT_M1, LN_M1)
                        yield from route(AT_M1, XS_M1, "route1", E1)
                        yield from turn_gates(AT_M1 + 13, G_M1, oh1, E1)
                        for m in range(MT):
                            for l in own:
                                yield AT_M1 + 16 + M1_STEP * m + LATER * (l - own[0])
                                ps = (psA, psB)[m % 2]
                                if m == 0:
                                    pe.wait_ge(gTb_ready[g], nth(l))
                                    pe.wait_ge(gT_ready[g], nth(l, G_M1))
                                    pe.wait_ge(xs_ready[g], nth(l, XS_M1))
                                if m >= 2:
                                    pe.wait_ge((m1_even, m1_odd)[m % 2][g], nth(l, 0))
                                up(ps[l][:, :], "w1_1", m, l)
                                pe.matmul(ps[l][:, :], sel1[:, P * m:P * (m + 1)], gTb[l][0:E1, :],
                                          start=False, stop=True).then_inc(m1_z[g], 1)
                        for l in own:
                            yield AT_M1 + 18 + M1_STEP * MT + LATER * (l - own[0])
                            pe.wait_ge(m1_even[g], nth(l, 1))
                            pe.wait_ge(m1_odd[g], nth(l, 1))
                            for t in range(TILES):
                                o = psA[l][:, D * t:D * (t + 1)]
                                for m in range(MT):
                                    a = C128["w2_1"][0] + D * m
                                    pe.matmul(o, tile(hid[l][:, m, :], t), k128[:, a:a + D], start=(m == 0), stop=False)
                                last = pe.matmul(o, tile(gT[l][:, :], t), c32("b2_1"), start=False, stop=True)
                            last.then_inc(m1_z[g], 1)

                        yield from turn_norm(AT_A2, LN_A2)
                        for l in own:
                            yield AT_A2 + 7 + LATER * (l - own[0])
                            pe.wait_ge(x_ready[g], nth(l, XT_A2))
                            pe.matmul(psB[l][0:64, :], c64("q2"), xT[l][0:64, :], start=True, stop=True).then_inc(pe_step[g], 1)
                        for l in own:
                            yield AT_A2 + 8 + LATER * (l - own[0])
                            for t in range(TILES):
                                last = pe.matmul(tile(psA[l], t), tile(xT[l][0:64, :], t), c64("kv2"), start=True, stop=True)
                            last.then_inc(pe_step[g], 1)
                        for l in own:
                            yield AT_A2 + 14 + LATER * (l - own[0])
                            pe.wait_ge(act_step[g], nth(l, AC_Q2))
                            pe.wait_ge(dve_step[g], nth(l, DV_KV2))
                            for t in range(TILES):
                                last = pe.matmul(psB[l][0:64, KV2 * t:KV2 * (t + 1)], kf[l][:, 0, t, :], v_sb[l][:, t, :],
                                                 start=True, stop=True)
                            last.then_inc(pe_step[g], 1)
                        for l in own:
                            yield AT_A2 + 17 + LATER * (l - own[0])
                            pe.wait_ge(dve_step[g], nth(l, DV_S2))
                            for t in range(TILES):
                                last = pe.matmul(psA[l][:, KV2 * t:KV2 * (t + 1)], tile(fm2[l][0:64, :], t), kvm[l][:, t, :],
                                                 start=True, stop=True)
                            last.then_inc(pe_step[g], 1)
                        yield from turn(AT_IN2 + 7, aff, affined[g], lambda l: nth(l, AFF_IN2))
                        for l in own:
                            yield AT_IN2 + 9 + LATER * (l - own[0])
                            pe.wait_ge(x_ready[g], nth(l, XT_IN2))
                            pe.matmul(psB[l][0:64, :], c64("w1_2a"), xT[l][0:64, :], start=True, stop=True).then_inc(pe_step[g], 1)
                        for l in own:
                            yield AT_IN2 + 13 + LATER * (l - own[0])
                            pe.wait_ge(act_step[g], nth(l, AC_G2))
                            for t in range(TILES):
                                last = pe.matmul(psA[l][:, D * t:D * (t + 1)], tile(fm[l], t), c65("w2_2a"),
                                                 start=True, stop=True)
                            last.then_inc(pe_step[g], 1)

                        yield from turn_norm(AT_M2, LN_M2)
                        yield from route(AT_M2, XS_M2, "route2", E2)
                        yield from turn_gates(AT_M2 + GATES_COPY, G_M2, g3, G3)
                        for m in range(MT):
                            for l in own:
                                yield AT_M2 + 20.5 + M2_STEP * m + LATER * (l - own[0])
                                if m == 0:
                                    pe.wait_ge(gT_ready[g], nth(l, G_M2))
                                    pe.wait_ge(xs_ready[g], nth(l, XS_M2))
                                else:
                                    pe.wait_ge(m2_h[g], nth(l, m - 1))
                                up(psA[l][:, :], "w1_2", m, l).then_inc(m2_z[g], 1)
                                if m:
                                    pe.wait_ge(m2_hg[g], nth(l, m - 1))
                                pe.matmul(psB[l][:, :], sel2[:, P * m:P * (m + 1)], gTb[l][0:SPLIT * E2, :],
                                          start=True, stop=True).then_inc(m2_g[g], 1)
                        for l in own:
                            yield AT_M2 + 22.5 + M2_STEP * MT + LATER * (l - own[0])
                            pe.wait_ge(m2_hg[g], nth(l, MT - 1))
                            for t in range(TILES):
                                o = psA[l][:, D * t:D * (t + 1)]
                                for m in range(MT):
                                    a = C128["w2_2"][0] + D * m
                                    pe.matmul(o, tile(hid[l][:, m, :], t), k128[:, a:a + D], start=(m == 0), stop=False)
                                last = pe.matmul(o, tile(gT[l][0:E2, :], t), c32("b2_2", E2), start=False, stop=True)
                            last.then_inc(m2_o[g], 1)

                        yield from turn_norm(AT_A3, LN_A3)
                        for l in own:
                            yield AT_A3 + 8 + LATER * (l - own[0])
                            pe.wait_ge(xs_ready[g], nth(l, XS_A3))
                            for i, ps in enumerate((psA, psB)):
                                pe.matmul(ps[l][:, :], b_hi[:, P * i:P * (i + 1)], xs[l][:, :], start=True, stop=False)
                                last = pe.matmul(ps[l][:, :], b_lo[:, P * i:P * (i + 1)], xs[l][:, :],
                                                 start=False, stop=True)
                            last.then_inc(pe_step[g], 1)
                        for l in own:
                            yield AT_A3 + 24 + LATER * (l - own[0])
                            pe.wait_ge(pool_step[g], nth(l, PL_TURN3))
                            for t in range(TILES):
                                o = psA[l][:, D * t:D * (t + 1)]
                                pe.matmul(o, tile(big_a[l], t), c_cos[:, :], start=True, stop=False)
                                last = pe.matmul(o, tile(big_b[l], t), c_sin[:, :], start=False, stop=True)
                            last.then_inc(pe_step[g], 1)

                        yield from turn_norm(AT_M3, LN_M3)
                        for l in own:
                            yield AT_M3 + 7 + LATER * (l - own[0])
                            pe.wait_ge(x_ready[g], nth(l, XT_M3))
                            pe.matmul(psB[l][0:G3, :], c65("proj3"), xT[l][:, :], start=True, stop=True).then_inc(m3_z[g], 1)

                        def weights3(at, p):
                            for l in own:
                                yield at + LATER * (l - own[0])
                                if p == 0:
                                    pe.wait_ge(m3_g[g], nth(l))
                                    pe.wait_ge(m3_x[g], nth(l))
                                else:
                                    pe.wait_ge(m3_s[g], nth(l, p - 1))
                                pe.matmul(psA[l][:, :], w3_rows[:, P * p:P * (p + 1)], gTb[l][:, :],
                                          start=True, stop=True).then_inc(m3_w[g], 1)

                        def gather3(at, p):
                            for l in own:
                                yield at + LATER * (l - own[0])
                                pe.wait_ge(m3_p[g], nth(l, p))
                                a = D - 2 * p
                                pe.matmul(psB[l][:, :], pick3[:, a:a + P], pr[l][:, p % 2, :],
                                          start=(p == 0), stop=(p == PAIRS - 1)).then_inc(m3_sum[g], 1)

                        for p in range(PAIRS + 1):
                            at = AT_M3 + 10 + M3_STEP * p
                            if p < PAIRS:
                                yield from weights3(at, p)
                            if p:
                                yield from gather3(at, p - 1)
                        for l in own:
                            yield AT_OUT - 2 + LATER * (l - own[0])
                            pe.wait_ge(m3_y[g], nth(l))
                            for t in range(TILES):
                                last = pe.transpose(psA[l][:, D * t:D * (t + 1)], tile(fm2[l][0:64, :], t),
                                                    cc("ident", 64)[:, 0:64])
                            last.then_inc(m3_t[g], 1)

                    in_order([program(g) for g in range(GROUPS)])

                @block.vector
                def _(dve):
                    V = nc.vector

                    def program(g):
                        own = lanes_of(g)

                        def norm(at, use, src, ready, value):
                            for l in own:
                                yield at + LATER * (l - own[0])
                                dve.wait_ge(ready, value(l))
                                for t in range(TILES):
                                    last = V.bn_stats(part(halves_stat[g], l)[:, t, :], src[l][:, t, :])
                                last.then_inc(norm_halves[g], 1)
                            for l in own:
                                yield at + MEAN + LATER * (l - own[0])
                                dve.wait_ge(norm_halves[g], nth(l, use))
                                for t in range(TILES):
                                    last = V.bn_aggr(part(stat[g], l)[:, t, :], part(halves_stat[g], l)[:, t, :])
                                last.then_inc(norm_var[g], 1)
                            for l in own:
                                yield at + CENTRE + LATER * (l - own[0])
                                dve.wait_ge(norm_var[g], nth(l, use))
                                V.tensor_tensor(xn[l][:, :, :], src[l][:, :, :], spread(part(stat[g], l)[:, :, 0], D),
                                                ALU.subtract).then_inc(norm_cen[g], 1)
                            for l in own:
                                yield at + OUT + LATER * (l - own[0])
                                dve.wait_ge(norm_cen[g], nth(l, use))
                                dve.wait_ge(norm_rstd[g], nth(l, use))
                                V.tensor_tensor(xn[l][:, :, :], xn[l][:, :, :], spread(part(inv_std[g], l), D),
                                                ALU.mult).then_inc(norm_out[g], 1)

                        def norm_h(at, use, h_use):
                            yield from norm(at, use, h, h_new[g], lambda l: nth(l, h_use))

                        def norm_y(at, use, y_use):
                            yield from norm(at, use, y, y_new[g], lambda l: nth(l, y_use))

                        def low_parts(at, use):
                            for l in own:
                                yield at + LOW + LATER * (l - own[0])
                                dve.wait_ge(xs_high[g], nth(l, use))
                                V.tensor_tensor(xs[l][D:P, :], psA[l][0:D, :], xs[l][0:D, :].bitcast(F32),
                                                ALU.subtract).then_inc(xs_ready[g], 1)

                        gating_count = [0]

                        def gating_step(at, emit):
                            yield at
                            dve.wait_ge(gating[g], gating_count[0])
                            emit().then_inc(gating[g], 1)
                            gating_count[0] += 1

                        def first_of(at, E, scores, peak, onehot):
                            s, eq, r, o = (b[g][:, :, 0:E] for b in (scores, ge, gk, onehot))
                            top, first = gs[g][:, peak, :], gs[g][:, 2, :]
                            yield from gating_step(at, lambda: V.tensor_reduce(top, s, X, ALU.max))
                            yield from gating_step(at + GATING_STEP, lambda: V.tensor_tensor(eq, s, spread(top, E), ALU.is_equal))
                            yield from gating_step(at + 2 * GATING_STEP, lambda: V.tensor_tensor(r, eq, rank(E), ALU.mult))
                            yield from gating_step(at + 3 * GATING_STEP, lambda: V.tensor_reduce(first, r, X, ALU.max))
                            yield from gating_step(at + 4 * GATING_STEP, lambda: V.tensor_tensor(o, r, spread(first, E), ALU.is_equal))

                        def copy_logits(at, use, E):
                            for l in own:
                                yield at + LATER * (l - own[0])
                                dve.wait_ge(logits[g], nth(l, use))
                                z = psB[l][:, 0:TILES * E].rearrange("p (t e) -> p t e", e=E)
                                if use == G_M2:
                                    last = V.tensor_copy(part(lg[g], l)[:, :, 0:E], z)
                                else:
                                    bias = crow({G_M0: "bias0", G_M1: "bias1"}[use])
                                    last = V.tensor_tensor(part(lg[g], l)[:, :, 0:E], z, bias, ALU.add)
                            last.then_inc(gating[g], 1)
                            gating_count[0] += 1

                        def top2(at, use, E, turn, result):
                            s, o1, o2, w1, w2 = (b[g][:, :, 0:E] for b in (lg, oh1, oh2, ge, gk))
                            l1, l2, diff, e, den, p1, p2 = (gs[g][:, i, :] for i in (0, 1, 3, 4, 5, 6, 7))
                            yield from copy_logits(at, use, E)
                            yield from first_of(at + GATING_STEP, E, lg, 0, oh1)
                            yield from gating_step(at + 6 * GATING_STEP, lambda: V.scalar_tensor_tensor(
                                s, o1, -BIG, s, ALU.mult, ALU.add))
                            yield from first_of(at + 7 * GATING_STEP, E, lg, 1, oh2)
                            yield from gating_step(at + TOP2_DIFF * GATING_STEP, lambda: V.tensor_tensor(diff, l2, l1, ALU.subtract))
                            yield at + 14 * GATING_STEP
                            dve.wait_ge(gate_exp[g], turn + 1)
                            yield from gating_step(at + 14 * GATING_STEP, lambda: V.tensor_scalar(den, e, 1.0, None, ALU.add))
                            yield from gating_step(at + 15 * GATING_STEP, lambda: V.reciprocal(p1, den))
                            yield from gating_step(at + 16 * GATING_STEP, lambda: V.tensor_tensor(p2, p1, e, ALU.mult))
                            yield from gating_step(at + 17 * GATING_STEP, lambda: V.tensor_tensor(w1, o1, spread(p1, E), ALU.mult))
                            yield from gating_step(at + 18 * GATING_STEP, lambda: V.tensor_tensor(w2, o2, spread(p2, E), ALU.mult))
                            yield from gating_step(at + 19 * GATING_STEP, lambda: V.tensor_tensor(result, w1, w2, ALU.add))

                        def add_psum(at, step, use):
                            for l in own:
                                yield at + LATER * (l - own[0])
                                dve.wait_ge(pe_step[g], nth(l, step))
                                V.tensor_tensor(h[l][:, :, :], rows(psA[l]), h[l][:, :, :], ALU.add).then_inc(h_new[g], 1)

                        def add_affine(at, use):
                            for l in own:
                                yield at + LATER * (l - own[0])
                                dve.wait_ge(affined[g], nth(l, use))
                                V.tensor_tensor(h[l][:, :, :], aff[l][:, :, :], h[l][:, :, :], ALU.add).then_inc(h_new[g], 1)

                        for l in own:
                            yield 0 + LATER * (l - own[0])
                            first = it * (LANES * TILES) + l * TILES
                            src = emb[:, l * TILES:(l + 1) * TILES, :]
                            kp = keep[:, bass.ds(first, TILES)]
                            V.tensor_tensor(h[l][:, :, :], src, kp[:, :, None].broadcast_to([P, TILES, D]),
                                            ALU.mult).then_inc(h_new[g], 1)

                        yield from norm_h(AT_A0, LN_A0, H_EMB)
                        for l in own:
                            yield AT_A0 + 9 + LATER * (l - own[0])
                            dve.wait_ge(pe_step[g], nth(l, PE_RV0))
                            V.tensor_copy(v_sb[l][:, :, 0:D], rows(psA[l])).then_inc(dve_step[g], 1)
                        for l in own:
                            yield AT_A0 + 13 + LATER * (l - own[0])
                            dve.wait_ge(pe_step[g], nth(l, PE_S0))
                            V.tensor_tensor(big_a[l][:, :].rearrange("p (t s) -> p t s", t=TILES),
                                            psB[l][:, :].rearrange("p (t s) -> p t s", t=TILES),
                                            cc("decay")[:, None, :].broadcast_to([P, TILES, P]), ALU.mult).then_inc(dve_step[g], 1)
                        yield from add_psum(AT_A0 + 17, PE_O0, H_A0)

                        yield from norm_h(AT_M0, LN_M0, H_A0)
                        yield from low_parts(AT_M0, XS_M0)
                        yield from top2(AT_M0 + GATES, G_M0, E0, 0, gate[g][:, :, 0:E0])
                        for q in range(E0 // 2):
                            for l in own:
                                yield AT_M0 + GATES_COPY + M0_STEP * (2 * q + 3) + 3 + LATER * (l - own[0])
                                dve.wait_ge(m0_o[g], nth(l, q))
                                if q == 0:
                                    dve.wait_ge(gating[g], GATING_END[G_M0])
                                if q >= 2:
                                    dve.wait_ge(m0_acc[g], nth(l, max(q - 3, 0)))
                                w = part(gate[g], l)[:, :, 2 * q:2 * q + 2].rearrange("p t e -> p e t")
                                V.tensor_tensor(prod(l, q).rearrange("p (e t d) -> p e t d", e=2, t=TILES),
                                                psB[l][:, :].rearrange("p (e t d) -> p e t d", e=2, t=TILES),
                                                w[:, :, :, None].broadcast_to([P, 2, TILES, D]), ALU.mult).then_inc(m0_prod[g], 1)
                        for l in own:
                            yield AT_IN0 - 3 + LATER * (l - own[0])
                            dve.wait_ge(m0_b[g], nth(l))
                            V.tensor_tensor(y[l][:, :, :], rows(psA[l]), xn[l][:, :, :], ALU.add).then_inc(y_part[g], 1)
                        for l in own:
                            yield AT_IN0 - 1 + LATER * (l - own[0])
                            dve.wait_ge(m0_acc[g], nth(l, E0 // 2 - 2))
                            dve.wait_ge(y_part[g], nth(l, 0))
                            V.tensor_tensor(y[l][:, :, :], rows(big_c[l]), y[l][:, :, :], ALU.add).then_inc(y_part[g], 1)
                        for l in own:
                            dve.wait_ge(y_part[g], nth(l, 1))
                            odd = big_c[l][:, TILES * D:].rearrange("p (t d) -> p t d", t=TILES)
                            V.tensor_tensor(y[l][:, :, :], odd, y[l][:, :, :], ALU.add).then_inc(y_new[g], 1)
                        yield from norm_y(AT_IN0, LN_IN0, Y_IN0)
                        yield from add_affine(AT_A1 - 1, AFF_IN0)

                        yield from norm_h(AT_A1, LN_A1, H_M0)
                        for l in own:
                            yield AT_A1 + 9 + LATER * (l - own[0])
                            dve.wait_ge(pe_step[g], nth(l, PE_QK1))
                            V.tensor_copy(fm2[l][0:64, :], psA[l][64:128, :]).then_inc(dve_step[g], 1)
                        for l in own:
                            yield AT_A1 + 12 + LATER * (l - own[0])
                            dve.wait_ge(pe_step[g], nth(l, PE_V1))
                            V.tensor_copy(v_sb[l][:, :, 0:D], rows(psB[l])).then_inc(dve_step[g], 1)
                        block1 = cc("block")[:, None, :].broadcast_to([P, TILES, P])
                        for l in own:
                            yield AT_A1 + 16 + LATER * (l - own[0])
                            dve.wait_ge(pe_step[g], nth(l, PE_S1))
                            for ps, dst in ((psA, big_a), (psB, big_b)):
                                last = V.tensor_tensor(dst[l][:, :].rearrange("p (t m) -> p t m", t=TILES),
                                                       ps[l][:, :].rearrange("p (t m) -> p t m", t=TILES), block1, ALU.mult)
                            last.then_inc(dve_step[g], 1)
                        for l in own:
                            yield AT_A1 + 19 + LATER * (l - own[0])
                            dve.wait_ge(dve_step[g], nth(l, DV_BLOCK1))
                            for hh, src in enumerate((big_a, big_b)):
                                at = TILES * (H1 * (l % GROUP_LANES) + hh)
                                last = V.tensor_reduce(s8[g][:, at:at + TILES, :],
                                                       src[l][:, :].rearrange("p (t g j) -> p t j g", t=TILES, j=BS1),
                                                       X, ALU.add)
                            last.then_inc(dve_step[g], 1)
                        yield AT_A1 + 22
                        both = GROUP_LANES
                        top, total, inverse = (s8s[g][:, i, :] for i in range(3))
                        dve.wait_ge(dve_step[g], nth(own[-1], DV_FOLD1))
                        V.tensor_reduce(top, s8[g][:, :, :], X, ALU.max).then_inc(dve_step[g], both)
                        dve.wait_ge(dve_step[g], nth(own[-1], DV_MAX1))
                        V.tensor_tensor(s8b[g][:, :, :], s8[g][:, :, :], spread(top, BS1), ALU.subtract).then_inc(dve_step[g], both)
                        yield AT_A1 + 25
                        dve.wait_ge(act_step[g], nth(own[-1], AC_EXP1))
                        V.tensor_reduce(total, s8b[g][:, :, :], X, ALU.add).then_inc(dve_step[g], both)
                        dve.wait_ge(dve_step[g], nth(own[-1], DV_SUM1))
                        V.reciprocal(inverse, total).then_inc(dve_step[g], both)
                        dve.wait_ge(dve_step[g], nth(own[-1], DV_REC1))
                        V.tensor_tensor(s8[g][:, :, :], s8b[g][:, :, :], spread(inverse, BS1), ALU.mult).then_inc(dve_step[g], both)
                        yield from add_psum(AT_M1 - 1, PE_O1, H_A1)

                        yield from norm_h(AT_M1, LN_M1, H_A1)
                        yield from low_parts(AT_M1, XS_M1)
                        yield from copy_logits(AT_M1 + GATES, G_M1, E1)
                        yield from first_of(AT_M1 + GATES + GATING_STEP, E1, lg, 0, oh1)
                        for l in own:
                            yield AT_M1 + 15 + LATER * (l - own[0])
                            dve.wait_ge(gT_ready[g], nth(l, G_M1))
                            V.tensor_scalar(gTb[l][0:E1, :], gT[l][:, :], -1.0, BIG, ALU.add, ALU.mult).then_inc(gTb_ready[g], 1)
                        for m in range(1, MT, 2):
                            for l in own:
                                yield AT_M1 + 18 + M1_STEP * m + LATER * (l - own[0])
                                dve.wait_ge(m1_z[g], nth(l, m))
                                V.tensor_scalar(hid[l][:, m, :], psB[l][:, :], c128("b1_1")[:, m:m + 1], 0.0,
                                                ALU.add, ALU.max).then_inc(m1_odd[g], 1)
                        for l in own:
                            yield AT_A2 - 1 + LATER * (l - own[0])
                            dve.wait_ge(m1_z[g], nth(l, MT))
                            V.scalar_tensor_tensor(h[l][:, :, :], rows(psA[l]), 0.0, h[l][:, :, :], ALU.max,
                                                   ALU.add).then_inc(h_new[g], 1)

                        yield from norm_h(AT_A2, LN_A2, H_M1)
                        for l in own:
                            yield AT_A2 + 12 + LATER * (l - own[0])
                            dve.wait_ge(act_step[g], nth(l, AC_K2))
                            kv = psA[l][:, :].rearrange("p (t c) -> p t c", t=TILES)
                            V.tensor_copy(v_sb[l][:, :, 0:D], kv[:, :, D:2 * D])
                            V.scalar_tensor_tensor(kf[l][:, 0, :, :], kf[l][:, 0, :, :], 1.0, kf[l][:, 1, :, :],
                                                   ALU.min, ALU.add).then_inc(dve_step[g], 1)
                        for l in own:
                            dve.wait_ge(act_step[g], nth(l, AC_Q2))
                            V.scalar_tensor_tensor(fm2[l][0:64, :], fm2[l][0:64, :], 1.0, big_a[l][0:64, :],
                                                   ALU.min, ALU.add).then_inc(dve_step[g], 1)
                        heads = cc("heads", 64)[:, None, :].broadcast_to([64, TILES, KV2])
                        for l in own:
                            yield AT_A2 + 16 + LATER * (l - own[0])
                            dve.wait_ge(pe_step[g], nth(l, PE_S2))
                            V.tensor_tensor(kvm[l][:, :, :], psB[l][0:64, 0:TILES * KV2].rearrange("p (t c) -> p t c", c=KV2),
                                            heads, ALU.mult).then_inc(dve_step[g], 1)
                        den, inverse = lg[g][:, :, 0:H2], lg[g][:, :, H2:2 * H2]
                        for l in own:
                            yield AT_A2 + 18 + LATER * (l - own[0])
                            dve.wait_ge(dve_step[g], nth(own[-1], DV_Q2))
                            dve.wait_ge(pe_step[g], nth(l, PE_N2))
                            nd = psA[l][:, 0:TILES * KV2].rearrange("p (t c) -> p t c", c=KV2)
                            V.tensor_scalar(part(den, l), nd[:, :, D:KV2], DEN_EPS, None, ALU.add).then_inc(dve_step[g], 1)
                        dve.wait_ge(dve_step[g], nth(own[-1], DV_DEN2))
                        V.reciprocal(inverse, den).then_inc(dve_step[g], GROUP_LANES)
                        dve.wait_ge(dve_step[g], nth(own[-1], DV_REC2))
                        for l in own:
                            for t in range(TILES):
                                num = psA[l][:, KV2 * t:KV2 * t + D].rearrange("p (h m) -> p h m", m=D2)
                                z = part(inverse, l)[:, t, :][:, :, None].broadcast_to([P, H2, D2])
                                last = V.tensor_tensor(y[l][:, t, :].rearrange("p (h m) -> p h m", m=D2), num, z, ALU.mult)
                            last.then_inc(dve_step[g], 1)
                        for l in own:
                            dve.wait_ge(dve_step[g], nth(l, DV_O2))
                            V.tensor_tensor(y[l][:, :, :], y[l][:, :, :], xn[l][:, :, :], ALU.add).then_inc(y_new[g], 1)
                        yield from norm_y(AT_IN2, LN_IN2, Y_IN2)
                        for l in own:
                            yield AT_OUT2 - 1 + LATER * (l - own[0])
                            dve.wait_ge(pe_step[g], nth(l, PE_Y2))
                            V.tensor_tensor(y[l][:, :, :], rows(psA[l]), aff[l][:, :, :], ALU.add).then_inc(y_new[g], 1)
                        yield from norm_y(AT_OUT2, LN_OUT2, Y_OUT2)
                        yield from add_affine(AT_M2 - 1, AFF_OUT2)

                        yield from norm_h(AT_M2, LN_M2, H_A2)
                        yield from low_parts(AT_M2, XS_M2)
                        parts = g3[g][:, :, :].rearrange("p t (s e) -> p s t e", s=SPLIT)
                        yield from top2(AT_M2 + GATES, G_M2, E2, 1, parts[:, 0])
                        at = AT_M2 + GATES + GATING_STEP * 20
                        yield from gating_step(at, lambda: V.tensor_copy(gh[g][:, :, :], parts[:, 0]))
                        yield from gating_step(at + GATING_STEP, lambda: V.tensor_tensor(
                            parts[:, 1], parts[:, 0], gh[g][:, :, :], ALU.subtract))
                        yield from gating_step(at + 2 * GATING_STEP, lambda: V.tensor_copy(gh[g][:, :, :], parts[:, 1]))
                        yield from gating_step(at + 3 * GATING_STEP, lambda: V.tensor_tensor(
                            parts[:, 2], parts[:, 1], gh[g][:, :, :], ALU.subtract))
                        for m in range(MT):
                            for l in own:
                                yield AT_M2 + 24.5 + M2_STEP * m + LATER * (l - own[0])
                                dve.wait_ge(m2_h[g], nth(l, m))
                                dve.wait_ge(m2_g[g], nth(l, m))
                                V.tensor_tensor(hid[l][:, m, :], psB[l][:, :], hid[l][:, m, :], ALU.mult).then_inc(m2_hg[g], 1)
                        for l in own:
                            yield AT_A3 - 1 + LATER * (l - own[0])
                            dve.wait_ge(m2_o[g], nth(l))
                            dve.wait_ge(m2_res[g], nth(l))
                            V.tensor_tensor(h[l][:, :, :], rows(psA[l]), y[l][:, :, :], ALU.add).then_inc(h_new[g], 1)

                        yield from norm_h(AT_A3, LN_A3, H_M2)
                        yield from low_parts(AT_A3, XS_A3)
                        for l in own:
                            yield AT_A3 + 11 + LATER * (l - own[0])
                            dve.wait_ge(pe_step[g], nth(l, PE_B3))
                            for ps, wave, dst in ((psA, cosines, big_a), (psB, sines, big_b)):
                                last = V.tensor_tensor(dst[l][:, :].rearrange("p (t s) -> p t s", t=TILES),
                                                       ps[l][:, :].rearrange("p (t s) -> p t s", t=TILES),
                                                       wave[:, None, :].broadcast_to([P, TILES, P]), ALU.mult)
                            last.then_inc(dve_step[g], 1)
                        for l in own:
                            yield AT_A3 + 16 + LATER * (l - own[0])
                            dve.wait_ge(pool_step[g], nth(l, PL_SUM3))
                            V.tensor_tensor_scan(hid[l][:, 0, :], decay3[:, :], big_c[l][:, :], 0.0,
                                                 ALU.mult, ALU.add).then_inc(dve_step[g], 1)
                        for l in own:
                            yield AT_M3 - 1 + LATER * (l - own[0])
                            dve.wait_ge(pool_step[g], nth(l, PL_RES3))
                            dve.wait_ge(pe_step[g], nth(l, PE_Y3))
                            V.tensor_tensor(h[l][:, :, :], rows(psA[l]), y[l][:, :, :], ALU.add).then_inc(h_new[g], 1)

                        yield from norm_h(AT_M3, LN_M3, H_A3)
                        for l in own:
                            yield AT_M3 + 9 + LATER * (l - own[0])
                            dve.wait_ge(m3_z[g], nth(l))
                            V.tensor_scalar(gTb[l][0:G3, :], psB[l][0:G3, :], GATE_MIN, None, ALU.is_gt).then_inc(m3_g[g], 1)
                        for p in range(PAIRS):
                            for l in own:
                                yield AT_M3 + 11 + M3_STEP * p + LATER * (l - own[0])
                                dve.wait_ge(m3_s[g], nth(l, p))
                                if p == 0:
                                    dve.wait_ge(m3_x[g], nth(l))
                                if p >= 2:
                                    dve.wait_ge(m3_sum[g], nth(l, p - 2))
                                V.tensor_tensor(pr[l][:, p % 2, :], sg[l][:, p % 2, :], sx[l][:, :], ALU.mult).then_inc(m3_p[g], 1)
                        for l in own:
                            yield AT_OUT - 3 + LATER * (l - own[0])
                            dve.wait_ge(m3_sum[g], nth(l, PAIRS - 1))
                            V.tensor_scalar(fm2[l][0:64, :], psB[l][0:D, :], c128("scale3")[0:D, :], None,
                                            ALU.mult).then_inc(m3_y[g], 1)
                        for l in own:
                            yield AT_OUT + LATER * (l - own[0])
                            dve.wait_ge(m3_t[g], nth(l))
                            V.tensor_tensor(h[l][:, :, :], rows(psA[l]), h[l][:, :, :], ALU.add).then_inc(h_new[g], 1)

                    in_order([program(g) for g in range(GROUPS)])

            nc.sync.sem_clear(range(sems[sems_setup].num, sems[-1].num + 1))
            nc.all_engine_barrier()


def shape_constants():
    import numpy as np
    c = np.zeros((P, CC["_"][1]), np.float32)
    b = np.zeros((P, CB["_"][1]), np.float32)

    def put(name, a):
        into, (s, e) = (c, CC[name]) if name in CC else (b, CB[name])
        a = np.asarray(a, np.float32)
        into[0:a.shape[0], s:e] = a

    i = np.arange(P)
    put("ident", np.eye(P))
    gap = i[None, :] - i[:, None]
    put("decay", np.where(gap >= 0, np.exp(gap * np.log(np.float64(0.96875))), 0.0))
    put("block", i[:, None] // BS1 == i[None, :] // BS1)
    j = np.arange(D)
    head = np.arange(H2)
    put("heads", np.concatenate([j[:, None] // D2 == j[None, :] // D2, j[:, None] // D2 == head[None, :]], 1))
    for name, E in (("rank0", E0), ("rank1", E1), ("rank2", E2)):
        put(name, np.tile(E - np.arange(E), (P, 1)))
    put("time", np.tile(i, (P, 1)))
    put("later", np.tile(i > 0, (P, 1)))
    put("sign", np.where(i < D, 1.0, -1.0)[:, None])
    hid = np.arange(HID)
    put("sel2", np.arange(SPLIT * E2)[:, None] % E2 == hid[None, :] // F2)
    put("exp1", np.arange(E1)[:, None] == hid[None, :] // F1)
    put("pick3", np.arange(3 * D)[None, :] == D + i[:, None] // D)
    return c, b


def kernel(**inputs):
    import numpy as np
    import concourse.bacc as bacc
    from concourse.bass_utils import run_bass_kernel_spmd

    a = {k: np.asarray(v) for k, v in inputs.items()}

    def row(x):
        return x.reshape(1, -1)

    def with_bias(w, b):
        return np.concatenate([w, row(b)], 0)

    zero = np.zeros((1, D), np.float32)
    w65 = np.concatenate([
        with_bias(a["L1_attn_Wv"].T, a["L1_attn_bv"]),
        with_bias(a["L2_attn_W2"].T, a["L2_attn_b2"]),
        np.concatenate([with_bias(a["L3_ffn_proj_w"].T, a["L3_ffn_proj_b"])] * SPLIT, 1),
    ], 1)
    wup = np.concatenate([a[n].transpose(1, 0, 2).reshape(D, -1) for n in ("L0_ffn_w1", "L1_ffn_W1", "L2_ffn_w1")]
                         + [a["L0_ffn_gate_w"], a["L1_ffn_router_w"].T, a["L2_ffn_router_w"].T], 1)
    scale3 = a["L3_ffn_scale"].reshape(D, 1)
    qkv = a["L2_attn_Wqkv"]
    w64 = np.concatenate([
        a["L0_attn_Wq"], a["L0_attn_Wk"], a["L0_attn_Wv"].T,
        qkv[0:D].T, qkv[D:3 * D].T, a["L2_attn_W1"].T, a["L2_attn_b1"].reshape(D, 1),
        a["L3_attn_B_re"], a["L3_attn_B_im"],
    ], 1)
    c_re, c_im = a["L3_attn_C_re"].T, a["L3_attn_C_im"].T
    nu, theta = a["L3_attn_nu_log"].reshape(D, 1), a["L3_attn_theta_log"].reshape(D, 1)
    logs = np.concatenate([np.concatenate([nu, nu], 0), np.concatenate([theta, theta], 0),
                           np.concatenate([a["L3_attn_gamma_log"].reshape(D, 1), np.zeros((D, 1), np.float32)], 0)], 1)
    w3 = a["L3_ffn_weight"][0].transpose(0, 2, 1).reshape(P, 256)
    w128 = np.concatenate([
        a["L0_ffn_w2"].transpose(1, 0, 2).reshape(F0, E0 * D),
        a["L1_ffn_W2"].reshape(MT, P, D).transpose(1, 0, 2).reshape(P, MT * D),
        a["L2_ffn_w2"].reshape(MT, P, D).transpose(1, 0, 2).reshape(P, MT * D),
        np.concatenate([c_re, c_im], 0), np.concatenate([c_im, c_re], 0),
        w3,
        a["L0_ffn_b1"].T, a["L1_ffn_b1"].reshape(MT, P).T, a["L2_ffn_b1"].reshape(MT, P).T,
        np.concatenate([scale3, scale3], 0),
    ], 1)

    def per_head(w, b):
        return np.concatenate([w.reshape(H1, D1, D), b.reshape(H1, D1, 1)], 2).transpose(1, 0, 2).reshape(D1, H1 * 65)

    def rows32(x):
        return np.concatenate([x, np.zeros((32 - x.shape[0], x.shape[1]), np.float32)], 0)

    w32 = np.concatenate([
        per_head(a["L1_attn_Wq"], a["L1_attn_bq"]), per_head(a["L1_attn_Wk"], a["L1_attn_bk"]),
        a["L1_attn_P"], rows32(a["L0_ffn_b2"]), a["L1_ffn_b2"], rows32(a["L2_ffn_b2"]),
    ], 1)
    wrow = np.concatenate([row(a[n]) for n in ("L0_ffn_gamma", "L0_ffn_beta", "L2_attn_ln1_g", "L2_attn_ln1_b",
                                               "L2_attn_ln2_g", "L2_attn_ln2_b",
                                               "L0_ffn_gate_b", "L1_ffn_router_b", "L3_attn_D")], 1)
    consts, binary = shape_constants()
    arrays = {
        "ids": np.ascontiguousarray(a["x"].T), "emb_w": np.ascontiguousarray(a["L0_tok_W"].T),
        "logs": logs, "w65": w65, "wup": wup, "w64": w64, "w128": w128, "w32": w32, "wrow": wrow, "consts": consts, "binary": binary,
    }
    nc = bacc.Bacc("TRN2", target_bir_lowering=False, num_devices=1)
    aps = {n: nc.dram_tensor(n, list(v.shape), mybir.dt.from_np(v.dtype), kind="ExternalInput").ap()
           for n, v in arrays.items()}
    out = nc.dram_tensor("out", [NSEQ, P, D], mybir.dt.float32, kind="ExternalOutput").ap()
    tower(nc, aps["ids"], aps["emb_w"], aps["logs"], aps["w65"], aps["wup"], aps["w64"], aps["w128"], aps["w32"], aps["wrow"],
          aps["consts"], aps["binary"], out.rearrange("(i l t) p d -> i l t p d", i=PASSES, l=LANES))
    r = run_bass_kernel_spmd(nc, [arrays], core_ids=[0])
    return r.results[0]["out"]
```
